# Optimizing a Trainium2 kernel written in Bass

```python
import numpy as np
import jax
import jax.numpy as jnp

def _softmax(x, axis=-1):
    return jax.nn.softmax(x, axis=axis)

def _gelu(x):
    return jax.nn.gelu(x, approximate=True)

def _silu(x):
    return jax.nn.silu(x)

def _sigmoid(x):
    return jax.nn.sigmoid(x)

def _layernorm(x, axis=-1, eps=1e-05):
    m = jnp.mean(x, axis=axis, keepdims=True)
    v = jnp.var(x, axis=axis, keepdims=True)
    return (x - m) / jnp.sqrt(v + eps)

def _scatter_add(tgt, idx, src, axis=0):
    return tgt.at[idx].add(src)

def _segment_sum(src, seg, n):
    return jax.ops.segment_sum(src, seg, n)
kernel_name = 'mk_decoder_postln_d2_seqx_r4_fa287e'

def setup_inputs(seed: int=0):
    np.random.seed(seed)
    _w = jnp.asarray

    def _rec_inputs():
        import jax
        import jax.numpy as jnp
        _rk = jax.random.key(seed)
        x = -0.0002928 + 1 * jax.random.normal(jax.random.fold_in(_rk, 1), (16, 112, 256), jnp.float32)
        _lenS = 112 - jax.random.randint(jax.random.fold_in(_rk, 7), (16,), 0, max(1, 112 // 4) + 1, jnp.int32)
        _lenS2 = 375 - jax.random.randint(jax.random.fold_in(_rk, 8), (16,), 0, max(1, 375 // 4) + 1, jnp.int32)
        _ctx_1024P = jax.random.normal(jax.random.fold_in(_rk, 11), (16, 16, 256), jnp.float32)
        _ctx_1024c = jax.random.dirichlet(jax.random.fold_in(_rk, 511), 0.3 * jnp.ones((16,), jnp.float32), (16, 375))
        _ctx_1024t = jnp.einsum('bsk,bkd->bsd', _ctx_1024c, _ctx_1024P)
        _ctx_1024t = _ctx_1024t * jax.lax.rsqrt(jnp.mean(jnp.square(_ctx_1024t)) + 1e-12) * 0.953939
        ctx_1024 = -1.39393e-06 + 0.999914 * (_ctx_1024t + 0.3 * jax.random.normal(jax.random.fold_in(_rk, 611), (16, 375, 256), jnp.float32))
        return (x, ctx_1024)
    x, ctx_1024 = _rec_inputs()

    def _L0_attn_setup():
        import jax, jax.numpy as jnp
        import numpy as np
        B, S, E, H, K = (2, 512, 256, 16, 32)
        D = E // H
        key = jax.random.key(seed)
        ks = jax.random.split(key, 9)
        sc = 1.0 / np.sqrt(E)
        return {'x': jax.random.normal(ks[0], (B, S, E), dtype=jnp.float32), 'Wq': jax.random.normal(ks[1], (E, E), dtype=jnp.float32) * sc, 'bq': jnp.zeros((E,), dtype=jnp.float32), 'Wk': jax.random.normal(ks[2], (E, E), dtype=jnp.float32) * sc, 'bk': jnp.zeros((E,), dtype=jnp.float32), 'Wv': jax.random.normal(ks[3], (E, E), dtype=jnp.float32) * sc, 'bv': jnp.zeros((E,), dtype=jnp.float32), 'Wo': jax.random.normal(ks[4], (E, E), dtype=jnp.float32) * sc, 'bo': jnp.zeros((E,), dtype=jnp.float32)}
    _L0_attn_all = _L0_attn_setup()
    _L0_attn_in = {k: v for k, v in _L0_attn_all.items() if k in ('Wq', 'bq', 'Wk', 'bk', 'Wv', 'bv', 'Wo', 'bo')}
    del _L0_attn_all

    def _L0_xattn_setup():
        import jax, jax.numpy as jnp
        import numpy as np
        D_MODEL = 256
        N_HEADS = 16
        D_K = D_MODEL // N_HEADS
        ROPE_BASE = 10000.0

        def rope_cos_sin(seq_len, d_k, base=ROPE_BASE, dtype=jnp.float32):
            inv_freq = 1.0 / base ** (jnp.arange(0, d_k, 2, dtype=dtype) / d_k)
            pos = jnp.arange(seq_len, dtype=dtype)
            freqs = jnp.outer(pos, inv_freq)
            return (jnp.cos(freqs), jnp.sin(freqs))

        def apply_rope(x, cos, sin):
            x1 = x[..., 0::2]
            x2 = x[..., 1::2]
            c = cos[None, None]
            s = sin[None, None]
            r1 = x1 * c - x2 * s
            r2 = x1 * s + x2 * c
            return jnp.stack([r1, r2], axis=-1).reshape(x.shape)
        key = jax.random.key(seed)
        ks = jax.random.split(key, 7)
        B, T = (2, 512)
        q = jax.random.normal(ks[0], (B, T, D_MODEL), dtype=jnp.float32)
        k = jax.random.normal(ks[1], (B, T, D_MODEL), dtype=jnp.float32)
        v = jax.random.normal(ks[2], (B, T, D_MODEL), dtype=jnp.float32)
        scale = 1.0 / np.sqrt(D_MODEL)
        W_q = jax.random.normal(ks[3], (D_MODEL, D_MODEL), dtype=jnp.float32) * scale
        W_k = jax.random.normal(ks[4], (D_MODEL, D_MODEL), dtype=jnp.float32) * scale
        W_v = jax.random.normal(ks[5], (D_MODEL, D_MODEL), dtype=jnp.float32) * scale
        W_o = jax.random.normal(ks[6], (D_MODEL, D_MODEL), dtype=jnp.float32) * scale
        return {'q': q, 'k': k, 'v': v, 'W_q': W_q, 'W_k': W_k, 'W_v': W_v, 'W_o': W_o}
    _L0_xattn_all = _L0_xattn_setup()
    _L0_xattn_in = {k: v for k, v in _L0_xattn_all.items() if k in ('W_q', 'W_k', 'W_v', 'W_o')}
    del _L0_xattn_all

    def _L0_ffn_setup():
        import jax, jax.numpy as jnp
        import numpy as np
        B, S, D_MODEL, D_HIDDEN = (4, 512, 256, 1024)

        def act_quant(x):
            scale = 127.0 / jnp.clip(jnp.max(jnp.abs(x), axis=-1, keepdims=True), 1e-05)
            return jnp.clip(jnp.round(x * scale), -128, 127) / scale

        def weight_quant(w):
            scale = 1.0 / jnp.clip(jnp.mean(jnp.abs(w)), 1e-05)
            return jnp.clip(jnp.round(w * scale), -1, 1) / scale

        def bit_linear(x, w):
            xq = x + jax.lax.stop_gradient(act_quant(x) - x)
            wq = w + jax.lax.stop_gradient(weight_quant(w) - w)
            return jnp.einsum('bsd,hd->bsh', xq, wq)

        def depthwise_conv1d(x_bcl, w, b):
            y = jax.lax.conv_general_dilated(x_bcl, w, window_strides=(1,), padding=[(1, 1)], dimension_numbers=('NCH', 'OIH', 'NCH'), feature_group_count=x_bcl.shape[1])
            return y + b[None, :, None]
        key = jax.random.key(seed)
        ks = jax.random.split(key, 5)
        lim1 = 1.0 / np.sqrt(D_MODEL)
        lim2 = 1.0 / np.sqrt(D_HIDDEN)
        limc = 1.0 / np.sqrt(3.0)
        return {'x': jax.random.normal(ks[0], (B, S, D_MODEL), dtype=jnp.float32), 'w1': jax.random.uniform(ks[1], (D_HIDDEN, D_MODEL), jnp.float32, -lim1, lim1), 'conv_w': jax.random.uniform(ks[2], (D_HIDDEN, 1, 3), jnp.float32, -limc, limc), 'conv_b': jax.random.uniform(ks[3], (D_HIDDEN,), jnp.float32, -limc, limc), 'w2': jax.random.uniform(ks[4], (D_MODEL, D_HIDDEN), jnp.float32, -lim2, lim2)}
    _L0_ffn_all = _L0_ffn_setup()
    _L0_ffn_in = {k: v for k, v in _L0_ffn_all.items() if k in ('w1', 'conv_w', 'conv_b', 'w2')}
    del _L0_ffn_all

    def _L1_attn_setup():
        import jax, jax.numpy as jnp
        import numpy as np
        EPS = float(np.finfo(np.float32).eps)
        SEQ_LEN = 512
        NUM_HEADS = 16
        DIM_EMB = 256
        DIM_HEAD = DIM_EMB // NUM_HEADS
        DIM_K = DIM_EMB
        BATCH = 2

        def cosine_positional_encoding(seq_len, dim):
            idx = jnp.arange(seq_len, dtype=jnp.float32)
            scale = 1.0 / (10000.0 ** (jnp.arange(0, dim, 2, dtype=jnp.float32) / dim) + EPS)
            ang = idx[:, None] * scale[None, :]
            return jnp.stack([jnp.sin(ang), jnp.cos(ang)], axis=-1).reshape(seq_len, dim)
        key = jax.random.key(seed)
        ks = jax.random.split(key, 5)
        s = DIM_EMB ** (-0.5)
        return {'x': jax.random.normal(ks[0], (BATCH, SEQ_LEN, DIM_EMB), dtype=jnp.float32), 'Wq': jax.random.normal(ks[1], (DIM_EMB, DIM_EMB), dtype=jnp.float32) * s, 'Wk': jax.random.normal(ks[2], (DIM_EMB, DIM_EMB), dtype=jnp.float32) * s, 'Wv': jax.random.normal(ks[3], (DIM_EMB, DIM_EMB), dtype=jnp.float32) * s, 'Wo': jax.random.normal(ks[4], (DIM_EMB, DIM_EMB), dtype=jnp.float32) * s}
    _L1_attn_all = _L1_attn_setup()
    _L1_attn_in = {k: v for k, v in _L1_attn_all.items() if k in ('Wq', 'Wk', 'Wv', 'Wo')}
    del _L1_attn_all

    def _L1_xattn_setup():
        import jax, jax.numpy as jnp
        import numpy as np
        H = 16
        D = 64
        SCALE = D ** (-0.5)
        TEXT = 77
        IMG = 16
        AUD = 32
        MAXREL = 16
        B, NQ, QD = (32, 256, 256)
        INNER = H * D

        def _heads(t):
            return t.reshape(t.shape[0], t.shape[1], H, D)
        key = jax.random.key(seed)
        ks = jax.random.split(key, 14)
        w = lambda k, s: jax.random.normal(k, s, jnp.float32) * 0.02
        return {'x': jax.random.normal(ks[0], (B, NQ, QD), jnp.float32), 'context': jax.random.normal(ks[1], (B, TEXT + IMG + AUD, QD), jnp.float32), 'Wq': w(ks[2], (QD, INNER)), 'Wk': w(ks[3], (QD, INNER)), 'Wv': w(ks[4], (QD, INNER)), 'Wk_ip': w(ks[5], (QD, INNER)), 'Wv_ip': w(ks[6], (QD, INNER)), 'Wk_ap': w(ks[7], (QD, INNER)), 'Wv_ap': w(ks[8], (QD, INNER)), 'Wo': w(ks[9], (INNER, QD)), 'bo': jnp.zeros((QD,), jnp.float32), 'rel_k': w(ks[10], (2 * MAXREL + 1, D)), 'rel_v': w(ks[11], (2 * MAXREL + 1, D)), 'alpha': jnp.zeros((), jnp.float32), 'beta': jnp.zeros((), jnp.float32)}
    _L1_xattn_all = _L1_xattn_setup()
    _L1_xattn_in = {k: v for k, v in _L1_xattn_all.items() if k in ('Wq', 'Wk', 'Wv', 'Wk_ip', 'Wv_ip', 'Wk_ap', 'Wv_ap', 'Wo', 'bo', 'rel_k', 'rel_v', 'alpha', 'beta')}
    del _L1_xattn_all

    def _L1_ffn_setup():
        import jax, jax.numpy as jnp
        import numpy as np

        def _binarize(w):
            alpha = jax.lax.stop_gradient(jnp.mean(jnp.abs(w), axis=1, keepdims=True))
            bw = alpha * jnp.sign(w)
            return w + jax.lax.stop_gradient(bw - w)
        key = jax.random.key(seed)
        k1, k2, k3, k4, k5 = jax.random.split(key, 5)
        D, H = (256, 1024)
        x = jax.random.normal(k1, (64, 196, D), dtype=jnp.float32)
        w1 = jax.random.normal(k2, (H, D), dtype=jnp.float32) * 0.02
        b1 = jax.random.normal(k3, (H,), dtype=jnp.float32) * 0.02
        w2 = jax.random.normal(k4, (D, H), dtype=jnp.float32) * 0.02
        b2 = jax.random.normal(k5, (D,), dtype=jnp.float32) * 0.02
        return {'x': x, 'w1': w1, 'b1': b1, 'w2': w2, 'b2': b2}
    _L1_ffn_all = _L1_ffn_setup()
    _L1_ffn_in = {k: v for k, v in _L1_ffn_all.items() if k in ('w1', 'b1', 'w2', 'b2')}
    del _L1_ffn_all
    return {'x': x, 'ctx_1024': ctx_1024, 'L0_attn_Wq': _L0_attn_in['Wq'], 'L0_attn_bq': _L0_attn_in['bq'], 'L0_attn_Wk': _L0_attn_in['Wk'], 'L0_attn_bk': _L0_attn_in['bk'], 'L0_attn_Wv': _L0_attn_in['Wv'], 'L0_attn_bv': _L0_attn_in['bv'], 'L0_attn_Wo': _L0_attn_in['Wo'], 'L0_attn_bo': _L0_attn_in['bo'], 'L0_xattn_W_q': _L0_xattn_in['W_q'], 'L0_xattn_W_k': _L0_xattn_in['W_k'], 'L0_xattn_W_v': _L0_xattn_in['W_v'], 'L0_xattn_W_o': _L0_xattn_in['W_o'], 'L0_ffn_w1': _L0_ffn_in['w1'], 'L0_ffn_conv_w': _L0_ffn_in['conv_w'], 'L0_ffn_conv_b': _L0_ffn_in['conv_b'], 'L0_ffn_w2': _L0_ffn_in['w2'], 'L1_attn_Wq': _L1_attn_in['Wq'], 'L1_attn_Wk': _L1_attn_in['Wk'], 'L1_attn_Wv': _L1_attn_in['Wv'], 'L1_attn_Wo': _L1_attn_in['Wo'], 'L1_xattn_Wq': _L1_xattn_in['Wq'], 'L1_xattn_Wk': _L1_xattn_in['Wk'], 'L1_xattn_Wv': _L1_xattn_in['Wv'], 'L1_xattn_Wk_ip': _L1_xattn_in['Wk_ip'], 'L1_xattn_Wv_ip': _L1_xattn_in['Wv_ip'], 'L1_xattn_Wk_ap': _L1_xattn_in['Wk_ap'], 'L1_xattn_Wv_ap': _L1_xattn_in['Wv_ap'], 'L1_xattn_Wo': _L1_xattn_in['Wo'], 'L1_xattn_bo': _L1_xattn_in['bo'], 'L1_xattn_rel_k': _L1_xattn_in['rel_k'], 'L1_xattn_rel_v': _L1_xattn_in['rel_v'], 'L1_xattn_alpha': _L1_xattn_in['alpha'], 'L1_xattn_beta': _L1_xattn_in['beta'], 'L1_ffn_w1': _L1_ffn_in['w1'], 'L1_ffn_b1': _L1_ffn_in['b1'], 'L1_ffn_w2': _L1_ffn_in['w2'], 'L1_ffn_b2': _L1_ffn_in['b2']}

def reference(x, ctx_1024, L0_attn_Wq, L0_attn_bq, L0_attn_Wk, L0_attn_bk, L0_attn_Wv, L0_attn_bv, L0_attn_Wo, L0_attn_bo, L0_xattn_W_q, L0_xattn_W_k, L0_xattn_W_v, L0_xattn_W_o, L0_ffn_w1, L0_ffn_conv_w, L0_ffn_conv_b, L0_ffn_w2, L1_attn_Wq, L1_attn_Wk, L1_attn_Wv, L1_attn_Wo, L1_xattn_Wq, L1_xattn_Wk, L1_xattn_Wv, L1_xattn_Wk_ip, L1_xattn_Wv_ip, L1_xattn_Wk_ap, L1_xattn_Wv_ap, L1_xattn_Wo, L1_xattn_bo, L1_xattn_rel_k, L1_xattn_rel_v, L1_xattn_alpha, L1_xattn_beta, L1_ffn_w1, L1_ffn_b1, L1_ffn_w2, L1_ffn_b2):
    import jax
    import jax.numpy as jnp

    def _L0_attn_ref(x, Wq, bq, Wk, bk, Wv, bv, Wo, bo):
        import jax, jax.numpy as jnp
        import numpy as np
        B, S, E, H, K = (2, 512, 256, 16, 32)
        D = E // H
        b, s, e = x.shape
        scale = jnp.sqrt(jnp.asarray(D, x.dtype))
        q = (x @ Wq.T + bq).reshape(b, s, H, D).transpose(0, 2, 1, 3)
        k = (x @ Wk.T + bk).reshape(b, s, H, D).transpose(0, 2, 1, 3)
        v = (x @ Wv.T + bv).reshape(b, s, H, D).transpose(0, 2, 1, 3)
        scores = jnp.einsum('bhsd,bhtd->bhst', q, k) / scale
        kk = min(K, s)
        top_s, top_i = jax.lax.top_k(scores, kk)
        probs = jax.nn.softmax(top_s, axis=-1)
        gather = jax.vmap(jax.vmap(lambda vv, ii: vv[ii]))
        v_g = gather(v, top_i)
        out = jnp.einsum('bhsk,bhskd->bhsd', probs, v_g)
        out = out.transpose(0, 2, 1, 3).reshape(b, s, e)
        return out @ Wo.T + bo

    def _L0_xattn_ref(q, k, v, W_q, W_k, W_v, W_o):
        import jax, jax.numpy as jnp
        import numpy as np
        D_MODEL = 256
        N_HEADS = 16
        D_K = D_MODEL // N_HEADS
        ROPE_BASE = 10000.0

        def rope_cos_sin(seq_len, d_k, base=ROPE_BASE, dtype=jnp.float32):
            inv_freq = 1.0 / base ** (jnp.arange(0, d_k, 2, dtype=dtype) / d_k)
            pos = jnp.arange(seq_len, dtype=dtype)
            freqs = jnp.outer(pos, inv_freq)
            return (jnp.cos(freqs), jnp.sin(freqs))

        def apply_rope(x, cos, sin):
            x1 = x[..., 0::2]
            x2 = x[..., 1::2]
            c = cos[None, None]
            s = sin[None, None]
            r1 = x1 * c - x2 * s
            r2 = x1 * s + x2 * c
            return jnp.stack([r1, r2], axis=-1).reshape(x.shape)
        B, T_q, _ = q.shape
        T_k = k.shape[1]
        Q = (q @ W_q.T).reshape(B, T_q, N_HEADS, D_K).transpose(0, 2, 1, 3)
        K = (k @ W_k.T).reshape(B, T_k, N_HEADS, D_K).transpose(0, 2, 1, 3)
        V = (v @ W_v.T).reshape(B, T_k, N_HEADS, D_K).transpose(0, 2, 1, 3)
        cos_q, sin_q = rope_cos_sin(T_q, D_K)
        cos_k, sin_k = rope_cos_sin(T_k, D_K)
        Q = apply_rope(Q, cos_q, sin_q)
        K = apply_rope(K, cos_k, sin_k)
        scale = jnp.sqrt(jnp.asarray(D_K, dtype=Q.dtype))
        scores = jnp.einsum('bhqd,bhkd->bhqk', Q, K) / scale
        attn = jax.nn.softmax(scores, axis=-1)
        out = jnp.einsum('bhqk,bhkd->bhqd', attn, V)
        out = out.transpose(0, 2, 1, 3).reshape(B, T_q, D_MODEL)
        return out @ W_o.T

    def _L0_ffn_ref(x, w1, conv_w, conv_b, w2):
        import jax, jax.numpy as jnp
        import numpy as np
        B, S, D_MODEL, D_HIDDEN = (4, 512, 256, 1024)

        def act_quant(x):
            scale = 127.0 / jnp.clip(jnp.max(jnp.abs(x), axis=-1, keepdims=True), 1e-05)
            return jnp.clip(jnp.round(x * scale), -128, 127) / scale

        def weight_quant(w):
            scale = 1.0 / jnp.clip(jnp.mean(jnp.abs(w)), 1e-05)
            return jnp.clip(jnp.round(w * scale), -1, 1) / scale

        def bit_linear(x, w):
            xq = x + jax.lax.stop_gradient(act_quant(x) - x)
            wq = w + jax.lax.stop_gradient(weight_quant(w) - w)
            return jnp.einsum('bsd,hd->bsh', xq, wq)

        def depthwise_conv1d(x_bcl, w, b):
            y = jax.lax.conv_general_dilated(x_bcl, w, window_strides=(1,), padding=[(1, 1)], dimension_numbers=('NCH', 'OIH', 'NCH'), feature_group_count=x_bcl.shape[1])
            return y + b[None, :, None]
        h = bit_linear(x, w1)
        h = depthwise_conv1d(h.transpose(0, 2, 1), conv_w, conv_b)
        h = h.transpose(0, 2, 1)
        h = jax.nn.silu(h)
        return bit_linear(h, w2)

    def _L1_attn_ref(x, Wq, Wk, Wv, Wo):
        import jax, jax.numpy as jnp
        import numpy as np
        EPS = float(np.finfo(np.float32).eps)
        SEQ_LEN = 512
        NUM_HEADS = 16
        DIM_EMB = 256
        DIM_HEAD = DIM_EMB // NUM_HEADS
        DIM_K = DIM_EMB
        BATCH = 2

        def cosine_positional_encoding(seq_len, dim):
            idx = jnp.arange(seq_len, dtype=jnp.float32)
            scale = 1.0 / (10000.0 ** (jnp.arange(0, dim, 2, dtype=jnp.float32) / dim) + EPS)
            ang = idx[:, None] * scale[None, :]
            return jnp.stack([jnp.sin(ang), jnp.cos(ang)], axis=-1).reshape(seq_len, dim)
        B, S, E = x.shape
        pos = cosine_positional_encoding(S, DIM_HEAD)

        def split_heads(t):
            return t.reshape(B, S, NUM_HEADS, DIM_HEAD).transpose(0, 2, 1, 3)
        q = split_heads(x @ Wq) + pos[None, None]
        k = split_heads(x @ Wk) + pos[None, None]
        v = split_heads(x @ Wv)
        scores = jnp.einsum('bhqd,bhkd->bhqk', q, k) * DIM_K ** (-0.5)
        causal_mask = jnp.triu(jnp.ones((S, S), dtype=bool), k=1)
        m_inf = -jnp.finfo(scores.dtype).max
        scores = jnp.where(causal_mask[None, None], m_inf, scores)
        attn = jax.nn.softmax(scores, axis=-1)
        out = jnp.einsum('bhqk,bhkd->bhqd', attn, v)
        out = out.transpose(0, 2, 1, 3).reshape(B, S, E)
        return out @ Wo

    def _L1_xattn_ref(x, context, Wq, Wk, Wv, Wk_ip, Wv_ip, Wk_ap, Wv_ap, Wo, bo, rel_k, rel_v, alpha, beta):
        import jax, jax.numpy as jnp
        import numpy as np
        H = 16
        D = 64
        SCALE = D ** (-0.5)
        TEXT = 77
        IMG = 16
        AUD = 32
        MAXREL = 16
        B, NQ, QD = (32, 256, 256)
        INNER = H * D

        def _heads(t):
            return t.reshape(t.shape[0], t.shape[1], H, D)
        b, nq, _ = x.shape
        q = _heads(x @ Wq)
        ctx_t = context[:, :TEXT]
        ctx_i = context[:, TEXT:TEXT + IMG]
        ctx_a = context[:, TEXT + IMG:]
        k = _heads(ctx_t @ Wk)
        v = _heads(ctx_t @ Wv)
        sim = jnp.einsum('bihd,bjhd->bhij', q, k) * SCALE
        dist = jnp.clip(jnp.arange(TEXT)[None, :] - jnp.arange(nq)[:, None], -MAXREL, MAXREL) + MAXREL
        k2 = rel_k[dist]
        sim = sim + jnp.einsum('bihd,ijd->bhij', q, k2) * SCALE
        attn = jax.nn.softmax(sim, axis=-1)
        out = jnp.einsum('bhij,bjhd->bihd', attn, v)
        out = out + jnp.einsum('bhij,ijd->bihd', attn, rel_v[dist])

        def stream(W_k, W_v, ctx):
            kh = _heads(ctx @ W_k)
            vh = _heads(ctx @ W_v)
            a = jax.nn.softmax(jnp.einsum('bihd,bjhd->bhij', q, kh) * SCALE, axis=-1)
            return jnp.einsum('bhij,bjhd->bihd', a, vh)
        out = out + stream(Wk_ip, Wv_ip, ctx_i) * (jnp.tanh(alpha) + 1.0)
        out = out + stream(Wk_ap, Wv_ap, ctx_a) * (jnp.tanh(beta) + 1.0)
        out = out.reshape(b, nq, INNER)
        return out @ Wo + bo

    def _L1_ffn_ref(x, w1, b1, w2, b2):
        import jax, jax.numpy as jnp
        import numpy as np

        def _binarize(w):
            alpha = jax.lax.stop_gradient(jnp.mean(jnp.abs(w), axis=1, keepdims=True))
            bw = alpha * jnp.sign(w)
            return w + jax.lax.stop_gradient(bw - w)
        bw1 = _binarize(w1)
        h = jnp.einsum('bsd,hd->bsh', x, bw1) + b1
        h = jax.nn.gelu(h, approximate=False)
        bw2 = _binarize(w2)
        out = jnp.einsum('bsh,dh->bsd', h, bw2) + b2
        return out
    x = _layernorm(x + _L0_attn_ref(x, L0_attn_Wq, L0_attn_bq, L0_attn_Wk, L0_attn_bk, L0_attn_Wv, L0_attn_bv, L0_attn_Wo, L0_attn_bo), axis=-1)
    x = _layernorm(x + _L0_xattn_ref(x, ctx_1024, ctx_1024, L0_xattn_W_q, L0_xattn_W_k, L0_xattn_W_v, L0_xattn_W_o), axis=-1)
    x = _layernorm(x + _L0_ffn_ref(x, L0_ffn_w1, L0_ffn_conv_w, L0_ffn_conv_b, L0_ffn_w2), axis=-1)
    x = _layernorm(x + _L1_attn_ref(x, L1_attn_Wq, L1_attn_Wk, L1_attn_Wv, L1_attn_Wo), axis=-1)
    x = _layernorm(x + _L1_xattn_ref(x, ctx_1024, L1_xattn_Wq, L1_xattn_Wk, L1_xattn_Wv, L1_xattn_Wk_ip, L1_xattn_Wv_ip, L1_xattn_Wk_ap, L1_xattn_Wv_ap, L1_xattn_Wo, L1_xattn_bo, L1_xattn_rel_k, L1_xattn_rel_v, L1_xattn_alpha, L1_xattn_beta), axis=-1)
    x = _layernorm(x + _L1_ffn_ref(x, L1_ffn_w1, L1_ffn_b1, L1_ffn_w2, L1_ffn_b2), axis=-1)
    return x

_drawn_inputs = setup_inputs


def setup_inputs(seed=0):
    import zlib

    import numpy as np

    out = dict(_drawn_inputs(seed))
    spreads = {'L0_attn_bq': (0.0, 0.1),
     'L0_attn_bk': (0.0, 2.0),
     'L0_attn_bv': (0.0, 0.1),
     'L0_attn_bo': (0.0, 0.1),
     'L1_xattn_bo': (0.0, 0.1)}
    factors = {'L1_xattn_Wq': 7.749,
     'L1_xattn_Wk': 8.0,
     'L1_xattn_Wk_ip': 8.0,
     'L1_xattn_Wk_ap': 8.0,
     'L1_xattn_rel_k': 32.346,
     'L1_xattn_rel_v': 5.68,
     'L1_ffn_b1': 8.0,
     'L1_ffn_b2': 2.925}
    for name, (base, spread) in spreads.items():
        noise = np.random.default_rng([zlib.crc32(name.encode()), seed]).standard_normal(out[name].shape)
        drawn = base * np.exp(spread * noise) if base else spread * noise
        out[name] = jnp.asarray(drawn.astype(out[name].dtype))
    for name, factor in factors.items():
        out[name] = (out[name] * factor).astype(out[name].dtype)
    return out
```

```python
from contextlib import ExitStack

import concourse.bass as bass
from concourse import mybir

F32 = mybir.dt.float32
BF16 = mybir.dt.bfloat16
ALU = mybir.AluOpType
ACT = mybir.ActivationFunctionType
AX_X = mybir.AxisListType.X

P = 128
B, S, E = 16, 112, 256
H, D = 16, 16
EC = E // P
HC = P // D
CTX = 375
TEXT, IMG = 77, 16
AUD = CTX - TEXT - IMG
HID = 1024
FC = HID // P
LN_EPS = 1e-5
ROUND = 12582912.0
TAKEN = -3.0e38
TOP_K = 32


def wait(engine, semaphore, value):
    if isinstance(value, int) and value <= 0:
        return
    engine.wait_ge(semaphore, value)


def wait_apart(engine, semaphore, value, passed):
    if isinstance(value, int) and value <= 0:
        return
    engine.wait_ge(semaphore, value)
    engine.sem_inc(passed, 1)


def sequences(engine, body):
    body(0, True, False)
    with engine.Fori(1, B - 1) as b:
        body(b, False, False)
    body(B - 1, False, True)


class Buffers:

    def __init__(self, nc, ctx, name, semaphores):
        self.nc, self.ctx, self.name, self.semaphores = nc, ctx, name, semaphores

    def sb(self, name, shape, dtype=F32):
        return self.ctx.enter_context(self.nc.sbuf_tensor(f"{self.name}_{name}", shape, dtype))

    def psum(self, name, dtype=F32):
        return self.ctx.enter_context(self.nc.psum_tensor(f"{self.name}_{name}", [P, 2048 // (4 if dtype == F32 else 2)], dtype))

    def sem(self, name):
        handle = self.nc.alloc_semaphore(name=f"{self.name}_{name}")
        self.semaphores.append(handle)
        return handle


def start_anew(nc, semaphores):
    nc.clear_and_free_semaphores(semaphores)
    semaphores.clear()
    nc.all_engine_barrier()


def row_of(x, b):
    return x[:, bass.ds(b, 1), :].rearrange("p a n -> p (a n)")


class Norm:

    def __init__(self, buf, shared):
        self.z = buf.sb("z", [S, E])
        self.stats = buf.sb("stats", [S, 6])
        self.mean_var = buf.sb("mean_var", [S, 2])
        self.rstd = buf.sb("rstd", [S, 1])
        self.shared = shared
        self.var_ready = buf.sem("var_ready")
        self.rstd_ready = buf.sem("rstd_ready")
        self.eps_added = buf.sem("eps_added")
        self.stats_ready = buf.sem("stats_ready")
        self.mean_ready = buf.sem("mean_ready")
        self.x_ready = buf.sem("x_ready")

    def vector(self, nc, dve, b, z_ready, count, passed):
        dve.wait_ge(z_ready, count)
        nc.vector.bn_stats(self.stats[:], self.z[:]).then_inc(self.stats_ready, 1)
        wait_apart(dve, self.stats_ready, b + 1, passed)
        nc.vector.bn_aggr(self.mean_var[:], self.stats[:]).then_inc(self.mean_ready, 1)
        dve.wait_ge(self.rstd_ready, b + 1)
        nc.vector.tensor_scalar(row_of(self.shared["x"], b), self.z[:], self.mean_var[:, 0:1], self.rstd[:, 0:1],
                                ALU.subtract, ALU.mult).then_inc(self.x_ready, 1)

    def gpsimd(self, nc, pool, b, passed):
        wait_apart(pool, self.mean_ready, b + 1, passed)
        nc.gpsimd.tensor_scalar(self.rstd[:], self.mean_var[:, 1:2], LN_EPS, None, ALU.add).then_inc(self.eps_added, 1)
        pool.wait_ge(self.eps_added, b + 1)
        nc.gpsimd.tensor_tensor(self.rstd[:], self.rstd[:], self.shared["minus_half"][:], ALU.pow).then_inc(
            self.rstd_ready, 1)


def self_attention(nc, shared, name, wq, wk, wv, wo, biases=None, pos=None):
    top_k = biases is not None
    G, HG = 4, 4
    T_LAG, AV_LAG = 2, 3
    DV = D + 1
    x, ident = shared["x"], shared["ident"]
    with ExitStack() as ctx:
        buf = Buffers(nc, ctx, name, shared["semaphores"])
        w_q, w_k, w_v, w_o = (buf.sb(n, [P, EC, E]) for n in ("w_q", "w_k", "w_v", "w_o"))
        head_mask = buf.sb("head_mask", [P, HC])
        xs = buf.sb("xs", [S, E])
        xT = buf.sb("xT", [P, EC, S])
        qT = buf.sb("qT", [P, EC, S])
        kT = buf.sb("kT", [P, EC, S])
        q_head = buf.sb("q_head", [P, EC, HC, S])
        v_one = buf.sb("v_one", [S, H, DV])
        s_sb = buf.sb("s_sb", [S, 2, HG, S])
        neg_max = buf.sb("neg_max", [S, 2, HG])
        probs = buf.sb("probs", [S, 2, HG, S])
        probsT = buf.sb("probsT", [S, 2, HG, S])
        rden = buf.sb("rden", [S, H])
        o_sb = buf.sb("o_sb", [S, E])
        oT = buf.sb("oT", [P, EC, S])
        norm = Norm(buf, shared)
        if top_k:
            b_q, b_k = buf.sb("b_q", [P, EC]), buf.sb("b_k", [P, EC])
            b_v, b_o = buf.sb("b_v", [S, E]), buf.sb("b_o", [S, E])
            top8 = buf.sb("top8", [S, 2, HG, TOP_K // 8, 8])
            left = buf.sb("left", [S, 2, HG, S])
            exps = buf.sb("exps", [S, 2, HG, S])
            taken = buf.sb("taken", [S, HG, S])
            z_raw = buf.sb("z_raw", [S, E])
        else:
            posT, causal = buf.sb("posT", [P, S]), buf.sb("causal", [S, S])
        ps_s = [buf.psum(f"ps_s{i}") for i in range(2)]
        ps_t = [buf.psum(f"ps_t{i}") for i in range(2)]
        ps_o = buf.psum("ps_o")
        ps_a, ps_b, ps_c = buf.psum("ps_a"), buf.psum("ps_b"), buf.psum("ps_c")

        loaded, passed = buf.sem("loaded"), buf.sem("passed")
        ones_ready = buf.sem("ones_ready")
        xs_ready, xT_raw, xT_ready = buf.sem("xs_ready"), buf.sem("xT_raw"), buf.sem("xT_ready")
        q_raw, q_ready, k_raw, k_ready = (buf.sem(n) for n in ("q_raw", "q_ready", "k_raw", "k_ready"))
        v_raw, v_ready, q_head_ready = buf.sem("v_raw"), buf.sem("v_ready"), buf.sem("q_head_ready")
        scores_raw, scores_ready = buf.sem("scores_raw"), buf.sem("scores_ready")
        top_first, top_chain, top_done = buf.sem("top_first"), buf.sem("top_chain"), buf.sem("top_done")
        neg_ready, exps_done = buf.sem("neg_ready"), buf.sem("exps_done")
        taken_ready, probs_ready = buf.sem("taken_ready"), buf.sem("probs_ready")
        probsT_raw, probsT_ready = buf.sem("probsT_raw"), buf.sem("probsT_ready")
        av_done, rden_ready, o_ready = buf.sem("av_done"), buf.sem("rden_ready"), buf.sem("o_ready")
        oT_raw, oT_ready, y_raw = buf.sem("oT_raw"), buf.sem("oT_ready"), buf.sem("y_raw")
        z_ready, zb_ready = buf.sem("z_ready"), buf.sem("zb_ready")

        loads = [(w_q, wq), (w_k, wk), (w_v, wv), (w_o, wo)]
        loads = [(to[:], a.rearrange("(c p) n -> p c n", p=P)) for to, a in loads]
        loads.append((head_mask[:], shared["mask16"] if top_k else shared["mask16_fine"]))
        if top_k:
            loads += [(b_q[:], biases[0]),
                      (b_k[:], biases[1]),
                      (b_v[:], biases[2].rearrange("(a n) -> a n", a=1).partition_broadcast(S)),
                      (b_o[:], biases[3].rearrange("(a n) -> a n", a=1).partition_broadcast(S))]
        else:
            loads += [(posT[:], pos[0]), (causal[:], pos[1])]

        all_loaded = 16 * len(loads)

        def back(b, g, lag):
            return (b, g - lag) if g >= lag else (b - 1, g - lag + G)

        block = ctx.enter_context(nc.Block())

        @block.sync
        def _(sp):
            for to, a in loads:
                sp.dma_start(to, a).then_inc(loaded, 16)

        @block.tensor
        def _(pe):
            def project_xT(b):
                pe.wait_ge(xs_ready, b + 1)
                wait(pe, v_ready, b)
                for c in range(EC):
                    last = nc.tensor.transpose(ps_a[:, c * S:(c + 1) * S], xs[:, c * P:(c + 1) * P], ident[:S, :S])
                last.then_inc(xT_raw, 1)

            def project_qk(b, w, out, raw):
                pe.wait_ge(xT_ready, b + 1)
                for m in range(EC):
                    for c in range(EC):
                        last = nc.tensor.matmul(out[:, m * S:(m + 1) * S], w[:, c, m * P:(m + 1) * P], xT[:, c, :],
                                                start=(c == 0), stop=(c == EC - 1))
                last.then_inc(raw, 1)

            def project_v(b):
                for c in range(EC):
                    last = nc.tensor.matmul(ps_a[:S, 0:E], xT[:, c, :], w_v[:, c, :], start=(c == 0), stop=(c == EC - 1))
                last.then_inc(v_raw, 1)

            def scores(b, g):
                if g == 0:
                    pe.wait_ge(q_head_ready, b + 1)
                    pe.wait_ge(k_ready, b + 1)
                wait(pe, scores_ready, b * G + g - 1)
                for i in range(HG):
                    h = g * HG + i
                    last = nc.tensor.matmul(ps_s[g % 2][:S, i * S:(i + 1) * S], q_head[:, h // HC, h % HC, :],
                                            kT[:, h // HC, :], start=True, stop=True)
                last.then_inc(scores_raw, 1)

            def turn_probs(b, g):
                pe.wait_ge(probs_ready, b * G + g + 1)
                wait(pe, probsT_ready, b * G + g - 1)
                for i in range(HG):
                    last = nc.tensor.transpose(ps_t[g % 2][:S, i * S:(i + 1) * S], probs[:, g % 2, i, :], ident[:S, :S])
                last.then_inc(probsT_raw, 1)

            def weigh_values(b, g):
                pe.wait_ge(probsT_ready, b * G + g + 1)
                if g == 0:
                    pe.wait_ge(v_ready, b + 1)
                    wait(pe, o_ready, b)
                for i in range(HG):
                    h = g * HG + i
                    last = nc.tensor.matmul(ps_o[:S, h * DV:(h + 1) * DV], probsT[:, g % 2, i, :], v_one[:, h, :],
                                            start=True, stop=True)
                last.then_inc(av_done, 1)

            def turn_output(b):
                pe.wait_ge(o_ready, b + 1)
                for c in range(EC):
                    last = nc.tensor.transpose(ps_b[:, c * S:(c + 1) * S], o_sb[:, c * P:(c + 1) * P], ident[:S, :S])
                last.then_inc(oT_raw, 1)

            def project_out(b):
                pe.wait_ge(oT_ready, b + 1)
                for c in range(EC):
                    last = nc.tensor.matmul(ps_c[:S, 0:E], oT[:, c, :], w_o[:, c, :], start=(c == 0), stop=(c == EC - 1))
                last.then_inc(y_raw, 1)

            pe.wait_ge(loaded, all_loaded)
            project_xT(0)
            project_qk(0, w_q, ps_b, q_raw)
            project_qk(0, w_k, ps_c, k_raw)

            def body(b, first, last):
                for g in range(G):
                    scores(b, g)
                    if g >= T_LAG or not first:
                        turn_probs(*back(b, g, T_LAG))
                    if g >= AV_LAG or not first:
                        weigh_values(*back(b, g, AV_LAG))
                    if g == AV_LAG - 1:
                        project_v(b)
                if not first:
                    turn_output(b - 1)
                if not last:
                    project_xT(b + 1)
                if not first:
                    project_out(b - 1)
                if not last:
                    wait(pe, oT_ready, b)
                    project_qk(b + 1, w_q, ps_b, q_raw)
                    wait(pe, z_ready, b)
                    project_qk(b + 1, w_k, ps_c, k_raw)

            sequences(pe, body)
            turn_probs(B - 1, G - 2)
            weigh_values(B - 1, G - 3)
            turn_probs(B - 1, G - 1)
            weigh_values(B - 1, G - 2)
            weigh_values(B - 1, G - 1)
            turn_output(B - 1)
            project_out(B - 1)

        @block.scalar
        def _(act):
            def take_xT(b):
                act.wait_ge(xT_raw, b + 1)
                wait(act, v_raw, b)
                nc.scalar.copy(xT[:], ps_a[:, 0:EC * S].rearrange("p (c s) -> p c s", c=EC)).then_inc(xT_ready, 1)

            def take_qk(b):
                act.wait_ge(q_raw, b + 1)
                wait(act, q_head_ready, b)
                for m in range(EC):
                    last = nc.scalar.activation(qT[:, m, :], ps_b[:, m * S:(m + 1) * S], ACT.Identity,
                                                bias=b_q[:, m:m + 1])
                last.then_inc(q_ready, 1)
                act.wait_ge(k_raw, b + 1)
                for m in range(EC):
                    last = nc.scalar.activation(kT[:, m, :], ps_c[:, m * S:(m + 1) * S], ACT.Identity,
                                                bias=b_k[:, m:m + 1])
                last.then_inc(k_ready, 1)

            def take_scores(b, g):
                act.wait_ge(scores_raw, b * G + g + 1)
                wait(act, top_done, b * G + g - 1)
                nc.scalar.copy(s_sb[:, g % 2], ps_s[g % 2][:S, 0:HG * S].rearrange("p (h s) -> p h s", h=HG)).then_inc(
                    scores_ready, 1)

            def exponentials(b, g):
                out, out_free = (exps, taken_ready) if top_k else (probs, probsT_raw)
                if top_k:
                    act.wait_ge(top_first, b * G + g + 1)
                    nc.scalar.mul(neg_max[:, g % 2, :], top8[:, g % 2, :, 0, 0], -1.0).then_inc(neg_ready, 1)
                    wait(act, probs_ready, b * G + g - 1)
                else:
                    wait(act, probsT_raw, b * G + g - 1)
                act.wait_ge(neg_ready, b * G + g + 1)
                for i in range(HG):
                    last = nc.scalar.activation(out[:, g % 2, i, :], s_sb[:, g % 2, i, :], ACT.Exp,
                                                bias=neg_max[:, g % 2, i:i + 1])
                last.then_inc(exps_done if top_k else probs_ready, 1)

            def take_probsT(b, g):
                act.wait_ge(probsT_raw, b * G + g + 1)
                wait(act, av_done, b * G + g - 1)
                nc.scalar.copy(probsT[:, g % 2], ps_t[g % 2][:S, 0:HG * S].rearrange("p (h s) -> p h s", h=HG)).then_inc(
                    probsT_ready, 1)

            def take_oT(b):
                act.wait_ge(oT_raw, b + 1)
                nc.scalar.copy(oT[:], ps_b[:, 0:EC * S].rearrange("p (c s) -> p c s", c=EC)).then_inc(oT_ready, 1)

            act.wait_ge(loaded, all_loaded)
            take_xT(0)
            if top_k:
                take_qk(0)

            def body(b, first, last):
                for g in range(G):
                    if top_k:
                        take_scores(b, g)
                    if g >= T_LAG or not first:
                        take_probsT(*back(b, g, T_LAG))
                    if g == G - 1:
                        if not first:
                            take_oT(b - 1)
                        if not last:
                            take_xT(b + 1)
                            if top_k:
                                take_qk(b + 1)
                    exponentials(b, g)

            sequences(act, body)
            take_probsT(B - 1, G - 2)
            take_probsT(B - 1, G - 1)
            take_oT(B - 1)

        @block.vector
        def _(dve):
            def search(b, g):
                wait_apart(dve, scores_ready, b * G + g + 1, passed)
                wait(dve, exps_done, b * G + g - 1)
                wait_apart(dve, taken_ready, b * G + g - 1, passed)
                steps = 2 * (TOP_K // 8)
                for r in range(TOP_K // 8):
                    source = s_sb if r == 0 else left
                    if r:
                        wait_apart(dve, top_chain, (b * G + g) * (steps - 2) + 2 * r - 1, passed)
                    for i in range(HG):
                        ins = nc.vector.max(top8[:, g % 2, i, r, :], source[:, g % 2, i, :])
                    if r == 0:
                        ins.then_inc(top_first, 1)
                        wait_apart(dve, top_first, b * G + g + 1, passed)
                    else:
                        ins.then_inc(top_chain, 1)
                        wait_apart(dve, top_chain, (b * G + g) * (steps - 2) + 2 * r, passed)
                    for i in range(HG):
                        ins = nc.vector.match_replace(left[:, g % 2, i, :], top8[:, g % 2, i, r, :],
                                                      source[:, g % 2, i, :], TAKEN)
                    if r == 0:
                        ins.then_inc(top_chain, 1)
                    elif r < TOP_K // 8 - 1:
                        ins.then_inc(top_chain, 1)
                    else:
                        ins.then_inc(top_done, 1)

            def mask_scores(b, g):
                dve.wait_ge(scores_raw, b * G + g + 1)
                wait(dve, probs_ready, b * G + g - 1)
                nc.vector.tensor_tensor(s_sb[:, g % 2], ps_s[g % 2][:S, 0:HG * S].rearrange("p (h s) -> p h s", h=HG),
                                        causal[:].unsqueeze(1).broadcast_to([S, HG, S]), ALU.add).then_inc(
                    scores_ready, 1)
                dve.wait_ge(scores_ready, b * G + g + 1)
                nc.vector.tensor_reduce(neg_max[:, g % 2, :], s_sb[:, g % 2], AX_X, ALU.max, negate=True).then_inc(
                    neg_ready, 1)

            def take_qk(b):
                pos_all = posT[:].unsqueeze(1).broadcast_to([P, EC, S])
                dve.wait_ge(q_raw, b + 1)
                wait(dve, q_head_ready, b)
                nc.vector.tensor_tensor(qT[:], ps_b[:, 0:EC * S].rearrange("p (c s) -> p c s", c=EC), pos_all,
                                        ALU.add).then_inc(q_ready, 1)
                dve.wait_ge(k_raw, b + 1)
                nc.vector.tensor_tensor(kT[:], ps_c[:, 0:EC * S].rearrange("p (c s) -> p c s", c=EC), pos_all,
                                        ALU.add).then_inc(k_ready, 1)

            def take_v(b):
                dve.wait_ge(v_raw, b + 1)
                wait(dve, av_done, b * G)
                v_ps = ps_a[:S, 0:E].rearrange("p (h d) -> p h d", h=H)
                if top_k:
                    nc.vector.tensor_tensor(v_one[:, :, 0:D], v_ps, b_v[:].rearrange("p (h d) -> p h d", h=H),
                                            ALU.add).then_inc(v_ready, 1)
                else:
                    nc.vector.tensor_copy(v_one[:, :, 0:D], v_ps).then_inc(v_ready, 1)

            def normalise(b):
                o_ps = ps_o[:S, 0:H * DV].rearrange("p (h d) -> p h d", h=H)
                dve.wait_ge(av_done, (b + 1) * G)
                nc.vector.reciprocal(rden[:], o_ps[:, :, D]).then_inc(rden_ready, 1)
                dve.wait_ge(rden_ready, b + 1)
                wait(dve, oT_raw, b)
                nc.vector.tensor_tensor(o_sb[:].rearrange("p (h d) -> p h d", h=H), o_ps[:, :, 0:D],
                                        rden[:].unsqueeze(2).broadcast_to([S, H, D]), ALU.mult).then_inc(o_ready, 1)

            def add_residual(b):
                dve.wait_ge(y_raw, b + 1)
                if top_k:
                    wait(dve, zb_ready, b)
                    nc.vector.tensor_tensor(z_raw[:], ps_c[:S, 0:E], row_of(x, b), ALU.add).then_inc(z_ready, 1)
                else:
                    wait(dve, norm.x_ready, b)
                    nc.vector.tensor_tensor(norm.z[:], ps_c[:S, 0:E], row_of(x, b), ALU.add).then_inc(z_ready, 1)

            dve.wait_ge(loaded, all_loaded)
            dve.wait_ge(ones_ready, 1)
            if not top_k:
                take_qk(0)
            softmax_start = search if top_k else mask_scores

            def body(b, first, last):
                softmax_start(b, 0)
                softmax_start(b, 1)
                if not top_k:
                    softmax_start(b, 2)
                if not first:
                    normalise(b - 1)
                take_v(b)
                if top_k:
                    softmax_start(b, 2)
                    if not first:
                        add_residual(b - 1)
                        norm.vector(nc, dve, b - 1, zb_ready, b, passed)
                softmax_start(b, 3)
                if not top_k:
                    if not first:
                        add_residual(b - 1)
                        norm.vector(nc, dve, b - 1, z_ready, b, passed)
                    if not last:
                        take_qk(b + 1)

            sequences(dve, body)
            normalise(B - 1)
            add_residual(B - 1)
            norm.vector(nc, dve, B - 1, zb_ready if top_k else z_ready, B, passed)

        @block.gpsimd
        def _(pool):
            def take_x(b):
                wait(pool, xT_raw, b)
                nc.gpsimd.tensor_copy(xs[:], row_of(x, b)).then_inc(xs_ready, 1)

            def spread_q(b):
                pool.wait_ge(q_ready, b + 1)
                wait(pool, scores_raw, b * G)
                for c in range(EC):
                    last = nc.gpsimd.tensor_tensor(q_head[:, c], qT[:, c, :].unsqueeze(1).broadcast_to([P, HC, S]),
                                                   head_mask[:].unsqueeze(2).broadcast_to([P, HC, S]), ALU.mult)
                last.then_inc(q_head_ready, 1)

            def keep_taken(b, g):
                wait(pool, probs_ready, b * G + g)
                wait_apart(pool, top_done, b * G + g + 1, passed)
                nc.gpsimd.tensor_scalar(taken[:], left[:, g % 2], TAKEN * 0.9, None, ALU.is_le).then_inc(taken_ready, 1)
                pool.wait_ge(taken_ready, b * G + g + 1)
                pool.wait_ge(exps_done, b * G + g + 1)
                wait(pool, probsT_raw, b * G + g - 1)
                nc.gpsimd.tensor_tensor(probs[:, g % 2], taken[:], exps[:, g % 2], ALU.mult).then_inc(probs_ready, 1)

            def add_bias(b):
                pool.wait_ge(z_ready, b + 1)
                wait(pool, norm.x_ready, b)
                nc.gpsimd.tensor_tensor(norm.z[:], z_raw[:], b_o[:], ALU.add).then_inc(zb_ready, 1)

            nc.gpsimd.memset(v_one[:], 1.0).then_inc(ones_ready, 1)
            pool.wait_ge(loaded, all_loaded)
            take_x(0)
            spread_q(0)

            def body(b, first, last):
                for g in range(G):
                    if g == G - 1:
                        if not last:
                            take_x(b + 1)
                        if not first:
                            if top_k:
                                add_bias(b - 1)
                            norm.gpsimd(nc, pool, b - 1, passed)
                    if top_k:
                        keep_taken(b, g)
                if not last:
                    spread_q(b + 1)

            sequences(pool, body)
            if top_k:
                add_bias(B - 1)
            norm.gpsimd(nc, pool, B - 1, passed)


def cross_attention_rope(nc, shared, name, ctxT, wq, wq_swap, wk, wk_swap, wv, wo, rope):
    KC = CTX // 3
    NC = CTX // KC
    T_LAG, AV_LAG = 2, 3
    DV = D + 1
    x, ident = shared["x"], shared["ident"]
    with ExitStack() as ctx:
        buf = Buffers(nc, ctx, name, shared["semaphores"])
        w_q, w_qs, w_k, w_ks, w_v, w_o = (buf.sb(n, [P, EC, E]) for n in ("w_q", "w_qs", "w_k", "w_ks", "w_v", "w_o"))
        cos_sin = buf.sb("cos_sin", [P, 2, CTX])
        head_mask = buf.sb("head_mask", [P, HC])
        context = buf.sb("context", [P, EC, CTX])
        xs = buf.sb("xs", [S, E])
        xT = buf.sb("xT", [P, EC, S])
        q_cos, q_sin, qT = (buf.sb(n, [P, EC, S]) for n in ("q_cos", "q_sin", "qT"))
        k_cos, k_sin, kT = (buf.sb(n, [P, EC, CTX]) for n in ("k_cos", "k_sin", "kT"))
        q_head = buf.sb("q_head", [P, EC, HC, S])
        v_one = buf.sb("v_one", [KC, NC, H, DV])
        neg_max = buf.sb("neg_max", [S, 2])
        probs = buf.sb("probs", [S, 2, CTX])
        probsT = buf.sb("probsT", [KC, 2, NC, S])
        rden = buf.sb("rden", [S, H])
        o_sb = buf.sb("o_sb", [S, E])
        oT = buf.sb("oT", [P, EC, S])
        norm = Norm(buf, shared)
        ps_s = [buf.psum(f"ps_s{i}") for i in range(2)]
        ps_t = [buf.psum(f"ps_t{i}") for i in range(2)]
        ps_o = buf.psum("ps_o")
        ps_a, ps_b, ps_c = buf.psum("ps_a"), buf.psum("ps_b"), buf.psum("ps_c")

        loaded, ones_ready, passed = buf.sem("loaded"), buf.sem("ones_ready"), buf.sem("passed")
        context_loaded = buf.sem("context_loaded")
        xs_ready, xT_raw, xT_ready = buf.sem("xs_ready"), buf.sem("xT_raw"), buf.sem("xT_ready")
        q_raw, q_turned, q_ready, q_head_ready = (buf.sem(n) for n in ("q_raw", "q_turned", "q_ready", "q_head_ready"))
        k_raw = [buf.sem(f"k_raw{m}") for m in range(EC)]
        k_turned = [buf.sem(f"k_turned{m}") for m in range(EC)]
        k_ready = [buf.sem(f"k_ready{m}") for m in range(EC)]
        v_raw, v_ready = buf.sem("v_raw"), buf.sem("v_ready")
        scores_raw, max_ready, probs_ready = buf.sem("scores_raw"), buf.sem("max_ready"), buf.sem("probs_ready")
        probsT_raw, probsT_ready, av_done = buf.sem("probsT_raw"), buf.sem("probsT_ready"), buf.sem("av_done")
        rden_ready, o_ready = buf.sem("rden_ready"), buf.sem("o_ready")
        oT_raw, oT_ready, y_raw, z_ready = (buf.sem(n) for n in ("oT_raw", "oT_ready", "y_raw", "z_ready"))

        loads = [(w_q, wq), (w_qs, wq_swap), (w_k, wk), (w_ks, wk_swap), (w_v, wv), (w_o, wo)]
        loads = [(to[:], a.rearrange("(c p) n -> p c n", p=P)) for to, a in loads]
        loads += [(cos_sin[:], rope), (head_mask[:], shared["mask16"])]
        all_loaded = 16 * len(loads)
        context_of = ctxT.rearrange("(c p) b t -> p c b t", p=P)

        def back(b, h, lag):
            return (b, h - lag) if h >= lag else (b - 1, h - lag + H)

        block = ctx.enter_context(nc.Block())

        @block.sync
        def _(sp):
            for to, a in loads:
                sp.dma_start(to, a).then_inc(loaded, 16)

        @block.tensor
        def _(pe):
            def project_xT(b):
                pe.wait_ge(xs_ready, b + 1)
                for c in range(EC):
                    last = nc.tensor.transpose(ps_a[:, c * S:(c + 1) * S], xs[:, c * P:(c + 1) * P], ident[:S, :S])
                last.then_inc(xT_raw, 1)

            def project_q(b, w, out):
                pe.wait_ge(xT_ready, b + 1)
                for m in range(EC):
                    for c in range(EC):
                        last = nc.tensor.matmul(out[:, m * S:(m + 1) * S], w[:, c, m * P:(m + 1) * P], xT[:, c, :],
                                                start=(c == 0), stop=(c == EC - 1))
                last.then_inc(q_raw, 1)

            def project_k(b, m, w, out):
                pe.wait_ge(context_loaded, 16 * (b + 1))
                for c in range(EC):
                    last = nc.tensor.matmul(out[:, 0:CTX], w[:, c, m * P:(m + 1) * P], context[:, c, :],
                                            start=(c == 0), stop=(c == EC - 1))
                last.then_inc(k_raw[m], 1)

            def project_v(b):
                for t in range(NC):
                    out = (ps_a[:KC, 0:E], ps_a[:KC, E:2 * E], ps_b[:KC, 0:E])[t]
                    for c in range(EC):
                        last = nc.tensor.matmul(out, context[:, c, t * KC:(t + 1) * KC], w_v[:, c, :],
                                                start=(c == 0), stop=(c == EC - 1))
                last.then_inc(v_raw, 1)

            def scores(b, h):
                if h == 0:
                    pe.wait_ge(q_head_ready, EC * b + 1)
                    pe.wait_ge(k_ready[0], b + 1)
                if h == HC:
                    pe.wait_ge(q_head_ready, EC * b + 2)
                    pe.wait_ge(k_ready[1], b + 1)
                wait(pe, probs_ready, b * H + h - 1)
                nc.tensor.matmul(ps_s[h % 2][:S, 0:CTX], q_head[:, h // HC, h % HC, :], kT[:, h // HC, :],
                                 start=True, stop=True).then_inc(scores_raw, 1)

            def turn_probs(b, h):
                pe.wait_ge(probs_ready, b * H + h + 1)
                wait(pe, probsT_ready, b * H + h - 1)
                for t in range(NC):
                    last = nc.tensor.transpose(ps_t[h % 2][:KC, t * S:(t + 1) * S],
                                               probs[:, h % 2, t * KC:(t + 1) * KC], ident[:S, :S])
                last.then_inc(probsT_raw, 1)

            def weigh_values(b, h):
                pe.wait_ge(probsT_ready, b * H + h + 1)
                if h == 0:
                    pe.wait_ge(v_ready, b + 1)
                    wait(pe, o_ready, b)
                for t in range(NC):
                    last = nc.tensor.matmul(ps_o[:S, h * DV:(h + 1) * DV], probsT[:, h % 2, t, :], v_one[:, t, h, :],
                                            start=(t == 0), stop=(t == NC - 1))
                last.then_inc(av_done, 1)

            def turn_output(b):
                pe.wait_ge(o_ready, b + 1)
                for c in range(EC):
                    last = nc.tensor.transpose(ps_b[:, c * S:(c + 1) * S], o_sb[:, c * P:(c + 1) * P], ident[:S, :S])
                last.then_inc(oT_raw, 1)

            def project_out(b):
                pe.wait_ge(oT_ready, b + 1)
                for c in range(EC):
                    last = nc.tensor.matmul(ps_c[:S, 0:E], oT[:, c, :], w_o[:, c, :], start=(c == 0), stop=(c == EC - 1))
                last.then_inc(y_raw, 1)

            pe.wait_ge(loaded, all_loaded)
            project_xT(0)
            project_q(0, w_q, ps_b)
            project_q(0, w_qs, ps_c)
            project_k(0, 0, w_k, ps_a)
            pe.wait_ge(q_turned, 1)
            project_k(0, 0, w_ks, ps_b)

            def body(b, first, last):
                for h in range(H):
                    scores(b, h)
                    if h >= T_LAG or not first:
                        turn_probs(*back(b, h, T_LAG))
                    if h >= AV_LAG or not first:
                        weigh_values(*back(b, h, AV_LAG))
                    if h == AV_LAG - 1:
                        pe.wait_ge(k_turned[0], b + 1)
                        project_v(b)
                        pe.wait_ge(q_turned, b + 1)
                        project_k(b, 1, w_k, ps_c)
                        pe.wait_ge(v_ready, b + 1)
                        project_k(b, 1, w_ks, ps_a)
                    if h == 5 and not first:
                        turn_output(b - 1)
                    if h == 6 and not first:
                        pe.wait_ge(k_turned[1], b + 1)
                        project_out(b - 1)
                    if not last:
                        if h == 8:
                            pe.wait_ge(k_turned[1], b + 1)
                            project_xT(b + 1)
                        if h == 9:
                            wait(pe, oT_ready, b)
                            project_q(b + 1, w_q, ps_b)
                        if h == 10:
                            wait(pe, z_ready, b)
                            project_q(b + 1, w_qs, ps_c)
                        if h == 11:
                            project_k(b + 1, 0, w_k, ps_a)
                        if h == 12:
                            pe.wait_ge(q_turned, b + 2)
                            project_k(b + 1, 0, w_ks, ps_b)

            sequences(pe, body)
            turn_probs(B - 1, H - 2)
            weigh_values(B - 1, H - 3)
            turn_probs(B - 1, H - 1)
            weigh_values(B - 1, H - 2)
            weigh_values(B - 1, H - 1)
            turn_output(B - 1)
            project_out(B - 1)

        @block.scalar
        def _(act):
            def take_xT(b):
                act.wait_ge(xT_raw, b + 1)
                nc.scalar.copy(xT[:], ps_a[:, 0:EC * S].rearrange("p (c s) -> p c s", c=EC)).then_inc(xT_ready, 1)

            def take_v(b):
                act.wait_ge(v_raw, b + 1)
                nc.scalar.copy(v_one[:, 0:2, :, 0:D], ps_a[:KC, :].rearrange("p (t h d) -> p t h d", t=2, h=H))
                nc.scalar.copy(v_one[:, 2, :, 0:D], ps_b[:KC, 0:E].rearrange("p (h d) -> p h d", h=H)).then_inc(v_ready, 1)

            def exponentials(b, h):
                act.wait_ge(max_ready, b * H + h + 1)
                wait(act, probsT_raw, b * H + h - 1)
                nc.scalar.activation(probs[:, h % 2, :], ps_s[h % 2][:S, 0:CTX], ACT.Exp,
                                     bias=neg_max[:, h % 2:h % 2 + 1]).then_inc(probs_ready, 1)

            def take_oT(b):
                act.wait_ge(oT_raw, b + 1)
                nc.scalar.copy(oT[:], ps_b[:, 0:EC * S].rearrange("p (c s) -> p c s", c=EC)).then_inc(oT_ready, 1)

            act.wait_ge(ones_ready, 1)
            take_xT(0)

            def load_context(b):
                act.dma_start(context[:], context_of[:, :, bass.ds(b, 1), :].rearrange("p c b t -> p c (b t)")).then_inc(
                    context_loaded, 16)

            load_context(0)

            def body(b, first, last):
                for h in range(H):
                    exponentials(b, h)
                    if h == AV_LAG - 1:
                        take_v(b)
                    if h == 4 and not last:
                        act.wait_ge(k_raw[1], 2 * (b + 1))
                        load_context(b + 1)
                    if h == 5 and not first:
                        take_oT(b - 1)
                    if h == 8 and not last:
                        take_xT(b + 1)

            sequences(act, body)
            take_oT(B - 1)

        @block.vector
        def _(dve):
            def row_max(b, h):
                dve.wait_ge(scores_raw, b * H + h + 1)
                wait(dve, probs_ready, b * H + h - 1)
                nc.vector.tensor_reduce(neg_max[:, h % 2:h % 2 + 1], ps_s[h % 2][:S, 0:CTX], AX_X, ALU.max,
                                        negate=True).then_inc(max_ready, 1)

            def take_probsT(b, h):
                dve.wait_ge(probsT_raw, b * H + h + 1)
                wait(dve, av_done, b * H + h - 1)
                nc.vector.tensor_copy(probsT[:, h % 2], ps_t[h % 2][:KC, 0:NC * S].rearrange(
                    "p (t s) -> p t s", t=NC)).then_inc(probsT_ready, 1)

            def turn_q(b):
                dve.wait_ge(q_raw, 2 * (b + 1))
                wait(dve, q_ready, b)
                for which, ps, out in ((0, ps_b, q_cos), (1, ps_c, q_sin)):
                    last = nc.vector.tensor_tensor(out[:], ps[:, 0:EC * S].rearrange("p (c s) -> p c s", c=EC),
                                                   cos_sin[:, which, 0:S].unsqueeze(1).broadcast_to([P, EC, S]), ALU.mult)
                last.then_inc(q_turned, 1)

            def turn_k(b, m, ps_plain, ps_swapped):
                dve.wait_ge(k_raw[m], 2 * (b + 1))
                wait(dve, k_ready[m], b)
                nc.vector.tensor_tensor(k_cos[:, m], ps_plain[:, 0:CTX], cos_sin[:, 0, :], ALU.mult)
                nc.vector.tensor_tensor(k_sin[:, m], ps_swapped[:, 0:CTX], cos_sin[:, 1, :], ALU.mult).then_inc(
                    k_turned[m], 1)

            def normalise(b):
                o_ps = ps_o[:S, 0:H * DV].rearrange("p (h d) -> p h d", h=H)
                dve.wait_ge(av_done, (b + 1) * H)
                nc.vector.reciprocal(rden[:], o_ps[:, :, D]).then_inc(rden_ready, 1)
                dve.wait_ge(rden_ready, b + 1)
                wait(dve, oT_raw, b)
                nc.vector.tensor_tensor(o_sb[:].rearrange("p (h d) -> p h d", h=H), o_ps[:, :, 0:D],
                                        rden[:].unsqueeze(2).broadcast_to([S, H, D]), ALU.mult).then_inc(o_ready, 1)

            def add_residual(b):
                dve.wait_ge(y_raw, b + 1)
                wait(dve, norm.x_ready, b)
                nc.vector.tensor_tensor(norm.z[:], ps_c[:S, 0:E], row_of(x, b), ALU.add).then_inc(z_ready, 1)

            dve.wait_ge(loaded, all_loaded)
            turn_q(0)
            turn_k(0, 0, ps_a, ps_b)

            def body(b, first, last):
                for h in range(H):
                    row_max(b, h)
                    if h >= T_LAG or not first:
                        take_probsT(*back(b, h, T_LAG))
                    if h == AV_LAG - 1:
                        if not first:
                            normalise(b - 1)
                    if h == AV_LAG:
                        turn_k(b, 1, ps_c, ps_a)
                    if h == 7 and not first:
                        add_residual(b - 1)
                        norm.vector(nc, dve, b - 1, z_ready, b, passed)
                    if h == 11 and not last:
                        turn_q(b + 1)
                    if h == 13 and not last:
                        turn_k(b + 1, 0, ps_a, ps_b)

            sequences(dve, body)
            take_probsT(B - 1, H - 2)
            take_probsT(B - 1, H - 1)
            normalise(B - 1)
            add_residual(B - 1)
            norm.vector(nc, dve, B - 1, z_ready, B, passed)

        @block.gpsimd
        def _(pool):
            def take_x(b):
                wait(pool, xT_raw, b)
                nc.gpsimd.tensor_copy(xs[:], row_of(x, b)).then_inc(xs_ready, 1)

            def add_q(b):
                pool.wait_ge(q_turned, b + 1)
                wait(pool, q_head_ready, EC * b)
                nc.gpsimd.tensor_tensor(qT[:], q_cos[:], q_sin[:], ALU.add).then_inc(q_ready, 1)

            def spread_q(b, c):
                pool.wait_ge(q_ready, b + 1)
                wait(pool, scores_raw, (b - 1) * H + (c + 1) * HC)
                nc.gpsimd.tensor_tensor(q_head[:, c], qT[:, c, :].unsqueeze(1).broadcast_to([P, HC, S]),
                                        head_mask[:].unsqueeze(2).broadcast_to([P, HC, S]), ALU.mult).then_inc(
                    q_head_ready, 1)

            def add_k(b, m):
                pool.wait_ge(k_turned[m], b + 1)
                wait(pool, scores_raw, (b - 1) * H + (m + 1) * HC)
                nc.gpsimd.tensor_tensor(kT[:, m], k_cos[:, m], k_sin[:, m], ALU.add).then_inc(k_ready[m], 1)

            nc.gpsimd.memset(v_one[:], 1.0).then_inc(ones_ready, 1)
            pool.wait_ge(loaded, all_loaded)
            take_x(0)
            add_q(0)
            spread_q(0, 0)
            add_k(0, 0)

            def body(b, first, last):
                spread_q(b, 1)
                add_k(b, 1)
                if not first:
                    norm.gpsimd(nc, pool, b - 1, passed)
                if not last:
                    take_x(b + 1)
                    add_q(b + 1)
                    spread_q(b + 1, 0)
                    add_k(b + 1, 0)

            sequences(pool, body)
            norm.gpsimd(nc, pool, B - 1, passed)


def ffn_quantised(nc, shared, name, w1T, conv_w, conv_b, w2T):
    x, ident = shared["x"], shared["ident"]
    HALF = FC // 2
    with ExitStack() as ctx:
        buf = Buffers(nc, ctx, name, shared["semaphores"])
        raw = [buf.sb(f"raw{i}", [P, EC * HID]) for i in range(2)]
        w1 = buf.sb("w1", [P, EC, HID], BF16)
        w2 = buf.sb("w2", [P, FC, E], BF16)
        w_abs = buf.sb("w_abs", [P, EC * HID])
        taps, conv_bias = buf.sb("taps", [P, FC, 3]), buf.sb("conv_bias", [P, FC])
        ones, ident_bf = buf.sb("ones", [P, P]), buf.sb("ident_bf", [P, P], BF16)
        abs_sum, mean_abs, w_scale = (buf.sb(n, [P, 2]) for n in ("abs_sum", "mean_abs", "w_scale"))
        peak, peak_clip, inverse, scale, unscale = (buf.sb(n, [S, 2]) for n in (
            "peak", "peak_clip", "inverse", "scale", "unscale"))
        x_round, xq = buf.sb("x_round", [S, E]), buf.sb("xq", [S, E], BF16)
        xqT = buf.sb("xqT", [P, EC, S], BF16)
        unscale_diag, unscale_row = buf.sb("unscale_diag", [S, S]), buf.sb("unscale_row", [P, S])
        h = buf.sb("h", [P, FC, S + 2])
        conv, act_out = buf.sb("conv", [P, FC, S]), buf.sb("act_out", [P, FC, S])
        h_round, hq = buf.sb("h_round", [S, HID]), buf.sb("hq", [S, HID], BF16)
        hqT = buf.sb("hqT", [P, FC, S], BF16)
        norm = Norm(buf, shared)
        ps_xT, ps_row = buf.psum("ps_xT", BF16), buf.psum("ps_row")
        ps_h = [buf.psum(f"ps_h{i}") for i in range(2)]
        ps_u = ctx.enter_context(nc.psum_tensor(f"{name}_ps_u", [P, HID], F32))
        ps_hT, ps_y = buf.psum("ps_hT", BF16), buf.psum("ps_y")

        loaded, passed, passed_pool, zeroed = (buf.sem(n) for n in ("loaded", "passed", "passed_pool", "zeroed"))
        scale_ready = [buf.sem(f"scale_ready{i}") for i in range(2)]
        abs_done, w_sum_done, w_prep = buf.sem("abs_done"), buf.sem("w_sum_done"), buf.sem("w_prep")
        prep_chain, peak_chain = buf.sem("prep_chain"), [buf.sem(f"peak_chain{i}") for i in range(2)]
        unscale_ready, diag_ready = buf.sem("unscale_ready"), buf.sem("diag_ready")
        x_rounded, xq_ready, xqT_raw, xqT_ready = (buf.sem(n) for n in ("x_rounded", "xq_ready", "xqT_raw", "xqT_ready"))
        row_raw, row_ready, h_raw, h_ready = (buf.sem(n) for n in ("row_raw", "row_ready", "h_raw", "h_ready"))
        middle_done, tap0_done, conv_done, silu_done = (buf.sem(n) for n in (
            "middle_done", "tap0_done", "conv_done", "silu_done"))
        turned, h_rounded, hq_ready, hqT_raw, hqT_ready = (buf.sem(n) for n in (
            "turned", "h_rounded", "hq_ready", "hqT_raw", "hqT_ready"))
        y_raw, z_ready = buf.sem("y_raw"), buf.sem("z_ready")

        loads = [(raw[0][:].rearrange("p (c n) -> p c n", c=EC), w1T.rearrange("(c p) n -> p c n", p=P)),
                 (raw[1][:].rearrange("p (c n) -> p c n", c=FC), w2T.rearrange("(c p) n -> p c n", p=P)),
                 (taps[:], conv_w.rearrange("(c p) k -> p c k", p=P)), (conv_bias[:], conv_b)]
        all_loaded = 16 * len(loads)
        block = ctx.enter_context(nc.Block())

        @block.sync
        def _(sp):
            for to, a in loads:
                sp.dma_start(to, a).then_inc(loaded, 16)

        @block.tensor
        def _(pe):
            def turn_x(b):
                pe.wait_ge(xq_ready, b + 1)
                wait(pe, xqT_ready, b)
                for c in range(EC):
                    last = nc.tensor.transpose(ps_xT[:, c * S:(c + 1) * S], xq[:, c * P:(c + 1) * P], ident_bf[:S, :S])
                last.then_inc(xqT_raw, 1)
                pe.wait_ge(diag_ready, b + 1)
                wait(pe, row_ready, b)
                nc.tensor.matmul(ps_row[:, 0:S], ones[:S, :], unscale_diag[:], start=True, stop=True).then_inc(row_raw, 1)

            def up(b):
                pe.wait_ge(xqT_ready, b + 1)
                wait(pe, h_ready, 2 * b)
                for m in range(FC):
                    for c in range(EC):
                        last = nc.tensor.matmul(ps_h[m // HALF][:, m % HALF * S:(m % HALF + 1) * S],
                                                w1[:, c, m * P:(m + 1) * P], xqT[:, c, :],
                                                start=(c == 0), stop=(c == EC - 1))
                    if m % HALF == HALF - 1:
                        last.then_inc(h_raw, 1)

            def turn_hidden(b):
                wait(pe, h_rounded, b)
                for m in range(FC):
                    if m % HALF == 0:
                        pe.wait_ge(silu_done, 2 * b + m // HALF + 1)
                    last = nc.tensor.transpose(ps_u[:S, m * P:(m + 1) * P], act_out[:, m, :], ident[:])
                last.then_inc(turned, 1)

            def turn_quantised(b):
                pe.wait_ge(hq_ready, b + 1)
                wait(pe, hqT_ready, b)
                for m in range(FC):
                    last = nc.tensor.transpose(ps_hT[:, m * S:(m + 1) * S], hq[:, m * P:(m + 1) * P], ident_bf[:S, :S])
                last.then_inc(hqT_raw, 1)

            def down(b):
                pe.wait_ge(hqT_ready, b + 1)
                wait(pe, z_ready, b)
                for m in range(FC):
                    last = nc.tensor.matmul(ps_y[:S, 0:E], hqT[:, m, :], w2[:, m, :], start=(m == 0), stop=(m == FC - 1))
                last.then_inc(y_raw, 1)

            pe.wait_ge(zeroed, 4)
            pe.wait_ge(abs_done, 2)
            nc.tensor.matmul(ps_row[:, 0:2], ones[:], abs_sum[:], start=True, stop=True).then_inc(w_sum_done, 1)
            pe.wait_ge(w_prep, 2)
            turn_x(0)
            up(0)

            def body(b, first, last):
                turn_hidden(b)
                if not last:
                    turn_x(b + 1)
                    up(b + 1)
                turn_quantised(b)
                down(b)

            sequences(pe, body)

        @block.scalar
        def _(act):
            def take_xT(b):
                act.wait_ge(xqT_raw, b + 1)
                wait(act, h_raw, 2 * b)
                nc.scalar.copy(xqT[:], ps_xT[:, 0:EC * S].rearrange("p (c s) -> p c s", c=EC)).then_inc(xqT_ready, 1)
                act.wait_ge(row_raw, b + 1)
                wait(act, h_ready, 2 * b)
                nc.scalar.copy(unscale_row[:], ps_row[:, 0:S]).then_inc(row_ready, 1)

            def middle_tap(b):
                act.wait_ge(h_ready, 2 * (b + 1))
                wait(act, silu_done, 2 * b)
                for m in range(FC):
                    last = nc.scalar.activation(conv[:, m, :], h[:, m, 1:S + 1], ACT.Identity,
                                                bias=conv_bias[:, m:m + 1], scale=taps[:, m, 1:2])
                last.then_inc(middle_done, 1)

            def silu(b):
                act.wait_ge(conv_done, b + 1)
                wait(act, turned, b)
                for i in range(2):
                    nc.scalar.activation(act_out[:, i * HALF:(i + 1) * HALF, :], conv[:, i * HALF:(i + 1) * HALF, :],
                                         ACT.Silu).then_inc(silu_done, 1)

            def take_hqT(b):
                act.wait_ge(hqT_raw, b + 1)
                wait(act, y_raw, b)
                nc.scalar.copy(hqT[:], ps_hT[:, 0:FC * S].rearrange("p (c s) -> p c s", c=FC)).then_inc(hqT_ready, 1)

            act.wait_ge(loaded, all_loaded)
            for i in range(2):
                wait(act, abs_done, i)
                nc.scalar.activation(w_abs[:], raw[i][:], ACT.Abs, accum_out=abs_sum[:, i:i + 1]).then_inc(abs_done, 1)
            take_xT(0)
            middle_tap(0)
            silu(0)

            def body(b, first, last):
                if not last:
                    take_xT(b + 1)
                take_hqT(b)
                if not last:
                    middle_tap(b + 1)
                    silu(b + 1)

            sequences(act, body)

        @block.vector
        def _(dve):
            def scales(b, i):
                n = (2, 3)[i] * b
                wait_apart(dve, peak_chain[i], n + 1, passed)
                nc.vector.tensor_scalar(peak_clip[:, i:i + 1], peak[:, i:i + 1], 1e-5, None, ALU.max).then_inc(
                    peak_chain[i], 1)
                wait_apart(dve, peak_chain[i], n + 2, passed)
                nc.vector.reciprocal(inverse[:, i:i + 1], peak_clip[:, i:i + 1])
                nc.vector.tensor_scalar(unscale[:, i:i + 1], peak_clip[:, i:i + 1], 1.0 / 127.0, mean_abs[:S, i:i + 1],
                                        ALU.mult, ALU.mult).then_inc(unscale_ready if i == 0 else peak_chain[i], 1)
                if i == 0:
                    wait_apart(dve, unscale_ready, b + 1, passed)
                else:
                    wait_apart(dve, peak_chain[i], n + 3, passed)
                nc.vector.tensor_scalar(scale[:, i:i + 1], inverse[:, i:i + 1], 127.0, None, ALU.mult).then_inc(
                    scale_ready[i], 1)
                dve.wait_ge(scale_ready[i], b + 1)

            def quantise_x(b):
                wait(dve, diag_ready, b)
                nc.vector.tensor_reduce(peak[:, 0:1], row_of(x, b), AX_X, ALU.max, apply_absolute_value=True).then_inc(
                    peak_chain[0], 1)
                scales(b, 0)
                nc.vector.tensor_scalar(x_round[:], row_of(x, b), scale[:, 0:1], ROUND, ALU.mult, ALU.add).then_inc(
                    x_rounded, 1)
                dve.wait_ge(x_rounded, b + 1)
                wait(dve, xqT_raw, b)
                nc.vector.tensor_scalar(xq[:], x_round[:], ROUND, 127.0, ALU.subtract, ALU.min).then_inc(xq_ready, 1)

            def convolve(b):
                dve.wait_ge(row_ready, b + 1)
                for i in range(2):
                    dve.wait_ge(h_raw, 2 * b + i + 1)
                    nc.vector.tensor_tensor(h[:, i * HALF:(i + 1) * HALF, 1:S + 1],
                                            ps_h[i][:, 0:HALF * S].rearrange("p (c s) -> p c s", c=HALF),
                                            unscale_row[:].unsqueeze(1).broadcast_to([P, HALF, S]), ALU.mult).then_inc(
                        h_ready, 1)
                dve.wait_ge(middle_done, b + 1)
                for k, done in ((0, tap0_done), (2, conv_done)):
                    if k:
                        dve.wait_ge(tap0_done, b + 1)
                    for m in range(FC):
                        last = nc.vector.scalar_tensor_tensor(conv[:, m, :], h[:, m, k:k + S], taps[:, m, k:k + 1],
                                                              conv[:, m, :], ALU.mult, ALU.add)
                    last.then_inc(done, 1)

            def quantise_hidden(b):
                dve.wait_ge(turned, b + 1)
                nc.vector.tensor_reduce(peak[:, 1:2], ps_u[:S, :], AX_X, ALU.max, apply_absolute_value=True).then_inc(
                    peak_chain[1], 1)
                scales(b, 1)
                nc.vector.tensor_scalar(h_round[:], ps_u[:S, :], scale[:, 1:2], ROUND, ALU.mult, ALU.add).then_inc(
                    h_rounded, 1)
                dve.wait_ge(h_rounded, b + 1)
                wait(dve, hqT_raw, b)
                nc.vector.tensor_scalar(hq[:], h_round[:], ROUND, 127.0, ALU.subtract, ALU.min).then_inc(hq_ready, 1)

            def add_residual(b):
                dve.wait_ge(y_raw, b + 1)
                nc.vector.scalar_tensor_tensor(norm.z[:], ps_y[:S, 0:E], unscale[:, 1:2], row_of(x, b), ALU.mult,
                                               ALU.add).then_inc(z_ready, 1)

            dve.wait_ge(loaded, all_loaded)
            dve.wait_ge(w_sum_done, 1)
            dve.wait_ge(zeroed, 4)
            nc.vector.tensor_scalar(mean_abs[:], ps_row[:, 0:2], 1.0 / (E * HID), 1e-5, ALU.mult, ALU.max).then_inc(
                prep_chain, 1)
            dve.wait_ge(prep_chain, 1)
            nc.vector.reciprocal(w_scale[:], mean_abs[:]).then_inc(prep_chain, 1)
            dve.wait_ge(prep_chain, 2)
            for i, w in enumerate((w1, w2)):
                nc.vector.tensor_scalar(raw[i][:], raw[i][:], w_scale[:, i:i + 1], ROUND, ALU.mult, ALU.add).then_inc(
                    prep_chain, 1)
                dve.wait_ge(prep_chain, 3 + 2 * i)
                nc.vector.tensor_scalar(raw[i][:], raw[i][:], ROUND, 1.0, ALU.subtract, ALU.min).then_inc(prep_chain, 1)
                dve.wait_ge(prep_chain, 4 + 2 * i)
                nc.vector.tensor_scalar(w[:].rearrange("p c n -> p (c n)"), raw[i][:], -1.0, None, ALU.max).then_inc(
                    w_prep, 1)
            quantise_x(0)
            convolve(0)

            def body(b, first, last):
                if not last:
                    quantise_x(b + 1)
                quantise_hidden(b)
                if not last:
                    convolve(b + 1)
                add_residual(b)
                norm.vector(nc, dve, b, z_ready, b + 1, passed)

            sequences(dve, body)

        @block.gpsimd
        def _(pool):
            def scale_diagonal(b):
                wait(pool, row_raw, b)
                wait_apart(pool, unscale_ready, b + 1, passed_pool)
                nc.gpsimd.tensor_scalar(unscale_diag[:], ident[:S, :S], unscale[:, 0:1], None, ALU.mult).then_inc(
                    diag_ready, 1)

            nc.gpsimd.memset(ones[:], 1.0).then_inc(zeroed, 1)
            nc.gpsimd.tensor_copy(ident_bf[:], ident[:]).then_inc(zeroed, 1)
            for at in (0, S + 1):
                nc.gpsimd.memset(h[:, :, at:at + 1], 0.0).then_inc(zeroed, 1)
            scale_diagonal(0)

            def body(b, first, last):
                if not last:
                    scale_diagonal(b + 1)
                norm.gpsimd(nc, pool, b, passed_pool)

            sequences(pool, body)


def cross_attention_relative(nc, shared, name, a):
    K4 = 4
    NG = B // K4
    DH = 64
    NP = H // 2
    HH = H // 2
    AUD_C = AUD // 3
    IMG_AT = 96
    TI = IMG_AT + IMG
    PW = TI + AUD
    WIDE = S - 1 + TEXT
    T_LAG, AV_LAG = 3, 4
    RING = 4
    QI = 512 // (K4 * H)
    VI = 8
    x, ident = shared["x"], shared["ident"]
    with ExitStack() as ctx:
        buf = Buffers(nc, ctx, name, shared["semaphores"])
        w_q = buf.sb("w_q", [P, EC, H * DH])
        w_k = [buf.sb(f"w_k{n}", [P, EC, H * DH]) for n in ("", "_image", "_audio")]
        w_v = [buf.sb(f"w_v{n}", [P, EC, H * DH]) for n in ("", "_image", "_audio")]
        w_o = buf.sb("w_o", [P, NP, E])
        b_o = buf.sb("b_o", [S, E])
        gain = buf.sb("gain", [S, 3])
        rel_k = buf.sb("rel_k", [P, WIDE])
        rel_v = buf.sb("rel_v", [TEXT, 2, VI, DH])
        context = buf.sb("context", [P, 2, EC, CTX])
        xs = buf.sb("xs", [S, E])
        xT = buf.sb("xT", [P, EC, S])
        q_head = buf.sb("q_head", [P, K4, H, S])
        turned = buf.sb("turned", [TI, K4, H, S])
        outT = buf.sb("outT", [P, K4, NP, S])
        kT = buf.sb("kT", [P, NP, CTX])
        v = buf.sb("v", [TI, 4, H * DH])
        neg_max, total, inverse = (buf.sb(n, [S, RING, 3]) for n in ("neg_max", "total", "inverse"))
        probs = buf.sb("probs", [S, RING, PW])
        audT = buf.sb("audT", [AUD_C, 2, 3, S])
        norm = Norm(buf, shared)
        z_raw = buf.sb("z_raw", [S, E])
        ps_s = [buf.psum(f"ps_s{i}") for i in range(2)]
        ps_t = [buf.psum(f"ps_t{i}") for i in range(2)]
        ps_o = [buf.psum(f"ps_o{i}") for i in range(2)]
        ps_p = [buf.psum(f"ps_p{i}") for i in range(2)]

        loaded, passed, passed_pool, passed_sp = (buf.sem(n) for n in ("loaded", "passed", "passed_pool", "passed_sp"))
        zeroed, gain_ready, rel_k_ready, tanh_done = (buf.sem(n) for n in ("zeroed", "gain_ready", "rel_k_ready", "tanh_done"))
        context_loaded = [buf.sem(f"context_loaded{i}") for i in range(2)]
        rel_v_loaded = [buf.sem(f"rel_v_loaded{i}") for i in range(2)]
        raw = [buf.sem(f"raw{i}") for i in range(2)]
        taken = [buf.sem(f"taken{i}") for i in range(2)]
        xs_ready = buf.sem("xs_ready")
        rel_raw, rel_taken = [buf.sem(f"rel_raw{i}") for i in range(2)], [buf.sem(f"rel_taken{i}") for i in range(2)]
        scores_raw, max_ready, exps_done, inverse_ready = (buf.sem(n) for n in (
            "scores_raw", "max_ready", "exps_done", "inverse_ready"))
        probs_ready, probsT_raw, probsT_ready, av_done = (buf.sem(n) for n in (
            "probs_ready", "probsT_raw", "probsT_ready", "av_done"))
        out_taken = [buf.sem(f"out_taken{i}") for i in range(2)]
        rel_v_raw, rel_v_added = buf.sem("rel_v_raw"), buf.sem("rel_v_added")
        zb_ready = buf.sem("zb_ready")

        def use_x(k):
            return 3 * k

        def use_q(k, j):
            return 3 * k + 1 + j

        def use_k(k, m):
            return 3 * K4 + 16 * k + m

        def use_v(k, j):
            return use_k(k, 8 + j)

        EVEN = (3 * K4 + 16 * K4) // 2
        USES = (EVEN, EVEN + K4)

        def bank_count(g, u):
            return u % 2, USES[u % 2] * g + u // 2

        def head_count(g, k, h):
            return (g * K4 + k) * H + h + 1

        columns = ((0, TEXT), (TEXT, TEXT + IMG), (TEXT + IMG, CTX))
        places = ((0, TEXT), (IMG_AT, TI), (TI, PW))

        W = "L1_xattn_"
        loads = [(w_q, a[W + "Wq"])] + [(w_k[i], a[W + n]) for i, n in enumerate(("Wk", "Wk_ip", "Wk_ap"))]
        loads += [(w_v[i], a[W + n]) for i, n in enumerate(("Wv", "Wv_ip", "Wv_ap"))] + [(w_o, a[W + "Wo"])]
        loads = [(to[:], w.rearrange("(c p) n -> p c n", p=P)) for to, w in loads]
        loads += [(b_o[:], a[W + "bo"].rearrange("(a n) -> a n", a=1).partition_broadcast(S)),
                  (gain[:, 1:2], a[W + "alpha"].partition_broadcast(S)),
                  (gain[:, 2:3], a[W + "beta"].partition_broadcast(S)),
                  (rel_k[0:DH, S - 17:S + 16], a[W + "rel_k"]), (rel_k[DH:P, S - 17:S + 16], a[W + "rel_k"])]
        all_loaded = 16 * len(loads)
        context_of = a["ctxT"].rearrange("(c p) b t -> p c b t", p=P)
        wide = a["rel_v_wide"]

        def groups(engine, body):
            body(0, True)
            with engine.Fori(1, NG) as g:
                body(g, False)

        block = ctx.enter_context(nc.Block())

        @block.sync
        def _(sp):
            for to, w in loads:
                sp.dma_start(to, w).then_inc(loaded, 16)

            def load_context(g, k):
                if k >= 2 or not isinstance(g, int):
                    i, n = bank_count(g, use_v(k - 2, 7)) if k >= 2 else bank_count(g - 1, use_v(k + 2, 7))
                    wait_apart(sp, raw[i], n + 1, passed_sp)
                sp.dma_start(context[:, k % 2], context_of[:, :, bass.ds(g * K4 + k, 1), :].rearrange(
                    "p c b t -> p c (b t)")).then_inc(context_loaded[k % 2], 16)

            def load_rel_v(g, n):
                if n >= 2 or not isinstance(g, int):
                    wait_apart(sp, rel_v_raw, g * (S // VI) + n - 1, passed_sp)
                source = bass.AP(tensor=wide.tensor, offset=n * VI * DH, ap=[[DH, TEXT], [1, VI * DH]])
                sp.dma_start(rel_v[:, n % 2].rearrange("p i d -> p (i d)"), source).then_inc(rel_v_loaded[n % 2], 16)

            def body(g, first):
                for k in range(K4):
                    load_context(g, k)
                for n in range(S // VI):
                    load_rel_v(g, n)

            groups(sp, body)

        @block.tensor
        def _(pe):
            def free_bank(g, u):
                i, n = bank_count(g, u)
                wait(pe, taken[i], n)
                return i

            def project_x(g, k):
                pe.wait_ge(xs_ready, g * K4 + k + 1)
                i = free_bank(g, use_x(k))
                for c in range(EC):
                    last = nc.tensor.transpose(ps_p[i][:, c * S:(c + 1) * S], xs[:, c * P:(c + 1) * P], ident[:S, :S])
                last.then_inc(raw[i], 1)

            def project_q(g, k, j):
                if j == 0:
                    xi, xn = bank_count(g, use_x(k))
                    pe.wait_ge(taken[xi], xn + 1)
                i = free_bank(g, use_q(k, j))
                for m in range(4):
                    for c in range(EC):
                        at = (4 * j + m) * P
                        last = nc.tensor.matmul(ps_p[i][:, m * S:(m + 1) * S], w_q[:, c, at:at + P], xT[:, c, :],
                                                start=(c == 0), stop=(c == EC - 1))
                last.then_inc(raw[i], 1)

            def relative_keys(g):
                for n in range(S // QI):
                    if n == 0:
                        for i in range(2):
                            u = use_k(0, 0) - 2 + i
                            pe.wait_ge(taken[u % 2], bank_count(g, u)[1] + 1)
                        wait(pe, exps_done, head_count(g, 0, -1))
                    wait(pe, rel_taken[n % 2], g * (S // QI // 2) + n // 2)
                    for j in range(QI):
                        i = n * QI + j
                        last = nc.tensor.matmul(ps_s[n % 2][:TEXT, j * K4 * H:(j + 1) * K4 * H],
                                                rel_k[:, S - 1 - i:S - 1 - i + TEXT],
                                                q_head[:, :, :, i].rearrange("p k h -> p (k h)"), start=True, stop=True)
                    last.then_inc(rel_raw[n % 2], 1)

            def project_k(g, k, m):
                i = free_bank(g, use_k(k, m))
                if m == 0:
                    pe.wait_ge(context_loaded[k % 2], 16 * (g * (K4 // 2) + k // 2 + 1))
                for w, (lo, hi) in zip(w_k, columns):
                    for c in range(EC):
                        last = nc.tensor.matmul(ps_p[i][:, lo:hi], w[:, c, m * P:(m + 1) * P],
                                                context[:, k % 2, c, lo:hi], start=(c == 0), stop=(c == EC - 1))
                last.then_inc(raw[i], 1)

            def project_v(g, k, j):
                t, half = j // 2, slice(j % 2 * 512, j % 2 * 512 + 512)
                i = free_bank(g, use_v(k, j))
                if t == 0:
                    parts = [(0, TEXT, 0, w_v[0]), (IMG_AT, IMG, TEXT, w_v[1])]
                else:
                    parts = [(0, AUD_C, TEXT + IMG + (t - 1) * AUD_C, w_v[2])]
                for row, rows, token, w in parts:
                    for c in range(EC):
                        last = nc.tensor.matmul(ps_p[i][row:row + rows, :], context[:, k % 2, c, token:token + rows],
                                                w[:, c, half], start=(c == 0), stop=(c == EC - 1),
                                                tile_position=(0, row))
                last.then_inc(raw[i], 1)

            def scores(g, k, h):
                n = head_count(g, k, h)
                if h == 0:
                    u = use_v(k, 0) - 2
                    for i in range(2):
                        pe.wait_ge(taken[(u + i) % 2], bank_count(g, u + i)[1] + 1)
                    if k == 0:
                        for i in range(2):
                            pe.wait_ge(rel_taken[i], (g + 1) * (S // QI // 2))
                wait(pe, exps_done, n - 2)
                out = ps_s[h % 2]
                nc.tensor.matmul(out[:S, 0:CTX], q_head[:, k, h, :], kT[:, h // 2, :], start=True, stop=False)
                nc.tensor.matmul(out[:S, 0:TEXT], turned[:TEXT, k, h, :], ident[:TEXT, :TEXT], start=False,
                                 stop=True).then_inc(scores_raw, 1)

            def turn_probs(g, k, h):
                n = head_count(g, k, h)
                pe.wait_ge(probs_ready, n)
                wait(pe, probsT_ready, n - 2)
                if k == 0 and h < 2:
                    wait(pe, rel_v_added, g * (S // VI))
                out, slot = ps_t[h % 2], h % RING
                nc.tensor.transpose(out[:TI, 0:S], probs[:, slot, 0:TI], ident[:S, :S])
                for t in range(3):
                    at = TI + t * AUD_C
                    last = nc.tensor.transpose(out[:AUD_C, (t + 1) * S:(t + 2) * S], probs[:, slot, at:at + AUD_C],
                                               ident[:S, :S])
                last.then_inc(probsT_raw, 1)

            def weigh_values(g, k, h):
                pe.wait_ge(probsT_ready, head_count(g, k, h))
                if h % HH == 0:
                    wait(pe, out_taken[h // HH], g * K4 + k)
                if h == 0:
                    for i in range(2):
                        u = use_v(k, 6 + i)
                        pe.wait_ge(taken[u % 2], bank_count(g, u)[1] + 1)
                row, at = h % 2 * DH, h % HH // 2 * S
                out = ps_o[h // HH][row:row + DH, at:at + S]
                feat = slice(h * DH, (h + 1) * DH)
                nc.tensor.matmul(out, v[:TI, 0, feat], turned[:TI, k, h, :], start=True, stop=False,
                                 tile_position=(0, row), skip_group_check=True)
                for t in range(3):
                    last = nc.tensor.matmul(out, v[:AUD_C, t + 1, feat], audT[:, h % 2, t, :], start=False, stop=(t == 2),
                                            tile_position=(0, row), skip_group_check=True)
                last.then_inc(av_done, 1)

            def relative_values(g):
                for n in range(S // VI):
                    pe.wait_ge(rel_v_loaded[n % 2], 16 * (g * (S // VI // 2) + n // 2 + 1))
                    wait(pe, rel_v_added, g * (S // VI) + n - 1)
                    for j in range(VI):
                        i, at = S - 1 - (n * VI + j), (VI - 1 - j) * K4 * NP
                        for odd in range(2):
                            row = odd * DH
                            last = nc.tensor.matmul(ps_t[n % 2][row:row + DH, at:at + K4 * NP], rel_v[:, n % 2, j, :],
                                                    turned[:TEXT, :, odd:H:2, i], start=True, stop=True,
                                                    tile_position=(0, row))
                    last.then_inc(rel_v_raw, 1)

            def project_out(g, k):
                if k == 0:
                    pe.wait_ge(rel_v_added, (g + 1) * (S // VI))
                wait(pe, taken[1], USES[1] * g + EVEN + k)
                for m in range(NP):
                    last = nc.tensor.matmul(ps_p[1][:S, 0:E], outT[:, k, m, :], w_o[:, m, :], start=(m == 0),
                                            stop=(m == NP - 1))
                last.then_inc(raw[1], 1)

            pe.wait_ge(loaded, all_loaded)
            pe.wait_ge(zeroed, 3)
            pe.wait_ge(rel_k_ready, 1)

            def body(g, first):
                for k in range(K4):
                    project_x(g, k)
                    project_q(g, k, 0)
                    project_q(g, k, 1)
                relative_keys(g)
                for m in range(NP):
                    project_k(g, 0, m)
                for k in range(K4):
                    for j in range(8):
                        project_v(g, k, j)
                    for h in range(H + AV_LAG):
                        if h < H:
                            scores(g, k, h)
                        if T_LAG <= h < H + T_LAG:
                            turn_probs(g, k, h - T_LAG)
                        if AV_LAG <= h:
                            weigh_values(g, k, h - AV_LAG)
                        if h >= H and k < K4 - 1:
                            project_k(g, k + 1, 2 * (h - H))
                            project_k(g, k + 1, 2 * (h - H) + 1)
                relative_values(g)
                for k in range(K4):
                    project_out(g, k)

            groups(pe, body)

        @block.scalar
        def _(act):
            def arrived(g, u):
                act.wait_ge(raw[0], bank_count(g, u)[1] + 1)

            def take_x(g, k):
                arrived(g, use_x(k))
                nc.scalar.copy(xT[:], ps_p[0][:, 0:EC * S].rearrange("p (c s) -> p c s", c=EC)).then_inc(taken[0], 1)

            def take_q(g, k, j):
                arrived(g, use_q(k, j))
                if k == 0:
                    wait(act, scores_raw, head_count(g, 0, -1))
                for odd in range(2):
                    rows = slice(odd * DH, odd * DH + DH)
                    last = nc.scalar.mul(q_head[rows, k, 8 * j + odd:8 * j + 8:2, :],
                                         ps_p[0][rows, 0:4 * S].rearrange("p (m s) -> p m s", m=4), DH ** -0.5)
                last.then_inc(taken[0], 1)

            def take_rel(g, n):
                act.wait_ge(rel_raw[0], g * (S // QI // 2) + n // 2 + 1)
                wait(act, rel_v_raw, g * (S // VI))
                nc.scalar.copy(turned[:TEXT, :, :, n * QI:(n + 1) * QI].rearrange("p k h i -> p (k h) i"),
                               ps_s[0][:TEXT, :].rearrange("p (i n) -> p n i", i=QI)).then_inc(rel_taken[0], 1)

            def take_k(g, k, m):
                arrived(g, use_k(k, m))
                wait(act, scores_raw, head_count(g, k, -1))
                nc.scalar.copy(kT[:, m, :], ps_p[0][:, 0:CTX]).then_inc(taken[0], 1)

            def take_v(g, k, j):
                t, half = j // 2, slice(j % 2 * 512, j % 2 * 512 + 512)
                arrived(g, use_v(k, j))
                wait(act, av_done, head_count(g, k, -1))
                if t == 0:
                    nc.scalar.copy(v[:TEXT, 0, half], ps_p[0][:TEXT, :])
                    nc.scalar.copy(v[IMG_AT:TI, 0, half], ps_p[0][IMG_AT:TI, :]).then_inc(taken[0], 1)
                else:
                    nc.scalar.copy(v[:AUD_C, t, half], ps_p[0][:AUD_C, :]).then_inc(taken[0], 1)

            def exponentials(g, k, h):
                n = head_count(g, k, h)
                act.wait_ge(max_ready, n)
                wait(act, probsT_raw, n - RING)
                wait(act, inverse_ready, n - RING)
                slot = h % RING
                for j in range(3):
                    lo, hi = columns[j]
                    to, end = places[j]
                    last = nc.scalar.activation(probs[:, slot, to:end], ps_s[h % 2][:S, lo:hi], ACT.Exp,
                                                bias=neg_max[:, slot, j:j + 1], accum_out=total[:, slot, j:j + 1])
                last.then_inc(exps_done, 1)

            def take_out(g, k, half):
                act.wait_ge(av_done, head_count(g, k, (half + 1) * HH - 1))
                if k == 0:
                    wait(act, raw[1], USES[1] * g)
                nc.scalar.copy(outT[:, k, half * 4:half * 4 + 4, :],
                               ps_o[half][:, 0:4 * S].rearrange("p (m s) -> p m s", m=4)).then_inc(out_taken[half], 1)

            act.wait_ge(loaded, all_loaded)
            nc.scalar.activation(gain[:, 1:3], gain[:, 1:3], ACT.Tanh).then_inc(tanh_done, 1)
            act.wait_ge(zeroed, 3)

            def mine(u):
                return u % 2 == 0

            def body(g, first):
                for k in range(K4):
                    if mine(use_x(k)):
                        take_x(g, k)
                    for j in range(2):
                        if mine(use_q(k, j)):
                            take_q(g, k, j)
                for n in range(0, S // QI, 2):
                    take_rel(g, n)
                for m in range(0, NP, 2):
                    take_k(g, 0, m)
                for k in range(K4):
                    for j in range(0, 8, 2):
                        take_v(g, k, j)
                    for h in range(H + AV_LAG):
                        if h < H:
                            exponentials(g, k, h)
                        if h == HH + AV_LAG:
                            take_out(g, k, 0)
                        if h >= H and k < K4 - 1:
                            take_k(g, k + 1, 2 * (h - H))
                    take_out(g, k, 1)

            groups(act, body)

        @block.vector
        def _(dve):
            def arrived(g, u):
                dve.wait_ge(raw[1], bank_count(g, u)[1] + 1)

            def take_x(g, k):
                arrived(g, use_x(k))
                nc.vector.tensor_copy(xT[:], ps_p[1][:, 0:EC * S].rearrange("p (c s) -> p c s", c=EC)).then_inc(taken[1], 1)

            def take_q(g, k, j):
                arrived(g, use_q(k, j))
                if k == 0:
                    wait(dve, scores_raw, head_count(g, 0, -1))
                for odd in range(2):
                    rows = slice(odd * DH, odd * DH + DH)
                    last = nc.vector.tensor_scalar(q_head[rows, k, 8 * j + odd:8 * j + 8:2, :],
                                                   ps_p[1][rows, 0:4 * S].rearrange("p (m s) -> p m s", m=4),
                                                   DH ** -0.5, None, ALU.mult)
                last.then_inc(taken[1], 1)

            def take_rel(g, n):
                dve.wait_ge(rel_raw[1], g * (S // QI // 2) + n // 2 + 1)
                wait(dve, rel_v_raw, g * (S // VI))
                nc.vector.tensor_copy(turned[:TEXT, :, :, n * QI:(n + 1) * QI].rearrange("p k h i -> p (k h) i"),
                                      ps_s[1][:TEXT, :].rearrange("p (i n) -> p n i", i=QI)).then_inc(rel_taken[1], 1)

            def take_k(g, k, m):
                arrived(g, use_k(k, m))
                wait(dve, scores_raw, head_count(g, k, -1))
                nc.vector.tensor_copy(kT[:, m, :], ps_p[1][:, 0:CTX]).then_inc(taken[1], 1)

            def take_v(g, k, j):
                t, half = j // 2, slice(j % 2 * 512, j % 2 * 512 + 512)
                arrived(g, use_v(k, j))
                wait(dve, av_done, head_count(g, k, -1))
                if t == 0:
                    nc.vector.tensor_copy(v[:TEXT, 0, half], ps_p[1][:TEXT, :])
                    nc.vector.tensor_copy(v[IMG_AT:TI, 0, half], ps_p[1][IMG_AT:TI, :]).then_inc(taken[1], 1)
                else:
                    nc.vector.tensor_copy(v[:AUD_C, t, half], ps_p[1][:AUD_C, :]).then_inc(taken[1], 1)

            def row_max(g, k, h):
                n = head_count(g, k, h)
                dve.wait_ge(scores_raw, n)
                wait(dve, exps_done, n - RING)
                for j, (lo, hi) in enumerate(columns):
                    last = nc.vector.tensor_reduce(neg_max[:, h % RING, j:j + 1], ps_s[h % 2][:S, lo:hi], AX_X, ALU.max,
                                                   negate=True)
                last.then_inc(max_ready, 1)

            def invert(g, k, h):
                n = head_count(g, k, h)
                dve.wait_ge(exps_done, n)
                wait(dve, probs_ready, n - RING)
                nc.vector.reciprocal(inverse[:, h % RING, :], total[:, h % RING, :]).then_inc(inverse_ready, 1)

            def take_probsT(g, k, h):
                n = head_count(g, k, h)
                dve.wait_ge(probsT_raw, n)
                wait(dve, av_done, n - 2)
                nc.vector.tensor_copy(turned[:, k, h, :], ps_t[h % 2][:TI, 0:S])
                nc.vector.tensor_copy(audT[:, h % 2], ps_t[h % 2][:AUD_C, S:4 * S].rearrange(
                    "p (t s) -> p t s", t=3)).then_inc(probsT_ready, 1)

            def add_rel_v(g, n):
                dve.wait_ge(rel_v_raw, g * (S // VI) + n + 1)
                if n == 0:
                    for i in range(2):
                        dve.wait_ge(out_taken[i], (g + 1) * K4)
                lo = S - (n + 1) * VI
                to = outT[:, :, :, lo:lo + VI].rearrange("p k m i -> p (k m) i")
                nc.vector.tensor_tensor(to, ps_t[n % 2][:, 0:VI * K4 * NP].rearrange("p (i n) -> p n i", i=VI), to,
                                        ALU.add).then_inc(rel_v_added, 1)

            def add_residual(g, k):
                b = g * K4 + k
                dve.wait_ge(raw[1], USES[1] * g + EVEN + k + 1)
                wait(dve, zb_ready, b)
                nc.vector.tensor_tensor(z_raw[:], ps_p[1][:S, 0:E], row_of(x, b), ALU.add).then_inc(taken[1], 1)

            dve.wait_ge(loaded, all_loaded)
            nc.vector.tensor_copy(rel_k[:, 0:S - 17], rel_k[:, S - 17:S - 16].broadcast_to([P, S - 17]))
            nc.vector.tensor_copy(rel_k[:, S + 16:WIDE], rel_k[:, S + 15:S + 16].broadcast_to([P, WIDE - S - 16])).then_inc(
                rel_k_ready, 1)
            dve.wait_ge(tanh_done, 1)
            nc.vector.tensor_scalar(gain[:, 1:3], gain[:, 1:3], 1.0, None, ALU.add).then_inc(gain_ready, 1)
            dve.wait_ge(zeroed, 3)

            def mine(u):
                return u % 2 == 1

            def body(g, first):
                for k in range(K4):
                    if mine(use_x(k)):
                        take_x(g, k)
                    for j in range(2):
                        if mine(use_q(k, j)):
                            take_q(g, k, j)
                for n in range(1, S // QI, 2):
                    take_rel(g, n)
                for m in range(1, NP, 2):
                    take_k(g, 0, m)
                for k in range(K4):
                    for j in range(1, 8, 2):
                        take_v(g, k, j)
                    for h in range(H + AV_LAG):
                        if h < H:
                            row_max(g, k, h)
                        if 1 <= h <= H:
                            invert(g, k, h - 1)
                        if T_LAG <= h < H + T_LAG:
                            take_probsT(g, k, h - T_LAG)
                        if h >= H and k < K4 - 1:
                            take_k(g, k + 1, 2 * (h - H) + 1)
                for n in range(S // VI):
                    add_rel_v(g, n)
                for k in range(K4):
                    add_residual(g, k)
                    norm.vector(nc, dve, g * K4 + k, zb_ready, g * K4 + k + 1, passed)

            groups(dve, body)

        @block.gpsimd
        def _(pool):
            def take_x(g, k):
                b = g * K4 + k
                if k > 0:
                    i, n = bank_count(g, use_x(k - 1))
                    wait(pool, raw[i], n + 1)
                nc.gpsimd.tensor_copy(xs[:], row_of(x, b)).then_inc(xs_ready, 1)

            def normalise(g, k, h):
                n = head_count(g, k, h)
                wait_apart(pool, inverse_ready, n, passed_pool)
                for j, (lo, hi) in enumerate(places):
                    at = probs[:, h % RING, lo:hi]
                    last = nc.gpsimd.tensor_scalar(at, at, inverse[:, h % RING, j:j + 1], gain[:, j:j + 1], ALU.mult,
                                                   ALU.mult)
                last.then_inc(probs_ready, 1)

            def add_bias(g, k):
                b = g * K4 + k
                pool.wait_ge(taken[1], USES[1] * g + EVEN + k + 1)
                wait(pool, norm.x_ready, b)
                nc.gpsimd.tensor_tensor(norm.z[:], z_raw[:], b_o[:], ALU.add).then_inc(zb_ready, 1)

            nc.gpsimd.memset(q_head[:], 0.0).then_inc(zeroed, 1)
            nc.gpsimd.memset(v[:], 0.0).then_inc(zeroed, 1)
            nc.gpsimd.memset(probs[:], 0.0).then_inc(zeroed, 1)
            nc.gpsimd.memset(gain[:, 0:1], 1.0)
            pool.wait_ge(gain_ready, 1)

            def body(g, first):
                for k in range(K4):
                    take_x(g, k)
                for k in range(K4):
                    for h in range(H):
                        normalise(g, k, h)
                for k in range(K4):
                    add_bias(g, k)
                    norm.gpsimd(nc, pool, g * K4 + k, passed_pool)

            groups(pool, body)


def ffn_binary(nc, shared, name, a):
    x, ident = shared["x"], shared["ident"]
    HALF = FC // 2
    with ExitStack() as ctx:
        buf = Buffers(nc, ctx, name, shared["semaphores"])
        w1, w2 = buf.sb("w1", [P, EC, HID]), buf.sb("w2", [P, FC, E])
        w1_rows, w2_rows = buf.sb("w1_rows", [P, FC, E]), buf.sb("w2_rows", [P, EC, HID])
        negative = buf.sb("negative", [P, EC * HID])
        alpha1, alpha2 = buf.sb("alpha1", [P, FC]), buf.sb("alpha2", [P, EC])
        alpha2_diag, alpha2_row = buf.sb("alpha2_diag", [P, E]), buf.sb("alpha2_row", [S, E])
        bias1, bias2 = buf.sb("bias1", [P, FC]), buf.sb("bias2", [S, E])
        ones = buf.sb("ones", [P, P])
        xs, xT = buf.sb("xs", [S, E]), buf.sb("xT", [P, EC, S])
        hidden = buf.sb("hidden", [P, FC, S])
        x_bias, z_raw = buf.sb("x_bias", [S, E]), buf.sb("z_raw", [S, E])
        norm = Norm(buf, shared)
        ps_x, ps_y, ps_w = buf.psum("ps_x"), buf.psum("ps_y"), buf.psum("ps_w")
        ps_h = [buf.psum(f"ps_h{i}") for i in range(2)]

        loaded, passed, passed_pool, ones_ready = (buf.sem(n) for n in ("loaded", "passed", "passed_pool", "ones_ready"))
        prep, signs_ready, diag_ready, row_raw, row_ready = (buf.sem(n) for n in (
            "prep", "signs_ready", "diag_ready", "row_raw", "row_ready"))
        xs_ready, xT_raw, xT_ready, h_raw, gelu_done = (buf.sem(n) for n in (
            "xs_ready", "xT_raw", "xT_ready", "h_raw", "gelu_done"))
        y_raw, scaled, x_bias_ready, z_ready = (buf.sem(n) for n in ("y_raw", "scaled", "x_bias_ready", "z_ready"))

        loads = [(w1[:], a["L1_ffn_w1T"].rearrange("(c p) n -> p c n", p=P)),
                 (w2[:], a["L1_ffn_w2T"].rearrange("(c p) n -> p c n", p=P)),
                 (w1_rows[:], a["L1_ffn_w1"].rearrange("(c p) n -> p c n", p=P)),
                 (w2_rows[:], a["L1_ffn_w2"].rearrange("(c p) n -> p c n", p=P)),
                 (bias1[:], a["L1_ffn_b1"]),
                 (bias2[:], a["L1_ffn_b2"].rearrange("(a n) -> a n", a=1).partition_broadcast(S))]
        all_loaded = 16 * len(loads)
        block = ctx.enter_context(nc.Block())

        @block.sync
        def _(sp):
            for to, w in loads:
                sp.dma_start(to, w).then_inc(loaded, 16)

        @block.tensor
        def _(pe):
            def turn_x(b):
                pe.wait_ge(xs_ready, b + 1)
                wait(pe, xT_ready, b)
                for c in range(EC):
                    last = nc.tensor.transpose(ps_x[:, c * S:(c + 1) * S], xs[:, c * P:(c + 1) * P], ident[:S, :S])
                last.then_inc(xT_raw, 1)

            def up(b):
                pe.wait_ge(xT_ready, b + 1)
                for m in range(FC):
                    if m % HALF == 0:
                        wait(pe, gelu_done, 2 * (b - 1) + m // HALF + 1)
                    for c in range(EC):
                        last = nc.tensor.matmul(ps_h[m // HALF][:, m % HALF * S:(m % HALF + 1) * S],
                                                w1[:, c, m * P:(m + 1) * P], xT[:, c, :],
                                                start=(c == 0), stop=(c == EC - 1))
                    if m % HALF == HALF - 1:
                        last.then_inc(h_raw, 1)

            def down(b):
                wait(pe, scaled, b)
                for m in range(FC):
                    if m % HALF == 0:
                        pe.wait_ge(gelu_done, 2 * b + m // HALF + 1)
                    last = nc.tensor.matmul(ps_y[:S, 0:E], hidden[:, m, :], w2[:, m, :], start=(m == 0), stop=(m == FC - 1))
                last.then_inc(y_raw, 1)

            pe.wait_ge(diag_ready, 1)
            pe.wait_ge(ones_ready, 1)
            nc.tensor.matmul(ps_w[:S, 0:E], ones[:, 0:S], alpha2_diag[:], start=True, stop=True).then_inc(row_raw, 1)
            pe.wait_ge(signs_ready, 2)
            turn_x(0)
            up(0)

            def body(b, first, last):
                if not last:
                    turn_x(b + 1)
                down(b)
                if not last:
                    up(b + 1)

            sequences(pe, body)

        @block.scalar
        def _(act):
            def take_xT(b):
                act.wait_ge(xT_raw, b + 1)
                wait(act, h_raw, 2 * b)
                nc.scalar.copy(xT[:], ps_x[:, 0:EC * S].rearrange("p (c s) -> p c s", c=EC)).then_inc(xT_ready, 1)

            def gelu(b):
                wait(act, y_raw, b)
                for m in range(FC):
                    if m % HALF == 0:
                        act.wait_ge(h_raw, 2 * b + m // HALF + 1)
                    last = nc.scalar.activation(hidden[:, m, :], ps_h[m // HALF][:, m % HALF * S:(m % HALF + 1) * S],
                                                ACT.Gelu, bias=bias1[:, m:m + 1], scale=alpha1[:, m:m + 1])
                    if m % HALF == HALF - 1:
                        last.then_inc(gelu_done, 1)

            act.wait_ge(row_raw, 1)
            nc.scalar.copy(alpha2_row[:], ps_w[:S, 0:E]).then_inc(row_ready, 1)
            act.wait_ge(prep, 2)
            take_xT(0)
            gelu(0)

            def body(b, first, last):
                if not last:
                    take_xT(b + 1)
                    gelu(b + 1)

            sequences(act, body)

        @block.vector
        def _(dve):
            dve.wait_ge(loaded, all_loaded)
            nc.vector.tensor_reduce(alpha2[:], w2_rows[:], AX_X, ALU.add, apply_absolute_value=True)
            nc.vector.tensor_reduce(alpha1[:], w1_rows[:], AX_X, ALU.add, apply_absolute_value=True).then_inc(prep, 1)
            dve.wait_ge(prep, 1)
            nc.vector.tensor_scalar(alpha1[:], alpha1[:], 1.0 / E, None, ALU.mult)
            nc.vector.tensor_scalar(alpha2[:], alpha2[:], 1.0 / HID, None, ALU.mult).then_inc(prep, 1)
            dve.wait_ge(prep, 2)
            for c in range(EC):
                last = nc.vector.tensor_scalar(alpha2_diag[:, c * P:(c + 1) * P], ident[:], alpha2[:, c:c + 1], None,
                                               ALU.mult)
            last.then_inc(diag_ready, 1)
            for i, w in enumerate((w1, w2)):
                flat = w[:].rearrange("p c n -> p (c n)")
                wait(dve, signs_ready, i)
                nc.vector.tensor_scalar(negative[:], flat, 0.0, None, ALU.is_lt).then_inc(prep, 1)
                dve.wait_ge(prep, 3 + i)
                nc.vector.scalar_tensor_tensor(flat, flat, 0.0, negative[:], ALU.is_gt, ALU.subtract).then_inc(
                    signs_ready, 1)
            dve.wait_ge(row_ready, 1)

            def body(b, first, last):
                dve.wait_ge(y_raw, b + 1)
                nc.vector.tensor_tensor(z_raw[:], ps_y[:S, 0:E], alpha2_row[:], ALU.mult).then_inc(scaled, 1)
                dve.wait_ge(scaled, b + 1)
                dve.wait_ge(x_bias_ready, b + 1)
                nc.vector.tensor_tensor(norm.z[:], z_raw[:], x_bias[:], ALU.add).then_inc(z_ready, 1)
                norm.vector(nc, dve, b, z_ready, b + 1, passed)

            sequences(dve, body)

        @block.gpsimd
        def _(pool):
            def take_x(b):
                wait(pool, xT_raw, b)
                nc.gpsimd.tensor_copy(xs[:], row_of(x, b)).then_inc(xs_ready, 1)

            def add_bias(b):
                wait(pool, z_ready, b)
                nc.gpsimd.tensor_tensor(x_bias[:], row_of(x, b), bias2[:], ALU.add).then_inc(x_bias_ready, 1)

            nc.gpsimd.memset(ones[:], 1.0).then_inc(ones_ready, 1)
            pool.wait_ge(loaded, all_loaded)
            take_x(0)

            def body(b, first, last):
                if not last:
                    take_x(b + 1)
                add_bias(b)
                norm.gpsimd(nc, pool, b, passed_pool)

            sequences(pool, body)


def build(nc, a, out):
    with ExitStack() as ctx:
        semaphores = []
        buf = Buffers(nc, ctx, "all", semaphores)
        shared = {
            "semaphores": semaphores,
            "x": buf.sb("x", [S, B, E]),
            "ident": buf.sb("ident", [P, P]),
            "minus_half": buf.sb("minus_half", [S, 1]),
            "mask16": a["c_mask16"],
            "mask16_fine": a["c_mask16_fine"],
        }
        with ExitStack() as inner:
            start = Buffers(nc, inner, "start", semaphores)
            x_loaded, zeroed, ident_ready = start.sem("x_loaded"), start.sem("zeroed"), start.sem("ident_ready")
            block = inner.enter_context(nc.Block())

            @block.sync
            def _(sp):
                sp.dma_start(shared["x"][:], a["x"].rearrange("b s e -> s b e")).then_inc(x_loaded, 16)
                sp.wait_ge(x_loaded, 16)

            @block.gpsimd
            def _(pool):
                nc.gpsimd.memset(shared["ident"][:], 0.0).then_inc(zeroed, 1)
                nc.gpsimd.memset(shared["minus_half"][:], -0.5)
                pool.wait_ge(zeroed, 1)
                nc.gpsimd.affine_select(out=shared["ident"][:], in_=shared["ident"][:], compare_op=ALU.not_equal,
                                        fill=1.0, base=0, pattern=[[-1, P]], channel_multiplier=1).then_inc(
                    ident_ready, 1)
                pool.wait_ge(ident_ready, 1)

        start_anew(nc, semaphores)
        for n in range(LAYERS):
            if n == 0:
                self_attention(nc, shared, "l0sa", a["L0_attn_Wq"], a["L0_attn_Wk"], a["L0_attn_Wv"], a["L0_attn_Wo"],
                               biases=[a["L0_attn_bq"], a["L0_attn_bk"], a["L0_attn_bv"], a["L0_attn_bo"]])
            if n == 1:
                cross_attention_rope(nc, shared, "l0xa", a["ctxT"], a["L0_xattn_W_q"], a["L0_xattn_W_q_swap"],
                                     a["L0_xattn_W_k"], a["L0_xattn_W_k_swap"], a["L0_xattn_W_v"], a["L0_xattn_W_o"],
                                     a["c_rope"])
            if n == 2:
                ffn_quantised(nc, shared, "l0ff", a["L0_ffn_w1"], a["L0_ffn_conv_w"], a["L0_ffn_conv_b"], a["L0_ffn_w2"])
            if n == 3:
                self_attention(nc, shared, "l1sa", a["L1_attn_Wq"], a["L1_attn_Wk"], a["L1_attn_Wv"], a["L1_attn_Wo"],
                               pos=[a["c_posT"], a["c_causal"]])
            if n == 4:
                cross_attention_relative(nc, shared, "l1xa", a)
            if n == 5:
                ffn_binary(nc, shared, "l1ff", a)
            start_anew(nc, semaphores)

        with ExitStack() as inner:
            stored = Buffers(nc, inner, "end", semaphores).sem("stored")
            block = inner.enter_context(nc.Block())

            @block.sync
            def _(sp):
                sp.dma_start(out.rearrange("b s e -> s b e"), shared["x"][:]).then_inc(stored, 16)
                sp.wait_ge(stored, 16)


LAYERS = 6


def kernel(**inputs):
    import numpy as np
    import concourse.bacc as bacc
    from concourse.bass_utils import run_bass_kernel_spmd

    arrays = {n: np.ascontiguousarray(v) for n, v in inputs.items()}
    turned = ["L0_attn_Wq", "L0_attn_Wk", "L0_attn_Wv", "L0_attn_Wo", "L0_xattn_W_q", "L0_xattn_W_k", "L0_xattn_W_v",
              "L0_xattn_W_o", "L0_ffn_w1", "L0_ffn_w2"]
    for n in turned:
        arrays[n] = np.ascontiguousarray(arrays[n].T)
    for n in ("L0_attn_bq", "L0_attn_bk"):
        arrays[n] = np.ascontiguousarray(arrays[n].reshape(EC, P).T)
    swap = np.arange(E) ^ 1
    for n in ("L0_xattn_W_q", "L0_xattn_W_k"):
        arrays[n + "_swap"] = np.ascontiguousarray(arrays[n][:, swap])
    arrays["ctxT"] = np.ascontiguousarray(arrays.pop("ctx_1024").transpose(2, 0, 1))
    arrays["L0_ffn_conv_w"] = np.ascontiguousarray(arrays["L0_ffn_conv_w"].reshape(HID, 3))
    for n in ("L0_ffn_conv_b", "L1_ffn_b1"):
        arrays[n] = np.ascontiguousarray(arrays[n].reshape(FC, P).T)
    arrays["L1_ffn_w1T"] = np.ascontiguousarray(arrays["L1_ffn_w1"].T)
    arrays["L1_ffn_w2T"] = np.ascontiguousarray(arrays["L1_ffn_w2"].T)
    for n in ("L1_xattn_alpha", "L1_xattn_beta"):
        arrays[n] = arrays[n].reshape(1, 1)
    rel_v = arrays["L1_xattn_rel_v"]
    arrays["L1_xattn_rel_k"] = np.ascontiguousarray(arrays["L1_xattn_rel_k"].T)
    arrays["rel_v_wide"] = np.ascontiguousarray(
        np.concatenate([np.repeat(rel_v[:1], S - 1 - 16, 0), rel_v, np.repeat(rel_v[-1:], TEXT - 1 - 16, 0)]))

    own = (np.arange(P)[:, None] // D == np.arange(HC)[None, :])
    arrays["c_mask16"] = (own * 0.25).astype(np.float32)
    arrays["c_mask16_fine"] = (own * 0.0625).astype(np.float32)
    f = np.float32
    inv_freq = (f(1.0) / f(10000.0) ** (np.arange(0, D, 2, dtype=f) / f(D))).astype(f)
    ang = np.outer(np.arange(CTX, dtype=f), inv_freq).astype(f)
    cos, sin = np.cos(ang).T, np.sin(ang).T
    pair, odd = (np.arange(P) % D) // 2, np.arange(P) % 2
    arrays["c_rope"] = np.stack([cos[pair], sin[pair] * np.where(odd, 1.0, -1.0)[:, None]], 1).astype(f)
    idx = np.arange(S, dtype=f)
    scale = (f(1.0) / (f(10000.0) ** (np.arange(0, D, 2, dtype=f) / f(D)) + np.finfo(f).eps)).astype(f)
    ang = (idx[:, None] * scale[None, :]).astype(f)
    pos = np.stack([np.sin(ang), np.cos(ang)], -1).reshape(S, D)
    arrays["c_posT"] = np.ascontiguousarray(pos.T[np.arange(P) % D]).astype(f)
    arrays["c_causal"] = np.where(np.triu(np.ones((S, S), bool), 1), f(-1e37), f(0.0)).astype(f)

    nc = bacc.Bacc("TRN2", target_bir_lowering=False, num_devices=1)
    args = {n: nc.dram_tensor(f"in_{n}", v.shape, mybir.dt.from_np(v.dtype), kind="ExternalInput").ap()
            for n, v in arrays.items()}
    out = nc.dram_tensor("out_x", (B, S, E), F32, kind="ExternalOutput").ap()
    build(nc, args, out)
    result = run_bass_kernel_spmd(nc, [{f"in_{n}": v for n, v in arrays.items()}], core_ids=[0])
    return result.results[0]["out_x"]
```

```python
from contextlib import ExitStack

import concourse.bass as bass
from concourse import mybir

F32 = mybir.dt.float32
BF16 = mybir.dt.bfloat16
ALU = mybir.AluOpType
ACT = mybir.ActivationFunctionType
AX_X = mybir.AxisListType.X

P = 128
B, S, E = 16, 112, 256
H, D = 16, 16
EC = E // P
HC = P // D
CTX = 375
TEXT, IMG = 77, 16
AUD = CTX - TEXT - IMG
HID = 1024
FC = HID // P
LN_EPS = 1e-5
ROUND = 12582912.0
TAKEN = -3.0e38
TOP_K = 32


def wait(engine, semaphore, value):
    if isinstance(value, int) and value <= 0:
        return
    engine.wait_ge(semaphore, value)


def wait_apart(engine, semaphore, value, passed):
    if isinstance(value, int) and value <= 0:
        return
    engine.wait_ge(semaphore, value)
    engine.sem_inc(passed, 1)


def sequences(engine, body):
    body(0, True, False)
    with engine.Fori(1, B - 1) as b:
        body(b, False, False)
    body(B - 1, False, True)


class Buffers:

    def __init__(self, nc, ctx, name, semaphores):
        self.nc, self.ctx, self.name, self.semaphores = nc, ctx, name, semaphores

    def sb(self, name, shape, dtype=F32):
        return self.ctx.enter_context(self.nc.sbuf_tensor(f"{self.name}_{name}", shape, dtype))

    def psum(self, name, dtype=F32):
        return self.ctx.enter_context(self.nc.psum_tensor(f"{self.name}_{name}", [P, 2048 // (4 if dtype == F32 else 2)], dtype))

    def sem(self, name):
        handle = self.nc.alloc_semaphore(name=f"{self.name}_{name}")
        self.semaphores.append(handle)
        return handle


def start_anew(nc, semaphores):
    nc.clear_and_free_semaphores(semaphores)
    semaphores.clear()
    nc.all_engine_barrier()


def row_of(x, b):
    return x[:, bass.ds(b, 1), :].rearrange("p a n -> p (a n)")


class Norm:

    def __init__(self, buf, shared):
        self.z = buf.sb("z", [S, E])
        self.stats = buf.sb("stats", [S, 6])
        self.mean_var = buf.sb("mean_var", [S, 2])
        self.rstd = buf.sb("rstd", [S, 1])
        self.shared = shared
        self.var_ready = buf.sem("var_ready")
        self.rstd_ready = buf.sem("rstd_ready")
        self.eps_added = buf.sem("eps_added")
        self.stats_ready = buf.sem("stats_ready")
        self.mean_ready = buf.sem("mean_ready")
        self.x_ready = buf.sem("x_ready")

    def vector(self, nc, dve, b, z_ready, count, passed):
        self.take_stats(nc, dve, b, z_ready, count, passed)
        self.apply(nc, dve, b)

    def take_stats(self, nc, dve, b, z_ready, count, passed):
        dve.wait_ge(z_ready, count)
        nc.vector.bn_stats(self.stats[:], self.z[:]).then_inc(self.stats_ready, 1)
        wait_apart(dve, self.stats_ready, b + 1, passed)
        nc.vector.bn_aggr(self.mean_var[:], self.stats[:]).then_inc(self.mean_ready, 1)

    def apply(self, nc, dve, b):
        dve.wait_ge(self.rstd_ready, b + 1)
        nc.vector.tensor_scalar(row_of(self.shared["x"], b), self.z[:], self.mean_var[:, 0:1], self.rstd[:, 0:1],
                                ALU.subtract, ALU.mult).then_inc(self.x_ready, 1)

    def gpsimd(self, nc, pool, b, passed):
        wait_apart(pool, self.mean_ready, b + 1, passed)
        nc.gpsimd.tensor_scalar(self.rstd[:], self.mean_var[:, 1:2], LN_EPS, None, ALU.add).then_inc(self.eps_added, 1)
        pool.wait_ge(self.eps_added, b + 1)
        nc.gpsimd.tensor_tensor(self.rstd[:], self.rstd[:], self.shared["minus_half"][:], ALU.pow).then_inc(
            self.rstd_ready, 1)


def self_attention(nc, shared, name, wq, wk, wv, wo, biases=None, pos=None):
    top_k = biases is not None
    G, HG = 4, 4
    PAIR = 2
    CHAIN = 2 * (TOP_K // 8) * (HG // PAIR)
    FOUND_MAX = HG // PAIR
    DV = D + 1
    x, ident = shared["x"], shared["ident"]
    with ExitStack() as ctx:
        buf = Buffers(nc, ctx, name, shared["semaphores"])
        w_q, w_k, w_v, w_o = (buf.sb(n, [P, EC, E]) for n in ("w_q", "w_k", "w_v", "w_o"))
        head_mask = buf.sb("head_mask", [P, HC])
        xs = buf.sb("xs", [S, E])
        xT = buf.sb("xT", [P, EC, S])
        qT = buf.sb("qT", [P, EC, S])
        kT = buf.sb("kT", [P, EC, S])
        q_head = buf.sb("q_head", [P, EC, HC, S])
        v_one = buf.sb("v_one", [S, H, DV])
        s_sb = buf.sb("s_sb", [S, 2, HG, S])
        neg_max = buf.sb("neg_max", [S, 2, HG])
        probs = buf.sb("probs", [S, 2, HG, S])
        probsT = buf.sb("probsT", [S, 2, HG, S])
        rden = buf.sb("rden", [S, H])
        o_sb = buf.sb("o_sb", [S, E])
        oT = buf.sb("oT", [P, EC, S])
        norm = Norm(buf, shared)
        if top_k:
            b_q, b_k = buf.sb("b_q", [P, EC]), buf.sb("b_k", [P, EC])
            b_v, b_o = buf.sb("b_v", [S, E]), buf.sb("b_o", [S, E])
            top8 = buf.sb("top8", [S, 2, HG, TOP_K // 8, 8])
            left = buf.sb("left", [S, 2, HG, S])
            exps = buf.sb("exps", [S, 2, HG, S])
            taken = buf.sb("taken", [S, HG, S])
            x_bias = buf.sb("x_bias", [S, E])
        else:
            posT, causal = buf.sb("posT", [P, S]), buf.sb("causal", [S, S])
        ps_s = [buf.psum(f"ps_s{i}") for i in range(2)]
        ps_t = [buf.psum(f"ps_t{i}") for i in range(2)]
        ps_o = buf.psum("ps_o")
        ps_a, ps_b, ps_c = buf.psum("ps_a"), buf.psum("ps_b"), buf.psum("ps_c")

        loaded, passed = buf.sem("loaded"), buf.sem("passed")
        ones_ready = buf.sem("ones_ready")
        xs_ready, xT_raw, xT_ready = buf.sem("xs_ready"), buf.sem("xT_raw"), buf.sem("xT_ready")
        q_raw, q_ready, k_raw, k_ready = (buf.sem(n) for n in ("q_raw", "q_ready", "k_raw", "k_ready"))
        v_raw, v_ready, q_head_ready = buf.sem("v_raw"), buf.sem("v_ready"), buf.sem("q_head_ready")
        scores_raw, scores_ready = buf.sem("scores_raw"), buf.sem("scores_ready")
        searched = buf.sem("searched")
        neg_ready, exps_done = buf.sem("neg_ready"), buf.sem("exps_done")
        taken_ready, probs_ready = buf.sem("taken_ready"), buf.sem("probs_ready")
        probsT_raw, probsT_ready = buf.sem("probsT_raw"), buf.sem("probsT_ready")
        av_done, rden_ready, o_ready = buf.sem("av_done"), buf.sem("rden_ready"), buf.sem("o_ready")
        oT_raw, oT_ready, y_raw = buf.sem("oT_raw"), buf.sem("oT_ready"), buf.sem("y_raw")
        z_ready, x_bias_ready = buf.sem("z_ready"), buf.sem("x_bias_ready")

        loads = [(w_q, wq), (w_k, wk), (w_v, wv), (w_o, wo)]
        loads = [(to[:], a.rearrange("(c p) n -> p c n", p=P)) for to, a in loads]
        loads.append((head_mask[:], shared["mask16"] if top_k else shared["mask16_fine"]))
        if top_k:
            loads += [(b_q[:], biases[0]),
                      (b_k[:], biases[1]),
                      (b_v[:], biases[2].rearrange("(a n) -> a n", a=1).partition_broadcast(S)),
                      (b_o[:], biases[3].rearrange("(a n) -> a n", a=1).partition_broadcast(S))]
        else:
            loads += [(posT[:], pos[0]), (causal[:], pos[1])]

        all_loaded = 16 * len(loads)

        block = ctx.enter_context(nc.Block())

        @block.sync
        def _(sp):
            for to, a in loads:
                sp.dma_start(to, a).then_inc(loaded, 16)

        @block.tensor
        def _(pe):
            def project_xT(b):
                pe.wait_ge(xs_ready, b + 1)
                wait(pe, q_ready, b)
                for c in range(EC):
                    last = nc.tensor.transpose(ps_b[:, c * S:(c + 1) * S], xs[:, c * P:(c + 1) * P], ident[:S, :S])
                last.then_inc(xT_raw, 1)

            def project_qk(b):
                pe.wait_ge(xT_ready, b + 1)
                for w, out, raw in ((w_q, ps_b, q_raw), (w_k, ps_c, k_raw)):
                    for m in range(EC):
                        for c in range(EC):
                            last = nc.tensor.matmul(out[:, m * S:(m + 1) * S], w[:, c, m * P:(m + 1) * P], xT[:, c, :],
                                                    start=(c == 0), stop=(c == EC - 1))
                    last.then_inc(raw, 1)

            def project_v(b):
                wait(pe, z_ready, b)
                for c in range(EC):
                    last = nc.tensor.matmul(ps_a[:S, 0:E], xT[:, c, :], w_v[:, c, :], start=(c == 0), stop=(c == EC - 1))
                last.then_inc(v_raw, 1)

            def scores(b, g):
                if g == 0:
                    pe.wait_ge(k_ready, b + 1)
                if g % (G // EC) == 0:
                    pe.wait_ge(q_head_ready, b * EC + g // (G // EC) + 1)
                wait(pe, scores_ready, b * G + g - 1)
                for i in range(HG):
                    h = g * HG + i
                    last = nc.tensor.matmul(ps_s[g % 2][:S, i * S:(i + 1) * S], q_head[:, h // HC, h % HC, :],
                                            kT[:, h // HC, :], start=True, stop=True)
                last.then_inc(scores_raw, 1)

            def turn_probs(b, g):
                pe.wait_ge(probs_ready, b * G + g + 1)
                wait(pe, probsT_ready, b * G + g - 1)
                for i in range(HG):
                    last = nc.tensor.transpose(ps_t[g % 2][:S, i * S:(i + 1) * S], probs[:, g % 2, i, :], ident[:S, :S])
                last.then_inc(probsT_raw, 1)

            def weigh_values(b, g):
                pe.wait_ge(probsT_ready, b * G + g + 1)
                if g == 0:
                    pe.wait_ge(v_ready, b + 1)
                    wait(pe, o_ready, b)
                for i in range(HG):
                    h = g * HG + i
                    last = nc.tensor.matmul(ps_o[:S, h * DV:(h + 1) * DV], probsT[:, g % 2, i, :], v_one[:, h, :],
                                            start=True, stop=True)
                last.then_inc(av_done, 1)

            def turn_output(b, last_b=False):
                pe.wait_ge(o_ready, b + 1)
                if not last_b:
                    pe.wait_ge(k_ready, b + 3)
                for c in range(EC):
                    last = nc.tensor.transpose(ps_c[:, c * S:(c + 1) * S], o_sb[:, c * P:(c + 1) * P], ident[:S, :S])
                last.then_inc(oT_raw, 1)

            def project_out(b, last_b=False):
                pe.wait_ge(oT_ready, b + 1)
                if not last_b:
                    pe.wait_ge(v_ready, b + 2)
                for c in range(EC):
                    last = nc.tensor.matmul(ps_a[:S, 0:E], oT[:, c, :], w_o[:, c, :], start=(c == 0), stop=(c == EC - 1))
                last.then_inc(y_raw, 1)

            pe.wait_ge(loaded, all_loaded)
            project_xT(0)
            project_qk(0)

            def body(b, first, last):
                scores(b, 0)
                if not first:
                    turn_probs(b - 1, 2)
                    weigh_values(b - 1, 1)
                project_v(b)
                scores(b, 1)
                if not first:
                    turn_probs(b - 1, 3)
                if not last:
                    project_xT(b + 1)
                if not first:
                    weigh_values(b - 1, 2)
                scores(b, 2)
                if not last:
                    project_qk(b + 1)
                if not first:
                    weigh_values(b - 1, 3)
                turn_probs(b, 0)
                scores(b, 3)
                if not first:
                    turn_output(b - 1, last)
                weigh_values(b, 0)
                if not first:
                    project_out(b - 1)
                turn_probs(b, 1)

            sequences(pe, body)
            turn_probs(B - 1, 2)
            weigh_values(B - 1, 1)
            turn_probs(B - 1, 3)
            weigh_values(B - 1, 2)
            weigh_values(B - 1, 3)
            turn_output(B - 1, True)
            project_out(B - 1, True)

        @block.scalar
        def _(act):
            def take_xT(b):
                act.wait_ge(xT_raw, b + 1)
                wait(act, v_raw, b)
                nc.scalar.copy(xT[:], ps_b[:, 0:EC * S].rearrange("p (c s) -> p c s", c=EC)).then_inc(xT_ready, 1)

            def take_q(b):
                act.wait_ge(q_raw, b + 1)
                wait(act, q_head_ready, b * EC)
                for m in range(EC):
                    last = nc.scalar.activation(qT[:, m, :], ps_b[:, m * S:(m + 1) * S], ACT.Identity,
                                                bias=b_q[:, m:m + 1])
                last.then_inc(q_ready, 1)

            def take_k(b):
                act.wait_ge(k_raw, b + 1)
                wait(act, scores_raw, b * G)
                for m in range(EC):
                    last = nc.scalar.activation(kT[:, m, :], ps_c[:, m * S:(m + 1) * S], ACT.Identity,
                                                bias=b_k[:, m:m + 1])
                last.then_inc(k_ready, 1)

            def take_scores(b, g):
                act.wait_ge(scores_raw, b * G + g + 1)
                wait(act, searched, (b * G + g - 1) * CHAIN)
                nc.scalar.copy(s_sb[:, g % 2], ps_s[g % 2][:S, 0:HG * S].rearrange("p (h s) -> p h s", h=HG)).then_inc(
                    scores_ready, 1)

            def exponentials(b, g):
                out, out_free = (exps, taken_ready) if top_k else (probs, probsT_raw)
                if top_k:
                    act.wait_ge(searched, (b * G + g) * CHAIN + FOUND_MAX)
                    nc.scalar.mul(neg_max[:, g % 2, :], top8[:, g % 2, :, 0, 0], -1.0).then_inc(neg_ready, 1)
                    wait(act, probs_ready, b * G + g - 1)
                else:
                    wait(act, probsT_raw, b * G + g - 1)
                act.wait_ge(neg_ready, b * G + g + 1)
                for i in range(HG):
                    last = nc.scalar.activation(out[:, g % 2, i, :], s_sb[:, g % 2, i, :], ACT.Exp,
                                                bias=neg_max[:, g % 2, i:i + 1])
                last.then_inc(exps_done if top_k else probs_ready, 1)

            def take_probsT(b, g):
                act.wait_ge(probsT_raw, b * G + g + 1)
                wait(act, av_done, b * G + g - 1)
                nc.scalar.copy(probsT[:, g % 2], ps_t[g % 2][:S, 0:HG * S].rearrange("p (h s) -> p h s", h=HG)).then_inc(
                    probsT_ready, 1)

            def take_oT(b):
                act.wait_ge(oT_raw, b + 1)
                nc.scalar.copy(oT[:], ps_c[:, 0:EC * S].rearrange("p (c s) -> p c s", c=EC)).then_inc(oT_ready, 1)

            act.wait_ge(loaded, all_loaded)
            take_xT(0)
            if top_k:
                take_q(0)
                take_k(0)

            def body(b, first, last):
                for g in range(G):
                    if top_k:
                        take_scores(b, g)
                    if top_k and g == 2 and not last:
                        take_q(b + 1)
                    if not top_k and g == 3 and not first:
                        take_oT(b - 1)
                    if g >= 2:
                        take_probsT(b, g - 2)
                    elif not first:
                        take_probsT(b - 1, g + 2)
                    if g == 1 and not last:
                        take_xT(b + 1)
                    if top_k and g == 2:
                        if not last:
                            take_k(b + 1)
                        if not first:
                            take_oT(b - 1)
                    exponentials(b, g)

            sequences(act, body)
            take_probsT(B - 1, 2)
            take_probsT(B - 1, 3)
            take_oT(B - 1)

        @block.vector
        def _(dve):
            def search(b, g):
                wait_apart(dve, scores_ready, b * G + g + 1, passed)
                wait(dve, exps_done, b * G + g - 1)
                wait_apart(dve, taken_ready, b * G + g - 1, passed)
                for step in range(2 * (TOP_K // 8)):
                    r = step // 2
                    source = s_sb if r == 0 else left
                    for pair in range(HG // PAIR):
                        if step:
                            wait_apart(dve, searched, (b * G + g) * CHAIN + (step - 1) * (HG // PAIR) + pair + 1, passed)
                        for i in range(pair * PAIR, (pair + 1) * PAIR):
                            if step % 2 == 0:
                                ins = nc.vector.max(top8[:, g % 2, i, r, :], source[:, g % 2, i, :])
                            else:
                                ins = nc.vector.match_replace(left[:, g % 2, i, :], top8[:, g % 2, i, r, :],
                                                              source[:, g % 2, i, :], TAKEN)
                        ins.then_inc(searched, 1)

            def mask_scores(b, g):
                dve.wait_ge(scores_raw, b * G + g + 1)
                wait(dve, probs_ready, b * G + g - 1)
                nc.vector.tensor_tensor(s_sb[:, g % 2], ps_s[g % 2][:S, 0:HG * S].rearrange("p (h s) -> p h s", h=HG),
                                        causal[:].unsqueeze(1).broadcast_to([S, HG, S]), ALU.add).then_inc(
                    scores_ready, 1)
                dve.wait_ge(scores_ready, b * G + g + 1)
                nc.vector.tensor_reduce(neg_max[:, g % 2, :], s_sb[:, g % 2], AX_X, ALU.max, negate=True).then_inc(
                    neg_ready, 1)

            def take_q(b):
                dve.wait_ge(q_raw, b + 1)
                wait(dve, q_head_ready, b * EC)
                nc.vector.tensor_tensor(qT[:], ps_b[:, 0:EC * S].rearrange("p (c s) -> p c s", c=EC),
                                        posT[:].unsqueeze(1).broadcast_to([P, EC, S]), ALU.add).then_inc(q_ready, 1)

            def take_k(b):
                dve.wait_ge(k_raw, b + 1)
                wait(dve, scores_raw, b * G)
                nc.vector.tensor_tensor(kT[:], ps_c[:, 0:EC * S].rearrange("p (c s) -> p c s", c=EC),
                                        posT[:].unsqueeze(1).broadcast_to([P, EC, S]), ALU.add).then_inc(k_ready, 1)

            def take_v(b):
                dve.wait_ge(v_raw, b + 1)
                wait(dve, av_done, b * G)
                v_ps = ps_a[:S, 0:E].rearrange("p (h d) -> p h d", h=H)
                if top_k:
                    nc.vector.tensor_tensor(v_one[:, :, 0:D], v_ps, b_v[:].rearrange("p (h d) -> p h d", h=H),
                                            ALU.add).then_inc(v_ready, 1)
                else:
                    nc.vector.tensor_copy(v_one[:, :, 0:D], v_ps).then_inc(v_ready, 1)

            def normalise(b):
                o_ps = ps_o[:S, 0:H * DV].rearrange("p (h d) -> p h d", h=H)
                dve.wait_ge(av_done, (b + 1) * G)
                nc.vector.reciprocal(rden[:], o_ps[:, :, D]).then_inc(rden_ready, 1)
                dve.wait_ge(rden_ready, b + 1)
                wait(dve, oT_raw, b)
                nc.vector.tensor_tensor(o_sb[:].rearrange("p (h d) -> p h d", h=H), o_ps[:, :, 0:D],
                                        rden[:].unsqueeze(2).broadcast_to([S, H, D]), ALU.mult).then_inc(o_ready, 1)

            def add_residual(b):
                dve.wait_ge(y_raw, b + 1)
                wait(dve, norm.x_ready, b)
                if top_k:
                    dve.wait_ge(x_bias_ready, b + 1)
                nc.vector.tensor_tensor(norm.z[:], ps_a[:S, 0:E], x_bias[:] if top_k else row_of(x, b), ALU.add).then_inc(
                    z_ready, 1)
                norm.take_stats(nc, dve, b, z_ready, b + 2, passed)

            dve.wait_ge(loaded, all_loaded)
            dve.wait_ge(ones_ready, 1)
            dve.sem_inc(z_ready, 1)
            if top_k:
                def body(b, first, last):
                    search(b, 0)
                    search(b, 1)
                    if not first:
                        normalise(b - 1)
                    take_v(b)
                    search(b, 2)
                    if not first:
                        add_residual(b - 1)
                    search(b, 3)
                    if not first:
                        norm.apply(nc, dve, b - 1)
            else:
                def body(b, first, last):
                    mask_scores(b, 1)
                    mask_scores(b, 2)
                    if not last:
                        take_q(b + 1)
                    if not first:
                        normalise(b - 1)
                    take_v(b)
                    mask_scores(b, 3)
                    if not last:
                        take_k(b + 1)
                    if not first:
                        add_residual(b - 1)
                    if not last:
                        mask_scores(b + 1, 0)
                    if not first:
                        norm.apply(nc, dve, b - 1)

                take_q(0)
                take_k(0)
                mask_scores(0, 0)

            sequences(dve, body)
            normalise(B - 1)
            add_residual(B - 1)
            norm.apply(nc, dve, B - 1)

        @block.gpsimd
        def _(pool):
            def take_x(b):
                wait(pool, xT_raw, b)
                nc.gpsimd.tensor_copy(xs[:], row_of(x, b)).then_inc(xs_ready, 1)

            def spread_q(b):
                pool.wait_ge(q_ready, b + 1)
                for c in range(EC):
                    wait(pool, scores_raw, (b - 1) * G + (c + 1) * (G // EC))
                    nc.gpsimd.tensor_tensor(q_head[:, c], qT[:, c, :].unsqueeze(1).broadcast_to([P, HC, S]),
                                            head_mask[:].unsqueeze(2).broadcast_to([P, HC, S]), ALU.mult).then_inc(
                        q_head_ready, 1)

            def keep_taken(b, g):
                wait(pool, probs_ready, b * G + g)
                wait_apart(pool, searched, (b * G + g + 1) * CHAIN, passed)
                nc.gpsimd.tensor_scalar(taken[:], left[:, g % 2], TAKEN * 0.9, None, ALU.is_le).then_inc(taken_ready, 1)
                pool.wait_ge(taken_ready, b * G + g + 1)
                pool.wait_ge(exps_done, b * G + g + 1)
                wait(pool, probsT_raw, b * G + g - 1)
                nc.gpsimd.tensor_tensor(probs[:, g % 2], taken[:], exps[:, g % 2], ALU.mult).then_inc(probs_ready, 1)

            def add_bias(b):
                wait(pool, z_ready, b + 1)
                nc.gpsimd.tensor_tensor(x_bias[:], row_of(x, b), b_o[:], ALU.add).then_inc(x_bias_ready, 1)

            nc.gpsimd.memset(v_one[:], 1.0).then_inc(ones_ready, 1)
            pool.wait_ge(loaded, all_loaded)
            take_x(0)
            spread_q(0)

            def body(b, first, last):
                if not last:
                    take_x(b + 1)
                if top_k:
                    if not first:
                        add_bias(b - 1)
                    keep_taken(b, 0)
                if not last:
                    spread_q(b + 1)
                if top_k:
                    keep_taken(b, 1)
                    keep_taken(b, 2)
                if not first:
                    norm.gpsimd(nc, pool, b - 1, passed)
                if top_k:
                    keep_taken(b, 3)

            sequences(pool, body)
            if top_k:
                add_bias(B - 1)
            norm.gpsimd(nc, pool, B - 1, passed)


def cross_attention_rope(nc, shared, name, ctxT, wq, wq_swap, wk, wk_swap, wv, wo, rope):
    KC = CTX // 3
    NC = CTX // KC
    T_LAG, AV_LAG = 2, 3
    DV = D + 1
    x, ident = shared["x"], shared["ident"]
    with ExitStack() as ctx:
        buf = Buffers(nc, ctx, name, shared["semaphores"])
        w_q, w_qs, w_k, w_ks, w_v, w_o = (buf.sb(n, [P, EC, E]) for n in ("w_q", "w_qs", "w_k", "w_ks", "w_v", "w_o"))
        cos_sin = buf.sb("cos_sin", [P, 2, CTX])
        head_mask = buf.sb("head_mask", [P, HC])
        context = buf.sb("context", [P, EC, CTX])
        xs = buf.sb("xs", [S, E])
        xT = buf.sb("xT", [P, EC, S])
        q_cos, q_sin, qT = (buf.sb(n, [P, EC, S]) for n in ("q_cos", "q_sin", "qT"))
        k_cos, k_sin, kT = (buf.sb(n, [P, EC, CTX]) for n in ("k_cos", "k_sin", "kT"))
        q_head = buf.sb("q_head", [P, EC, HC, S])
        v_one = buf.sb("v_one", [KC, NC, H, DV])
        neg_max = buf.sb("neg_max", [S, 2])
        probs = buf.sb("probs", [S, 2, CTX])
        probsT = buf.sb("probsT", [KC, 2, NC, S])
        rden = buf.sb("rden", [S, H])
        o_sb = buf.sb("o_sb", [S, E])
        oT = buf.sb("oT", [P, EC, S])
        norm = Norm(buf, shared)
        ps_s = [buf.psum(f"ps_s{i}") for i in range(2)]
        ps_t = [buf.psum(f"ps_t{i}") for i in range(2)]
        ps_o = buf.psum("ps_o")
        ps_a, ps_b, ps_c = buf.psum("ps_a"), buf.psum("ps_b"), buf.psum("ps_c")

        loaded, ones_ready, passed = buf.sem("loaded"), buf.sem("ones_ready"), buf.sem("passed")
        context_loaded = buf.sem("context_loaded")
        xs_ready, xT_raw, xT_ready = buf.sem("xs_ready"), buf.sem("xT_raw"), buf.sem("xT_ready")
        q_raw, q_turned, q_ready, q_head_ready = (buf.sem(n) for n in ("q_raw", "q_turned", "q_ready", "q_head_ready"))
        k_raw = [buf.sem(f"k_raw{m}") for m in range(EC)]
        k_turned = [buf.sem(f"k_turned{m}") for m in range(EC)]
        k_ready = [buf.sem(f"k_ready{m}") for m in range(EC)]
        v_raw, v_ready = buf.sem("v_raw"), buf.sem("v_ready")
        scores_raw, max_ready, probs_ready = buf.sem("scores_raw"), buf.sem("max_ready"), buf.sem("probs_ready")
        probsT_raw, probsT_ready, av_done = buf.sem("probsT_raw"), buf.sem("probsT_ready"), buf.sem("av_done")
        rden_ready, o_ready = buf.sem("rden_ready"), buf.sem("o_ready")
        oT_raw, oT_ready, y_raw, z_ready = (buf.sem(n) for n in ("oT_raw", "oT_ready", "y_raw", "z_ready"))

        loads = [(w_q, wq), (w_qs, wq_swap), (w_k, wk), (w_ks, wk_swap), (w_v, wv), (w_o, wo)]
        loads = [(to[:], a.rearrange("(c p) n -> p c n", p=P)) for to, a in loads]
        loads += [(cos_sin[:], rope), (head_mask[:], shared["mask16"])]
        all_loaded = 16 * len(loads)
        context_of = ctxT.rearrange("(c p) b t -> p c b t", p=P)

        def back(b, h, lag):
            return (b, h - lag) if h >= lag else (b - 1, h - lag + H)

        block = ctx.enter_context(nc.Block())

        @block.sync
        def _(sp):
            for to, a in loads:
                sp.dma_start(to, a).then_inc(loaded, 16)

        @block.tensor
        def _(pe):
            def project_xT(b):
                pe.wait_ge(xs_ready, b + 1)
                for c in range(EC):
                    last = nc.tensor.transpose(ps_a[:, c * S:(c + 1) * S], xs[:, c * P:(c + 1) * P], ident[:S, :S])
                last.then_inc(xT_raw, 1)

            def project_q(b, w, out):
                pe.wait_ge(xT_ready, b + 1)
                for m in range(EC):
                    for c in range(EC):
                        last = nc.tensor.matmul(out[:, m * S:(m + 1) * S], w[:, c, m * P:(m + 1) * P], xT[:, c, :],
                                                start=(c == 0), stop=(c == EC - 1))
                last.then_inc(q_raw, 1)

            def project_k(b, m, w, out):
                pe.wait_ge(context_loaded, 16 * (b + 1))
                for c in range(EC):
                    last = nc.tensor.matmul(out[:, 0:CTX], w[:, c, m * P:(m + 1) * P], context[:, c, :],
                                            start=(c == 0), stop=(c == EC - 1))
                last.then_inc(k_raw[m], 1)

            def project_v(b):
                for t in range(NC):
                    out = (ps_a[:KC, 0:E], ps_a[:KC, E:2 * E], ps_b[:KC, 0:E])[t]
                    for c in range(EC):
                        last = nc.tensor.matmul(out, context[:, c, t * KC:(t + 1) * KC], w_v[:, c, :],
                                                start=(c == 0), stop=(c == EC - 1))
                last.then_inc(v_raw, 1)

            def scores(b, h):
                if h == 0:
                    pe.wait_ge(q_head_ready, EC * b + 1)
                    pe.wait_ge(k_ready[0], b + 1)
                if h == HC:
                    pe.wait_ge(q_head_ready, EC * b + 2)
                    pe.wait_ge(k_ready[1], b + 1)
                wait(pe, probs_ready, b * H + h - 1)
                nc.tensor.matmul(ps_s[h % 2][:S, 0:CTX], q_head[:, h // HC, h % HC, :], kT[:, h // HC, :],
                                 start=True, stop=True).then_inc(scores_raw, 1)

            def turn_probs(b, h):
                pe.wait_ge(probs_ready, b * H + h + 1)
                wait(pe, probsT_ready, b * H + h - 1)
                for t in range(NC):
                    last = nc.tensor.transpose(ps_t[h % 2][:KC, t * S:(t + 1) * S],
                                               probs[:, h % 2, t * KC:(t + 1) * KC], ident[:S, :S])
                last.then_inc(probsT_raw, 1)

            def weigh_values(b, h):
                pe.wait_ge(probsT_ready, b * H + h + 1)
                if h == 0:
                    pe.wait_ge(v_ready, b + 1)
                    wait(pe, o_ready, b)
                for t in range(NC):
                    last = nc.tensor.matmul(ps_o[:S, h * DV:(h + 1) * DV], probsT[:, h % 2, t, :], v_one[:, t, h, :],
                                            start=(t == 0), stop=(t == NC - 1))
                last.then_inc(av_done, 1)

            def turn_output(b):
                pe.wait_ge(o_ready, b + 1)
                for c in range(EC):
                    last = nc.tensor.transpose(ps_b[:, c * S:(c + 1) * S], o_sb[:, c * P:(c + 1) * P], ident[:S, :S])
                last.then_inc(oT_raw, 1)

            def project_out(b):
                pe.wait_ge(oT_ready, b + 1)
                for c in range(EC):
                    last = nc.tensor.matmul(ps_c[:S, 0:E], oT[:, c, :], w_o[:, c, :], start=(c == 0), stop=(c == EC - 1))
                last.then_inc(y_raw, 1)

            pe.wait_ge(loaded, all_loaded)
            project_xT(0)
            project_q(0, w_q, ps_b)
            project_q(0, w_qs, ps_c)
            project_k(0, 0, w_k, ps_a)
            pe.wait_ge(q_turned, 1)
            project_k(0, 0, w_ks, ps_b)

            def body(b, first, last):
                for h in range(H):
                    scores(b, h)
                    if h >= T_LAG or not first:
                        turn_probs(*back(b, h, T_LAG))
                    if h >= AV_LAG or not first:
                        weigh_values(*back(b, h, AV_LAG))
                    if h == AV_LAG - 1:
                        pe.wait_ge(k_turned[0], b + 1)
                        project_v(b)
                        pe.wait_ge(q_turned, b + 1)
                        project_k(b, 1, w_k, ps_c)
                        pe.wait_ge(v_ready, b + 1)
                        project_k(b, 1, w_ks, ps_a)
                    if h == 5 and not first:
                        turn_output(b - 1)
                    if h == 6 and not first:
                        pe.wait_ge(k_turned[1], b + 1)
                        project_out(b - 1)
                    if not last:
                        if h == 8:
                            pe.wait_ge(k_turned[1], b + 1)
                            project_xT(b + 1)
                        if h == 9:
                            wait(pe, oT_ready, b)
                            project_q(b + 1, w_q, ps_b)
                        if h == 10:
                            wait(pe, z_ready, b)
                            project_q(b + 1, w_qs, ps_c)
                        if h == 11:
                            project_k(b + 1, 0, w_k, ps_a)
                        if h == 12:
                            pe.wait_ge(q_turned, b + 2)
                            project_k(b + 1, 0, w_ks, ps_b)

            sequences(pe, body)
            turn_probs(B - 1, H - 2)
            weigh_values(B - 1, H - 3)
            turn_probs(B - 1, H - 1)
            weigh_values(B - 1, H - 2)
            weigh_values(B - 1, H - 1)
            turn_output(B - 1)
            project_out(B - 1)

        @block.scalar
        def _(act):
            def take_xT(b):
                act.wait_ge(xT_raw, b + 1)
                nc.scalar.copy(xT[:], ps_a[:, 0:EC * S].rearrange("p (c s) -> p c s", c=EC)).then_inc(xT_ready, 1)

            def take_v(b):
                act.wait_ge(v_raw, b + 1)
                nc.scalar.copy(v_one[:, 0:2, :, 0:D], ps_a[:KC, :].rearrange("p (t h d) -> p t h d", t=2, h=H))
                nc.scalar.copy(v_one[:, 2, :, 0:D], ps_b[:KC, 0:E].rearrange("p (h d) -> p h d", h=H)).then_inc(v_ready, 1)

            def exponentials(b, h):
                act.wait_ge(max_ready, b * H + h + 1)
                wait(act, probsT_raw, b * H + h - 1)
                nc.scalar.activation(probs[:, h % 2, :], ps_s[h % 2][:S, 0:CTX], ACT.Exp,
                                     bias=neg_max[:, h % 2:h % 2 + 1]).then_inc(probs_ready, 1)

            def take_oT(b):
                act.wait_ge(oT_raw, b + 1)
                nc.scalar.copy(oT[:], ps_b[:, 0:EC * S].rearrange("p (c s) -> p c s", c=EC)).then_inc(oT_ready, 1)

            act.wait_ge(ones_ready, 1)
            take_xT(0)

            def load_context(b):
                act.dma_start(context[:], context_of[:, :, bass.ds(b, 1), :].rearrange("p c b t -> p c (b t)")).then_inc(
                    context_loaded, 16)

            load_context(0)

            def body(b, first, last):
                for h in range(H):
                    exponentials(b, h)
                    if h == AV_LAG - 1:
                        take_v(b)
                    if h == 4 and not last:
                        act.wait_ge(k_raw[1], 2 * (b + 1))
                        load_context(b + 1)
                    if h == 5 and not first:
                        take_oT(b - 1)
                    if h == 8 and not last:
                        take_xT(b + 1)

            sequences(act, body)
            take_oT(B - 1)

        @block.vector
        def _(dve):
            def row_max(b, h):
                dve.wait_ge(scores_raw, b * H + h + 1)
                wait(dve, probs_ready, b * H + h - 1)
                nc.vector.tensor_reduce(neg_max[:, h % 2:h % 2 + 1], ps_s[h % 2][:S, 0:CTX], AX_X, ALU.max,
                                        negate=True).then_inc(max_ready, 1)

            def take_probsT(b, h):
                dve.wait_ge(probsT_raw, b * H + h + 1)
                wait(dve, av_done, b * H + h - 1)
                nc.vector.tensor_copy(probsT[:, h % 2], ps_t[h % 2][:KC, 0:NC * S].rearrange(
                    "p (t s) -> p t s", t=NC)).then_inc(probsT_ready, 1)

            def turn_q(b):
                dve.wait_ge(q_raw, 2 * (b + 1))
                wait(dve, q_ready, b)
                for which, ps, out in ((0, ps_b, q_cos), (1, ps_c, q_sin)):
                    last = nc.vector.tensor_tensor(out[:], ps[:, 0:EC * S].rearrange("p (c s) -> p c s", c=EC),
                                                   cos_sin[:, which, 0:S].unsqueeze(1).broadcast_to([P, EC, S]), ALU.mult)
                last.then_inc(q_turned, 1)

            def turn_k(b, m, ps_plain, ps_swapped):
                dve.wait_ge(k_raw[m], 2 * (b + 1))
                wait(dve, k_ready[m], b)
                nc.vector.tensor_tensor(k_cos[:, m], ps_plain[:, 0:CTX], cos_sin[:, 0, :], ALU.mult)
                nc.vector.tensor_tensor(k_sin[:, m], ps_swapped[:, 0:CTX], cos_sin[:, 1, :], ALU.mult).then_inc(
                    k_turned[m], 1)

            def normalise(b):
                o_ps = ps_o[:S, 0:H * DV].rearrange("p (h d) -> p h d", h=H)
                dve.wait_ge(av_done, (b + 1) * H)
                nc.vector.reciprocal(rden[:], o_ps[:, :, D]).then_inc(rden_ready, 1)
                dve.wait_ge(rden_ready, b + 1)
                wait(dve, oT_raw, b)
                nc.vector.tensor_tensor(o_sb[:].rearrange("p (h d) -> p h d", h=H), o_ps[:, :, 0:D],
                                        rden[:].unsqueeze(2).broadcast_to([S, H, D]), ALU.mult).then_inc(o_ready, 1)

            def add_residual(b):
                dve.wait_ge(y_raw, b + 1)
                wait(dve, norm.x_ready, b)
                nc.vector.tensor_tensor(norm.z[:], ps_c[:S, 0:E], row_of(x, b), ALU.add).then_inc(z_ready, 1)

            dve.wait_ge(loaded, all_loaded)
            turn_q(0)
            turn_k(0, 0, ps_a, ps_b)

            def body(b, first, last):
                for h in range(H):
                    row_max(b, h)
                    if h >= T_LAG or not first:
                        take_probsT(*back(b, h, T_LAG))
                    if h == AV_LAG - 1:
                        if not first:
                            normalise(b - 1)
                    if h == AV_LAG:
                        turn_k(b, 1, ps_c, ps_a)
                    if h == 7 and not first:
                        add_residual(b - 1)
                        norm.take_stats(nc, dve, b - 1, z_ready, b, passed)
                    if h == 10 and not first:
                        norm.apply(nc, dve, b - 1)
                    if h == 11 and not last:
                        turn_q(b + 1)
                    if h == 13 and not last:
                        turn_k(b + 1, 0, ps_a, ps_b)

            sequences(dve, body)
            take_probsT(B - 1, H - 2)
            take_probsT(B - 1, H - 1)
            normalise(B - 1)
            add_residual(B - 1)
            norm.vector(nc, dve, B - 1, z_ready, B, passed)

        @block.gpsimd
        def _(pool):
            def take_x(b):
                wait(pool, xT_raw, b)
                nc.gpsimd.tensor_copy(xs[:], row_of(x, b)).then_inc(xs_ready, 1)

            def add_q(b):
                pool.wait_ge(q_turned, b + 1)
                wait(pool, q_head_ready, EC * b)
                nc.gpsimd.tensor_tensor(qT[:], q_cos[:], q_sin[:], ALU.add).then_inc(q_ready, 1)

            def spread_q(b, c):
                pool.wait_ge(q_ready, b + 1)
                wait(pool, scores_raw, (b - 1) * H + (c + 1) * HC)
                nc.gpsimd.tensor_tensor(q_head[:, c], qT[:, c, :].unsqueeze(1).broadcast_to([P, HC, S]),
                                        head_mask[:].unsqueeze(2).broadcast_to([P, HC, S]), ALU.mult).then_inc(
                    q_head_ready, 1)

            def add_k(b, m):
                pool.wait_ge(k_turned[m], b + 1)
                wait(pool, scores_raw, (b - 1) * H + (m + 1) * HC)
                nc.gpsimd.tensor_tensor(kT[:, m], k_cos[:, m], k_sin[:, m], ALU.add).then_inc(k_ready[m], 1)

            nc.gpsimd.memset(v_one[:], 1.0).then_inc(ones_ready, 1)
            pool.wait_ge(loaded, all_loaded)
            take_x(0)
            add_q(0)
            spread_q(0, 0)
            add_k(0, 0)

            def body(b, first, last):
                spread_q(b, 1)
                add_k(b, 1)
                if not first:
                    norm.gpsimd(nc, pool, b - 1, passed)
                if not last:
                    take_x(b + 1)
                    add_q(b + 1)
                    spread_q(b + 1, 0)
                    add_k(b + 1, 0)

            sequences(pool, body)
            norm.gpsimd(nc, pool, B - 1, passed)


def ffn_quantised(nc, shared, name, w1T, conv_w, conv_b, w2T):
    x, ident = shared["x"], shared["ident"]
    HALF = FC // 2
    with ExitStack() as ctx:
        buf = Buffers(nc, ctx, name, shared["semaphores"])
        raw = [buf.sb(f"raw{i}", [P, EC * HID]) for i in range(2)]
        w1 = buf.sb("w1", [P, EC, HID], BF16)
        w2 = buf.sb("w2", [P, FC, E], BF16)
        w_abs = buf.sb("w_abs", [P, EC * HID])
        taps, conv_bias = buf.sb("taps", [P, FC, 3]), buf.sb("conv_bias", [P, FC])
        ones, ident_bf = buf.sb("ones", [P, P]), buf.sb("ident_bf", [P, P], BF16)
        abs_sum, mean_abs, w_scale = (buf.sb(n, [P, 2]) for n in ("abs_sum", "mean_abs", "w_scale"))
        peak, peak_clip, inverse, scale, unscale = (buf.sb(n, [S, 2]) for n in (
            "peak", "peak_clip", "inverse", "scale", "unscale"))
        x_round, xq = buf.sb("x_round", [S, E]), buf.sb("xq", [S, E], BF16)
        xqT = buf.sb("xqT", [P, EC, S], BF16)
        unscale_diag, unscale_row = buf.sb("unscale_diag", [S, S]), buf.sb("unscale_row", [P, S])
        h = buf.sb("h", [P, FC, S + 2])
        conv, act_out = buf.sb("conv", [P, FC, S]), buf.sb("act_out", [P, FC, S])
        h_round, hq = buf.sb("h_round", [S, HID]), buf.sb("hq", [S, HID], BF16)
        hqT = buf.sb("hqT", [P, FC, S], BF16)
        norm = Norm(buf, shared)
        ps_xT, ps_row = buf.psum("ps_xT", BF16), buf.psum("ps_row")
        ps_h = [buf.psum(f"ps_h{i}") for i in range(2)]
        ps_u = ctx.enter_context(nc.psum_tensor(f"{name}_ps_u", [P, HID], F32))
        ps_hT, ps_y = buf.psum("ps_hT", BF16), buf.psum("ps_y")

        loaded, passed, passed_pool, zeroed = (buf.sem(n) for n in ("loaded", "passed", "passed_pool", "zeroed"))
        scale_ready = [buf.sem(f"scale_ready{i}") for i in range(2)]
        abs_done, w_sum_done, w_prep = buf.sem("abs_done"), buf.sem("w_sum_done"), buf.sem("w_prep")
        prep_chain, peak_chain = buf.sem("prep_chain"), [buf.sem(f"peak_chain{i}") for i in range(2)]
        unscale_ready, diag_ready = buf.sem("unscale_ready"), buf.sem("diag_ready")
        x_rounded, xq_ready, xqT_raw, xqT_ready = (buf.sem(n) for n in ("x_rounded", "xq_ready", "xqT_raw", "xqT_ready"))
        row_raw, row_ready, h_raw, h_ready = (buf.sem(n) for n in ("row_raw", "row_ready", "h_raw", "h_ready"))
        middle_done, tap0_done, conv_done, silu_done = (buf.sem(n) for n in (
            "middle_done", "tap0_done", "conv_done", "silu_done"))
        turned, h_rounded, hq_ready, hqT_raw, hqT_ready = (buf.sem(n) for n in (
            "turned", "h_rounded", "hq_ready", "hqT_raw", "hqT_ready"))
        y_raw, z_ready = buf.sem("y_raw"), buf.sem("z_ready")

        loads = [(raw[0][:].rearrange("p (c n) -> p c n", c=EC), w1T.rearrange("(c p) n -> p c n", p=P)),
                 (raw[1][:].rearrange("p (c n) -> p c n", c=FC), w2T.rearrange("(c p) n -> p c n", p=P)),
                 (taps[:], conv_w.rearrange("(c p) k -> p c k", p=P)), (conv_bias[:], conv_b)]
        all_loaded = 16 * len(loads)
        block = ctx.enter_context(nc.Block())

        @block.sync
        def _(sp):
            for to, a in loads:
                sp.dma_start(to, a).then_inc(loaded, 16)

        @block.tensor
        def _(pe):
            def turn_x(b):
                pe.wait_ge(xq_ready, b + 1)
                wait(pe, xqT_ready, b)
                for c in range(EC):
                    last = nc.tensor.transpose(ps_xT[:, c * S:(c + 1) * S], xq[:, c * P:(c + 1) * P], ident_bf[:S, :S])
                last.then_inc(xqT_raw, 1)
                pe.wait_ge(diag_ready, b + 1)
                wait(pe, row_ready, b)
                nc.tensor.matmul(ps_row[:, 0:S], ones[:S, :], unscale_diag[:], start=True, stop=True).then_inc(row_raw, 1)

            def up(b):
                pe.wait_ge(xqT_ready, b + 1)
                wait(pe, h_ready, 2 * b)
                for m in range(FC):
                    for c in range(EC):
                        last = nc.tensor.matmul(ps_h[m // HALF][:, m % HALF * S:(m % HALF + 1) * S],
                                                w1[:, c, m * P:(m + 1) * P], xqT[:, c, :],
                                                start=(c == 0), stop=(c == EC - 1))
                    if m % HALF == HALF - 1:
                        last.then_inc(h_raw, 1)

            def turn_hidden(b):
                wait(pe, h_rounded, b)
                for m in range(FC):
                    if m % HALF == 0:
                        pe.wait_ge(silu_done, 2 * b + m // HALF + 1)
                    last = nc.tensor.transpose(ps_u[:S, m * P:(m + 1) * P], act_out[:, m, :], ident[:])
                last.then_inc(turned, 1)

            def turn_quantised(b):
                pe.wait_ge(hq_ready, b + 1)
                wait(pe, hqT_ready, b)
                for m in range(FC):
                    last = nc.tensor.transpose(ps_hT[:, m * S:(m + 1) * S], hq[:, m * P:(m + 1) * P], ident_bf[:S, :S])
                last.then_inc(hqT_raw, 1)

            def down(b):
                pe.wait_ge(hqT_ready, b + 1)
                wait(pe, z_ready, b)
                for m in range(FC):
                    last = nc.tensor.matmul(ps_y[:S, 0:E], hqT[:, m, :], w2[:, m, :], start=(m == 0), stop=(m == FC - 1))
                last.then_inc(y_raw, 1)

            pe.wait_ge(zeroed, 4)
            pe.wait_ge(abs_done, 2)
            nc.tensor.matmul(ps_row[:, 0:2], ones[:], abs_sum[:], start=True, stop=True).then_inc(w_sum_done, 1)
            pe.wait_ge(w_prep, 2)
            turn_x(0)
            up(0)

            def body(b, first, last):
                turn_hidden(b)
                if not last:
                    turn_x(b + 1)
                    up(b + 1)
                turn_quantised(b)
                down(b)

            sequences(pe, body)

        @block.scalar
        def _(act):
            def take_xT(b):
                act.wait_ge(xqT_raw, b + 1)
                wait(act, h_raw, 2 * b)
                nc.scalar.copy(xqT[:], ps_xT[:, 0:EC * S].rearrange("p (c s) -> p c s", c=EC)).then_inc(xqT_ready, 1)
                act.wait_ge(row_raw, b + 1)
                wait(act, h_ready, 2 * b)
                nc.scalar.copy(unscale_row[:], ps_row[:, 0:S]).then_inc(row_ready, 1)

            def middle_tap(b):
                act.wait_ge(h_ready, 2 * (b + 1))
                wait(act, silu_done, 2 * b)
                for m in range(FC):
                    last = nc.scalar.activation(conv[:, m, :], h[:, m, 1:S + 1], ACT.Identity,
                                                bias=conv_bias[:, m:m + 1], scale=taps[:, m, 1:2])
                last.then_inc(middle_done, 1)

            def silu(b):
                act.wait_ge(conv_done, b + 1)
                wait(act, turned, b)
                for i in range(2):
                    nc.scalar.activation(act_out[:, i * HALF:(i + 1) * HALF, :], conv[:, i * HALF:(i + 1) * HALF, :],
                                         ACT.Silu).then_inc(silu_done, 1)

            def take_hqT(b):
                act.wait_ge(hqT_raw, b + 1)
                wait(act, y_raw, b)
                nc.scalar.copy(hqT[:], ps_hT[:, 0:FC * S].rearrange("p (c s) -> p c s", c=FC)).then_inc(hqT_ready, 1)

            act.wait_ge(loaded, all_loaded)
            for i in range(2):
                wait(act, abs_done, i)
                nc.scalar.activation(w_abs[:], raw[i][:], ACT.Abs, accum_out=abs_sum[:, i:i + 1]).then_inc(abs_done, 1)
            take_xT(0)
            middle_tap(0)
            silu(0)

            def body(b, first, last):
                if not last:
                    take_xT(b + 1)
                take_hqT(b)
                if not last:
                    middle_tap(b + 1)
                    silu(b + 1)

            sequences(act, body)

        @block.vector
        def _(dve):
            def scales(b, i):
                n = (2, 3)[i] * b
                wait_apart(dve, peak_chain[i], n + 1, passed)
                nc.vector.tensor_scalar(peak_clip[:, i:i + 1], peak[:, i:i + 1], 1e-5, None, ALU.max).then_inc(
                    peak_chain[i], 1)
                wait_apart(dve, peak_chain[i], n + 2, passed)
                nc.vector.reciprocal(inverse[:, i:i + 1], peak_clip[:, i:i + 1])
                nc.vector.tensor_scalar(unscale[:, i:i + 1], peak_clip[:, i:i + 1], 1.0 / 127.0, mean_abs[:S, i:i + 1],
                                        ALU.mult, ALU.mult).then_inc(unscale_ready if i == 0 else peak_chain[i], 1)
                if i == 0:
                    wait_apart(dve, unscale_ready, b + 1, passed)
                else:
                    wait_apart(dve, peak_chain[i], n + 3, passed)
                nc.vector.tensor_scalar(scale[:, i:i + 1], inverse[:, i:i + 1], 127.0, None, ALU.mult).then_inc(
                    scale_ready[i], 1)
                dve.wait_ge(scale_ready[i], b + 1)

            def quantise_x(b):
                wait(dve, diag_ready, b)
                nc.vector.tensor_reduce(peak[:, 0:1], row_of(x, b), AX_X, ALU.max, apply_absolute_value=True).then_inc(
                    peak_chain[0], 1)
                scales(b, 0)
                nc.vector.tensor_scalar(x_round[:], row_of(x, b), scale[:, 0:1], ROUND, ALU.mult, ALU.add).then_inc(
                    x_rounded, 1)
                dve.wait_ge(x_rounded, b + 1)
                wait(dve, xqT_raw, b)
                nc.vector.tensor_scalar(xq[:], x_round[:], ROUND, 127.0, ALU.subtract, ALU.min).then_inc(xq_ready, 1)

            def convolve(b):
                dve.wait_ge(row_ready, b + 1)
                for i in range(2):
                    dve.wait_ge(h_raw, 2 * b + i + 1)
                    nc.vector.tensor_tensor(h[:, i * HALF:(i + 1) * HALF, 1:S + 1],
                                            ps_h[i][:, 0:HALF * S].rearrange("p (c s) -> p c s", c=HALF),
                                            unscale_row[:].unsqueeze(1).broadcast_to([P, HALF, S]), ALU.mult).then_inc(
                        h_ready, 1)
                dve.wait_ge(middle_done, b + 1)
                for k, done in ((0, tap0_done), (2, conv_done)):
                    if k:
                        dve.wait_ge(tap0_done, b + 1)
                    for m in range(FC):
                        last = nc.vector.scalar_tensor_tensor(conv[:, m, :], h[:, m, k:k + S], taps[:, m, k:k + 1],
                                                              conv[:, m, :], ALU.mult, ALU.add)
                    last.then_inc(done, 1)

            def quantise_hidden(b):
                dve.wait_ge(turned, b + 1)
                nc.vector.tensor_reduce(peak[:, 1:2], ps_u[:S, :], AX_X, ALU.max, apply_absolute_value=True).then_inc(
                    peak_chain[1], 1)
                scales(b, 1)
                nc.vector.tensor_scalar(h_round[:], ps_u[:S, :], scale[:, 1:2], ROUND, ALU.mult, ALU.add).then_inc(
                    h_rounded, 1)
                dve.wait_ge(h_rounded, b + 1)
                wait(dve, hqT_raw, b)
                nc.vector.tensor_scalar(hq[:], h_round[:], ROUND, 127.0, ALU.subtract, ALU.min).then_inc(hq_ready, 1)

            def add_residual(b):
                dve.wait_ge(y_raw, b + 1)
                nc.vector.scalar_tensor_tensor(norm.z[:], ps_y[:S, 0:E], unscale[:, 1:2], row_of(x, b), ALU.mult,
                                               ALU.add).then_inc(z_ready, 1)

            dve.wait_ge(loaded, all_loaded)
            dve.wait_ge(w_sum_done, 1)
            dve.wait_ge(zeroed, 4)
            nc.vector.tensor_scalar(mean_abs[:], ps_row[:, 0:2], 1.0 / (E * HID), 1e-5, ALU.mult, ALU.max).then_inc(
                prep_chain, 1)
            dve.wait_ge(prep_chain, 1)
            nc.vector.reciprocal(w_scale[:], mean_abs[:]).then_inc(prep_chain, 1)
            dve.wait_ge(prep_chain, 2)
            for i, w in enumerate((w1, w2)):
                nc.vector.tensor_scalar(raw[i][:], raw[i][:], w_scale[:, i:i + 1], ROUND, ALU.mult, ALU.add).then_inc(
                    prep_chain, 1)
                dve.wait_ge(prep_chain, 3 + 2 * i)
                nc.vector.tensor_scalar(raw[i][:], raw[i][:], ROUND, 1.0, ALU.subtract, ALU.min).then_inc(prep_chain, 1)
                dve.wait_ge(prep_chain, 4 + 2 * i)
                nc.vector.tensor_scalar(w[:].rearrange("p c n -> p (c n)"), raw[i][:], -1.0, None, ALU.max).then_inc(
                    w_prep, 1)
            quantise_x(0)
            convolve(0)

            def body(b, first, last):
                if not last:
                    quantise_x(b + 1)
                quantise_hidden(b)
                if not last:
                    convolve(b + 1)
                add_residual(b)
                norm.vector(nc, dve, b, z_ready, b + 1, passed)

            sequences(dve, body)

        @block.gpsimd
        def _(pool):
            def scale_diagonal(b):
                wait(pool, row_raw, b)
                wait_apart(pool, unscale_ready, b + 1, passed_pool)
                nc.gpsimd.tensor_scalar(unscale_diag[:], ident[:S, :S], unscale[:, 0:1], None, ALU.mult).then_inc(
                    diag_ready, 1)

            nc.gpsimd.memset(ones[:], 1.0).then_inc(zeroed, 1)
            nc.gpsimd.tensor_copy(ident_bf[:], ident[:]).then_inc(zeroed, 1)
            for at in (0, S + 1):
                nc.gpsimd.memset(h[:, :, at:at + 1], 0.0).then_inc(zeroed, 1)
            scale_diagonal(0)

            def body(b, first, last):
                if not last:
                    scale_diagonal(b + 1)
                norm.gpsimd(nc, pool, b, passed_pool)

            sequences(pool, body)


def cross_attention_relative(nc, shared, name, a):
    K4 = 4
    NG = B // K4
    DH = 64
    NP = H // 2
    HH = H // 2
    REST = AUD - 2 * P
    IMG_ROW = P // 2
    IMG_AT = TEXT + 2 * P + IMG_ROW
    PW = TEXT + 3 * P
    WIDE = S - 1 + TEXT
    T_LAG, AV_LAG = 3, 4
    RING = 4
    QI = 512 // (K4 * H)
    VI = 8
    NV = S // VI
    VSLOTS = 8
    x, ident = shared["x"], shared["ident"]
    with ExitStack() as ctx:
        buf = Buffers(nc, ctx, name, shared["semaphores"])
        w_q = buf.sb("w_q", [P, EC, H * DH])
        w_k = [buf.sb(f"w_k{n}", [P, EC, H * DH]) for n in ("", "_image", "_audio")]
        w_v = [buf.sb(f"w_v{n}", [P, EC, H * DH]) for n in ("", "_image", "_audio")]
        w_o = buf.sb("w_o", [P, NP, E])
        b_o = buf.sb("b_o", [S, E])
        gain = buf.sb("gain", [S, 3])
        rel_k = buf.sb("rel_k", [P, WIDE])
        context_image = buf.sb("context_image", [P, EC, K4, IMG])
        k_image = buf.sb("k_image", [P, NP, K4 * IMG])
        rel_v = buf.sb("rel_v", [TEXT, 2, VI, DH])
        context = buf.sb("context", [P, 2, EC, CTX])
        xs = buf.sb("xs", [S, E])
        xT = buf.sb("xT", [P, EC, S])
        q_head = buf.sb("q_head", [P, K4, H, S])
        turned = buf.sb("turned", [TEXT, K4, H, S])
        outT = buf.sb("outT", [P, K4, NP, S])
        kT = buf.sb("kT", [P, NP, CTX])
        v = buf.sb("v", [P, 4, H * DH])
        neg_max, total, inverse = (buf.sb(n, [S, RING, 3]) for n in ("neg_max", "total", "inverse"))
        probs = buf.sb("probs", [S, RING, PW])
        audT = buf.sb("audT", [P, 2, 3, S])
        norm = Norm(buf, shared)
        x_bias = buf.sb("x_bias", [S, E])
        ps_s = [buf.psum(f"ps_s{i}") for i in range(2)]
        ps_t = [buf.psum(f"ps_t{i}") for i in range(2)]
        ps_o = [buf.psum(f"ps_o{i}") for i in range(2)]
        ps_p = [buf.psum(f"ps_p{i}") for i in range(2)]

        loaded, passed, passed_pool, passed_sp = (buf.sem(n) for n in ("loaded", "passed", "passed_pool", "passed_sp"))
        zeroed, gain_ready, rel_k_ready, tanh_done = (buf.sem(n) for n in ("zeroed", "gain_ready", "rel_k_ready", "tanh_done"))
        image_loaded, k_image_placed = buf.sem("image_loaded"), buf.sem("k_image_placed")
        context_loaded = [buf.sem(f"context_loaded{i}") for i in range(2)]
        rel_v_loaded = [buf.sem(f"rel_v_loaded{i}") for i in range(VSLOTS)]
        raw = [buf.sem(f"raw{i}") for i in range(2)]
        taken = [buf.sem(f"taken{i}") for i in range(2)]
        xs_ready = buf.sem("xs_ready")
        rel_raw, rel_taken = [buf.sem(f"rel_raw{i}") for i in range(2)], [buf.sem(f"rel_taken{i}") for i in range(2)]
        scores_raw, max_ready, exps_done, inverse_ready = (buf.sem(n) for n in (
            "scores_raw", "max_ready", "exps_done", "inverse_ready"))
        probs_ready, probsT_raw, probsT_ready, av_done = (buf.sem(n) for n in (
            "probs_ready", "probsT_raw", "probsT_ready", "av_done"))
        out_taken = [buf.sem(f"out_taken{i}") for i in range(2)]
        rel_v_raw, rel_v_added = buf.sem("rel_v_raw"), buf.sem("rel_v_added")
        y_raw, z_ready, x_bias_ready = buf.sem("y_raw"), buf.sem("z_ready"), buf.sem("x_bias_ready")

        def use_x(k):
            return 3 * k

        def use_q(k, j):
            return 3 * k + 1 + j

        def use_image(j):
            return 3 * K4 + j

        def use_k(k, m):
            return 3 * K4 + 4 + 16 * k + m

        def use_v(k, j):
            return use_k(k, 8 + j)

        USES = use_k(K4, 0) // 2

        def bank_count(g, u):
            return u % 2, USES * g + u // 2

        def head_count(g, k, h):
            return (g * K4 + k) * H + h + 1

        columns = ((0, TEXT), (TEXT, TEXT + AUD), (TEXT + AUD, CTX))

        def places(k):
            return (columns[0], columns[1], (IMG_AT + k * IMG, IMG_AT + (k + 1) * IMG))

        def value_rows(t):
            return ((0, TEXT), (TEXT + IMG, P), (TEXT + IMG + P, P), (TEXT + IMG + 2 * P, REST))[t]

        W = "L1_xattn_"
        loads = [(w_q, a[W + "Wq"])] + [(w_k[i], a[W + n]) for i, n in enumerate(("Wk", "Wk_ip", "Wk_ap"))]
        loads += [(w_v[i], a[W + n]) for i, n in enumerate(("Wv", "Wv_ip", "Wv_ap"))] + [(w_o, a[W + "Wo"])]
        loads = [(to[:], w.rearrange("(c p) n -> p c n", p=P)) for to, w in loads]
        loads += [(b_o[:], a[W + "bo"].rearrange("(a n) -> a n", a=1).partition_broadcast(S)),
                  (gain[:, 1:2], a[W + "beta"].partition_broadcast(S)),
                  (gain[:, 2:3], a[W + "alpha"].partition_broadcast(S)),
                  (rel_k[0:DH, S - 17:S + 16], a[W + "rel_k"]), (rel_k[DH:P, S - 17:S + 16], a[W + "rel_k"])]
        all_loaded = 16 * len(loads)
        context_of = a["ctxT"].rearrange("(c p) b t -> p c b t", p=P)
        wide = a["rel_v_wide"]

        def rel_v_piece(n):
            slot = n % VSLOTS
            if slot < 2:
                return rel_v[:, slot].rearrange("p i d -> p (i d)")
            return v[:TEXT, slot // 2 - 1, slot % 2 * VI * DH:(slot % 2 + 1) * VI * DH]

        def groups(engine, body):
            body(0, False)
            with engine.Fori(1, NG - 1) as g:
                body(g, False)
            body(NG - 1, True)

        block = ctx.enter_context(nc.Block())

        @block.sync
        def _(sp):
            for to, w in loads:
                sp.dma_start(to, w).then_inc(loaded, 16)

            def load_image(g):
                if not isinstance(g, int) or g > 0:
                    i, n = bank_count(g - 1, use_image(3))
                    wait_apart(sp, raw[i], n + 1, passed_sp)
                for c in range(EC):
                    sp.dma_start(context_image[:, c], context_of[:, c, bass.ds(g * K4, K4), TEXT:TEXT + IMG]).then_inc(
                        image_loaded, 16)

            def load_context(g, k):
                if k >= 2 or not isinstance(g, int):
                    i, n = bank_count(g, use_v(k - 2, 7)) if k >= 2 else bank_count(g - 1, use_v(k + 2, 7))
                    wait_apart(sp, raw[i], n + 1, passed_sp)
                sp.dma_start(context[:, k % 2], context_of[:, :, bass.ds(g * K4 + k, 1), :].rearrange(
                    "p c b t -> p c (b t)")).then_inc(context_loaded[k % 2], 16)

            def load_rel_v(g, n):
                slot = n % VSLOTS
                if n >= VSLOTS:
                    wait_apart(sp, rel_v_raw, g * NV + n - VSLOTS + 1, passed_sp)
                elif slot >= 2:
                    wait_apart(sp, av_done, head_count(g, K4 - 1, H - 1), passed_sp)
                elif not isinstance(g, int) or g > 0:
                    wait_apart(sp, rel_v_raw, g * NV, passed_sp)
                source = bass.AP(tensor=wide.tensor, offset=n * VI * DH, ap=[[DH, TEXT], [1, VI * DH]])
                sp.dma_start(rel_v_piece(n), source).then_inc(rel_v_loaded[slot], 16)

            def body(g, last):
                load_image(g)
                for k in range(K4):
                    load_context(g, k)
                for n in range(NV):
                    load_rel_v(g, n)

            groups(sp, body)

        @block.tensor
        def _(pe):
            def free_bank(g, u):
                i, n = bank_count(g, u)
                wait(pe, taken[i], n)
                return i

            def project_x(g, k):
                pe.wait_ge(xs_ready, g * K4 + k + 1)
                i = free_bank(g, use_x(k))
                for c in range(EC):
                    last = nc.tensor.transpose(ps_p[i][:, c * S:(c + 1) * S], xs[:, c * P:(c + 1) * P], ident[:S, :S])
                last.then_inc(raw[i], 1)

            def project_q(g, k, j):
                if j == 0:
                    xi, xn = bank_count(g, use_x(k))
                    pe.wait_ge(taken[xi], xn + 1)
                i = free_bank(g, use_q(k, j))
                for m in range(4):
                    for c in range(EC):
                        at = (4 * j + m) * P
                        last = nc.tensor.matmul(ps_p[i][:, m * S:(m + 1) * S], w_q[:, c, at:at + P], xT[:, c, :],
                                                start=(c == 0), stop=(c == EC - 1))
                last.then_inc(raw[i], 1)

            def relative_keys(g):
                for n in range(S // QI):
                    if n == 0:
                        for i in range(2):
                            u = use_image(0) - 2 + i
                            pe.wait_ge(taken[u % 2], bank_count(g, u)[1] + 1)
                        wait(pe, exps_done, head_count(g, 0, -1))
                    wait(pe, rel_taken[n % 2], g * (S // QI // 2) + n // 2)
                    for j in range(QI):
                        i = n * QI + j
                        last = nc.tensor.matmul(ps_s[n % 2][:TEXT, j * K4 * H:(j + 1) * K4 * H],
                                                rel_k[:, S - 1 - i:S - 1 - i + TEXT],
                                                q_head[:, :, :, i].rearrange("p k h -> p (k h)"), start=True, stop=True)
                    last.then_inc(rel_raw[n % 2], 1)

            def project_image(g, j):
                i = free_bank(g, use_image(j))
                pe.wait_ge(image_loaded, 16 * EC * (g + 1))
                image = [context_image[:, c].rearrange("p k t -> p (k t)") for c in range(EC)]
                if j < 2:
                    for m in range(4):
                        at = (4 * j + m) * P
                        for c in range(EC):
                            last = nc.tensor.matmul(ps_p[i][:, m * K4 * IMG:(m + 1) * K4 * IMG], w_k[1][:, c, at:at + P],
                                                    image[c], start=(c == 0), stop=(c == EC - 1))
                else:
                    half = slice((j - 2) * 512, (j - 1) * 512)
                    for c in range(EC):
                        last = nc.tensor.matmul(ps_p[i][IMG_ROW:P, :], image[c], w_v[1][:, c, half], start=(c == 0),
                                                stop=(c == EC - 1), tile_position=(0, IMG_ROW))
                last.then_inc(raw[i], 1)

            def project_k(g, k, m):
                i = free_bank(g, use_k(k, m))
                if m == 0:
                    pe.wait_ge(context_loaded[k % 2], 16 * (g * (K4 // 2) + k // 2 + 1))
                for w, (lo, hi), token in ((w_k[0], columns[0], 0), (w_k[2], columns[1], TEXT + IMG)):
                    for c in range(EC):
                        last = nc.tensor.matmul(ps_p[i][:, lo:hi], w[:, c, m * P:(m + 1) * P],
                                                context[:, k % 2, c, token:token + hi - lo], start=(c == 0),
                                                stop=(c == EC - 1))
                last.then_inc(raw[i], 1)

            def project_v(g, k, j):
                t, half = j // 2, slice(j % 2 * 512, j % 2 * 512 + 512)
                i = free_bank(g, use_v(k, j))
                token, rows = value_rows(t)
                w = w_v[0] if t == 0 else w_v[2]
                for c in range(EC):
                    last = nc.tensor.matmul(ps_p[i][:rows, :], context[:, k % 2, c, token:token + rows], w[:, c, half],
                                            start=(c == 0), stop=(c == EC - 1))
                last.then_inc(raw[i], 1)

            def scores(g, k, h):
                n = head_count(g, k, h)
                if h == 0:
                    u = use_v(k, 0) - 2
                    for i in range(2):
                        pe.wait_ge(taken[(u + i) % 2], bank_count(g, u + i)[1] + 1)
                    pe.wait_ge(k_image_placed, g * K4 + k + 1)
                    if k == 0:
                        for i in range(2):
                            pe.wait_ge(rel_taken[i], (g + 1) * (S // QI // 2))
                wait(pe, exps_done, n - 2)
                out = ps_s[h % 2]
                nc.tensor.matmul(out[:S, 0:CTX], q_head[:, k, h, :], kT[:, h // 2, :], start=True, stop=False)
                nc.tensor.matmul(out[:S, 0:TEXT], turned[:TEXT, k, h, :], ident[:TEXT, :TEXT], start=False,
                                 stop=True).then_inc(scores_raw, 1)

            def turn_probs(g, k, h):
                n = head_count(g, k, h)
                pe.wait_ge(probs_ready, n)
                wait(pe, probsT_ready, n - 2)
                if k == 0 and h < 2:
                    wait(pe, rel_v_added, g * NV)
                out, slot = ps_t[h % 2], h % RING
                nc.tensor.transpose(out[:TEXT, 0:S], probs[:, slot, 0:TEXT], ident[:S, :S])
                for t in range(3):
                    at = TEXT + t * P
                    last = nc.tensor.transpose(out[:, (t + 1) * S:(t + 2) * S], probs[:, slot, at:at + P], ident[:S, :S])
                last.then_inc(probsT_raw, 1)

            def weigh_values(g, k, h):
                pe.wait_ge(probsT_ready, head_count(g, k, h))
                if h % HH == 0:
                    wait(pe, out_taken[h // HH], g * K4 + k)
                    if k == 0:
                        wait(pe, z_ready, g * K4)
                if h == 0:
                    for i in range(2):
                        u = use_v(k, 6 + i)
                        pe.wait_ge(taken[u % 2], bank_count(g, u)[1] + 1)
                row, at = h % 2 * DH, h % HH // 2 * S
                out = ps_o[h // HH][row:row + DH, at:at + S]
                feat = slice(h * DH, (h + 1) * DH)
                nc.tensor.matmul(out, v[:TEXT, 0, feat], turned[:TEXT, k, h, :], start=True, stop=False,
                                 tile_position=(0, row), skip_group_check=True)
                for t in range(3):
                    last = nc.tensor.matmul(out, v[:, t + 1, feat], audT[:, h % 2, t, :], start=False, stop=(t == 2),
                                            tile_position=(0, row), skip_group_check=True)
                last.then_inc(av_done, 1)

            def relative_values(g):
                for n in range(NV):
                    slot, used = n % VSLOTS, n // VSLOTS
                    a_group = (NV - 1 - slot) // VSLOTS + 1
                    pe.wait_ge(rel_v_loaded[slot], 16 * (g * a_group + used + 1))
                    wait(pe, rel_v_added, g * NV + n - 1)
                    for j in range(VI):
                        i, at = S - 1 - (n * VI + j), (VI - 1 - j) * K4 * H
                        last = nc.tensor.matmul(ps_t[n % 2][:DH, at:at + K4 * H], rel_v_piece(n)[:, j * DH:(j + 1) * DH],
                                                turned[:TEXT, :, :, i].rearrange("p k h -> p (k h)"),
                                                start=True, stop=True)
                    last.then_inc(rel_v_raw, 1)

            def project_out(g, k):
                if k == 0:
                    pe.wait_ge(rel_v_added, (g + 1) * NV)
                if k >= 2:
                    pe.wait_ge(z_ready, g * K4 + k - 1)
                for m in range(NP):
                    last = nc.tensor.matmul(ps_o[k % 2][:S, 0:E], outT[:, k, m, :], w_o[:, m, :], start=(m == 0),
                                            stop=(m == NP - 1))
                last.then_inc(y_raw, 1)

            pe.wait_ge(loaded, all_loaded)
            pe.wait_ge(zeroed, 3)
            pe.wait_ge(rel_k_ready, 1)

            for k in range(K4):
                project_x(0, k)
                project_q(0, k, 0)
                project_q(0, k, 1)

            def body(g, last):
                relative_keys(g)
                for j in range(4):
                    project_image(g, j)
                for m in range(NP):
                    project_k(g, 0, m)
                for k in range(K4):
                    for j in range(8):
                        project_v(g, k, j)
                    for h in range(H + AV_LAG):
                        if h < H:
                            scores(g, k, h)
                        if T_LAG <= h < H + T_LAG:
                            turn_probs(g, k, h - T_LAG)
                        if AV_LAG <= h:
                            weigh_values(g, k, h - AV_LAG)
                        if h >= H and k < K4 - 1:
                            project_k(g, k + 1, 2 * (h - H))
                            project_k(g, k + 1, 2 * (h - H) + 1)
                relative_values(g)
                for k in range(K4):
                    if not last:
                        project_x(g + 1, k)
                    project_out(g, k)
                    if not last:
                        project_q(g + 1, k, 0)
                        project_q(g + 1, k, 1)

            groups(pe, body)

        @block.scalar
        def _(act):
            def arrived(g, u):
                act.wait_ge(raw[0], bank_count(g, u)[1] + 1)

            def take_x(g, k):
                arrived(g, use_x(k))
                nc.scalar.copy(xT[:], ps_p[0][:, 0:EC * S].rearrange("p (c s) -> p c s", c=EC)).then_inc(taken[0], 1)

            def take_q(g, k, j):
                arrived(g, use_q(k, j))
                if k == 0:
                    wait(act, scores_raw, head_count(g, 0, -1))
                for odd in range(2):
                    rows = slice(odd * DH, odd * DH + DH)
                    last = nc.scalar.mul(q_head[rows, k, 8 * j + odd:8 * j + 8:2, :],
                                         ps_p[0][rows, 0:4 * S].rearrange("p (m s) -> p m s", m=4), DH ** -0.5)
                last.then_inc(taken[0], 1)

            def take_rel(g, n):
                act.wait_ge(rel_raw[0], g * (S // QI // 2) + n // 2 + 1)
                wait(act, rel_v_raw, g * NV)
                nc.scalar.copy(turned[:TEXT, :, :, n * QI:(n + 1) * QI].rearrange("p k h i -> p (k h) i"),
                               ps_s[0][:TEXT, :].rearrange("p (i n) -> p n i", i=QI)).then_inc(rel_taken[0], 1)

            def take_k(g, k, m):
                arrived(g, use_k(k, m))
                wait(act, scores_raw, head_count(g, k, -1))
                nc.scalar.copy(kT[:, m, 0:TEXT + AUD], ps_p[0][:, 0:TEXT + AUD]).then_inc(taken[0], 1)

            def take_image(g, j):
                arrived(g, use_image(j))
                if j < 2:
                    nc.scalar.copy(k_image[:, 4 * j:4 * j + 4].rearrange("p m t -> p (m t)"), ps_p[0][:, 0:4 * K4 * IMG]).then_inc(
                        taken[0], 1)
                else:
                    half = slice((j - 2) * 512, (j - 1) * 512)
                    wait(act, av_done, head_count(g, 0, -1))
                    nc.scalar.copy(v[IMG_ROW:P, 3, half], ps_p[0][IMG_ROW:P, :]).then_inc(taken[0], 1)

            def take_v(g, k, j):
                t, half = j // 2, slice(j % 2 * 512, j % 2 * 512 + 512)
                arrived(g, use_v(k, j))
                wait(act, av_done, head_count(g, k, -1))
                rows = value_rows(t)[1]
                nc.scalar.copy(v[:rows, t, half], ps_p[0][:rows, :]).then_inc(taken[0], 1)

            def exponentials(g, k, h):
                n = head_count(g, k, h)
                act.wait_ge(max_ready, n)
                wait(act, probsT_raw, n - RING)
                wait(act, inverse_ready, n - RING)
                slot = h % RING
                for j in range(3):
                    lo, hi = columns[j]
                    to, end = places(k)[j]
                    last = nc.scalar.activation(probs[:, slot, to:end], ps_s[h % 2][:S, lo:hi], ACT.Exp,
                                                bias=neg_max[:, slot, j:j + 1], accum_out=total[:, slot, j:j + 1])
                last.then_inc(exps_done, 1)

            def place_image(g, k):
                if k == 0:
                    for j in range(2):
                        i, n = bank_count(g, use_image(j))
                        act.wait_ge(taken[i], n + 1)
                wait(act, scores_raw, head_count(g, k, -1))
                nc.scalar.copy(kT[:, :, TEXT + AUD:CTX], k_image[:, :, k * IMG:(k + 1) * IMG]).then_inc(k_image_placed, 1)

            def take_out(g, k, half):
                act.wait_ge(av_done, head_count(g, k, (half + 1) * HH - 1))
                if k == 0:
                    wait(act, y_raw, g * K4)
                nc.scalar.copy(outT[:, k, half * 4:half * 4 + 4, :],
                               ps_o[half][:, 0:4 * S].rearrange("p (m s) -> p m s", m=4)).then_inc(out_taken[half], 1)

            act.wait_ge(loaded, all_loaded)
            nc.scalar.activation(gain[:, 1:3], gain[:, 1:3], ACT.Tanh).then_inc(tanh_done, 1)
            act.wait_ge(zeroed, 3)

            def mine(u):
                return u % 2 == 0

            def take_xq(g, k):
                if mine(use_x(k)):
                    take_x(g, k)
                for j in range(2):
                    if mine(use_q(k, j)):
                        take_q(g, k, j)

            for k in range(K4):
                take_xq(0, k)

            def body(g, last):
                for n in range(0, S // QI, 2):
                    take_rel(g, n)
                for j in range(0, 4, 2):
                    take_image(g, j)
                place_image(g, 0)
                for m in range(0, NP, 2):
                    take_k(g, 0, m)
                for k in range(K4):
                    for j in range(0, 8, 2):
                        take_v(g, k, j)
                    for h in range(H + AV_LAG):
                        if h < H:
                            exponentials(g, k, h)
                        if h == HH + AV_LAG:
                            take_out(g, k, 0)
                        if h == H and k < K4 - 1:
                            place_image(g, k + 1)
                        if h >= H and k < K4 - 1:
                            take_k(g, k + 1, 2 * (h - H))
                    take_out(g, k, 1)
                if not last:
                    for k in range(K4):
                        take_xq(g + 1, k)

            groups(act, body)

        @block.vector
        def _(dve):
            def arrived(g, u):
                dve.wait_ge(raw[1], bank_count(g, u)[1] + 1)

            def take_x(g, k):
                arrived(g, use_x(k))
                nc.vector.tensor_copy(xT[:], ps_p[1][:, 0:EC * S].rearrange("p (c s) -> p c s", c=EC)).then_inc(taken[1], 1)

            def take_q(g, k, j):
                arrived(g, use_q(k, j))
                if k == 0:
                    wait(dve, scores_raw, head_count(g, 0, -1))
                for odd in range(2):
                    rows = slice(odd * DH, odd * DH + DH)
                    last = nc.vector.tensor_scalar(q_head[rows, k, 8 * j + odd:8 * j + 8:2, :],
                                                   ps_p[1][rows, 0:4 * S].rearrange("p (m s) -> p m s", m=4),
                                                   DH ** -0.5, None, ALU.mult)
                last.then_inc(taken[1], 1)

            def take_rel(g, n):
                dve.wait_ge(rel_raw[1], g * (S // QI // 2) + n // 2 + 1)
                wait(dve, rel_v_raw, g * NV)
                nc.vector.tensor_copy(turned[:TEXT, :, :, n * QI:(n + 1) * QI].rearrange("p k h i -> p (k h) i"),
                                      ps_s[1][:TEXT, :].rearrange("p (i n) -> p n i", i=QI)).then_inc(rel_taken[1], 1)

            def take_k(g, k, m):
                arrived(g, use_k(k, m))
                wait(dve, scores_raw, head_count(g, k, -1))
                nc.vector.tensor_copy(kT[:, m, 0:TEXT + AUD], ps_p[1][:, 0:TEXT + AUD]).then_inc(taken[1], 1)

            def take_image(g, j):
                arrived(g, use_image(j))
                if j < 2:
                    nc.vector.tensor_copy(k_image[:, 4 * j:4 * j + 4].rearrange("p m t -> p (m t)"), ps_p[1][:, 0:4 * K4 * IMG]).then_inc(
                        taken[1], 1)
                else:
                    half = slice((j - 2) * 512, (j - 1) * 512)
                    wait(dve, av_done, head_count(g, 0, -1))
                    nc.vector.tensor_copy(v[IMG_ROW:P, 3, half], ps_p[1][IMG_ROW:P, :]).then_inc(taken[1], 1)

            def take_v(g, k, j):
                t, half = j // 2, slice(j % 2 * 512, j % 2 * 512 + 512)
                arrived(g, use_v(k, j))
                wait(dve, av_done, head_count(g, k, -1))
                rows = value_rows(t)[1]
                nc.vector.tensor_copy(v[:rows, t, half], ps_p[1][:rows, :]).then_inc(taken[1], 1)

            def row_max(g, k, h):
                n = head_count(g, k, h)
                dve.wait_ge(scores_raw, n)
                wait(dve, exps_done, n - RING)
                for j, (lo, hi) in enumerate(columns):
                    last = nc.vector.tensor_reduce(neg_max[:, h % RING, j:j + 1], ps_s[h % 2][:S, lo:hi], AX_X, ALU.max,
                                                   negate=True)
                last.then_inc(max_ready, 1)

            def invert(g, k, h):
                n = head_count(g, k, h)
                dve.wait_ge(exps_done, n)
                wait(dve, probs_ready, n - RING)
                nc.vector.reciprocal(inverse[:, h % RING, :], total[:, h % RING, :]).then_inc(inverse_ready, 1)

            def take_probsT(g, k, h):
                n = head_count(g, k, h)
                dve.wait_ge(probsT_raw, n)
                wait(dve, av_done, n - 2)
                nc.vector.tensor_copy(turned[:, k, h, :], ps_t[h % 2][:TEXT, 0:S])
                nc.vector.tensor_copy(audT[:, h % 2], ps_t[h % 2][:, S:4 * S].rearrange("p (t s) -> p t s", t=3)).then_inc(
                    probsT_ready, 1)

            def add_rel_v(g, n):
                dve.wait_ge(rel_v_raw, g * NV + n + 1)
                if n == 0:
                    for i in range(2):
                        dve.wait_ge(out_taken[i], (g + 1) * K4)
                lo = S - (n + 1) * VI
                for odd in range(2):
                    to = outT[odd * DH:(odd + 1) * DH, :, :, lo:lo + VI].rearrange("p k m i -> p (k m) i")
                    product = ps_t[n % 2][:DH, 0:VI * K4 * H].rearrange("p (i n two) -> p two n i", i=VI, two=2)
                    last = nc.vector.tensor_tensor(to, product[:, odd], to, ALU.add)
                last.then_inc(rel_v_added, 1)

            def add_residual(g, k):
                b = g * K4 + k
                dve.wait_ge(y_raw, b + 1)
                dve.wait_ge(x_bias_ready, b + 1)
                wait(dve, norm.x_ready, b)
                nc.vector.tensor_tensor(norm.z[:], ps_o[k % 2][:S, 0:E], x_bias[:], ALU.add).then_inc(z_ready, 1)
                norm.take_stats(nc, dve, b, z_ready, b + 1, passed)

            dve.wait_ge(loaded, all_loaded)
            nc.vector.tensor_copy(rel_k[:, 0:S - 17], rel_k[:, S - 17:S - 16].broadcast_to([P, S - 17]))
            nc.vector.tensor_copy(rel_k[:, S + 16:WIDE], rel_k[:, S + 15:S + 16].broadcast_to([P, WIDE - S - 16])).then_inc(
                rel_k_ready, 1)
            dve.wait_ge(tanh_done, 1)
            nc.vector.tensor_scalar(gain[:, 1:3], gain[:, 1:3], 1.0, None, ALU.add).then_inc(gain_ready, 1)
            dve.wait_ge(zeroed, 3)

            def mine(u):
                return u % 2 == 1

            for k in range(K4):
                if mine(use_x(k)):
                    take_x(0, k)
                for j in range(2):
                    if mine(use_q(k, j)):
                        take_q(0, k, j)

            def body(g, last):
                for n in range(1, S // QI, 2):
                    take_rel(g, n)
                for j in range(1, 4, 2):
                    take_image(g, j)
                for m in range(1, NP, 2):
                    take_k(g, 0, m)
                for k in range(K4):
                    for j in range(1, 8, 2):
                        take_v(g, k, j)
                    for h in range(H + AV_LAG):
                        if h < H:
                            row_max(g, k, h)
                        if 1 <= h <= H:
                            invert(g, k, h - 1)
                        if T_LAG <= h < H + T_LAG:
                            take_probsT(g, k, h - T_LAG)
                        if h >= H and k < K4 - 1:
                            take_k(g, k + 1, 2 * (h - H) + 1)
                for n in range(NV):
                    add_rel_v(g, n)
                for k in range(K4):
                    if not last and mine(use_x(k)):
                        take_x(g + 1, k)
                    add_residual(g, k)
                    for j in range(2):
                        if not last and mine(use_q(k, j)):
                            take_q(g + 1, k, j)
                    norm.apply(nc, dve, g * K4 + k)

            groups(dve, body)

        @block.gpsimd
        def _(pool):
            def take_x(g, k):
                b = g * K4 + k
                if k > 0:
                    i, n = bank_count(g, use_x(k - 1))
                    wait(pool, raw[i], n + 1)
                nc.gpsimd.tensor_copy(xs[:], row_of(x, b)).then_inc(xs_ready, 1)

            def normalise(g, k, h):
                n = head_count(g, k, h)
                wait_apart(pool, inverse_ready, n, passed_pool)
                if h < RING and not (isinstance(g, int) and g == 0 and k == 0):
                    lo, hi = places((k - 1) % K4)[2]
                    nc.gpsimd.memset(probs[:, h % RING, lo:hi], 0.0)
                for j, (lo, hi) in enumerate(places(k)):
                    at = probs[:, h % RING, lo:hi]
                    last = nc.gpsimd.tensor_scalar(at, at, inverse[:, h % RING, j:j + 1], gain[:, j:j + 1], ALU.mult,
                                                   ALU.mult)
                last.then_inc(probs_ready, 1)

            def add_bias(g, k):
                b = g * K4 + k
                wait(pool, z_ready, b)
                nc.gpsimd.tensor_tensor(x_bias[:], row_of(x, b), b_o[:], ALU.add).then_inc(x_bias_ready, 1)

            nc.gpsimd.memset(q_head[:], 0.0).then_inc(zeroed, 1)
            nc.gpsimd.memset(v[:], 0.0).then_inc(zeroed, 1)
            nc.gpsimd.memset(probs[:], 0.0).then_inc(zeroed, 1)
            nc.gpsimd.memset(gain[:, 0:1], 1.0)
            pool.wait_ge(gain_ready, 1)

            for k in range(K4):
                take_x(0, k)

            def body(g, last):
                for k in range(K4):
                    for h in range(H):
                        normalise(g, k, h)
                if not last:
                    take_x(g + 1, 0)
                for k in range(K4):
                    add_bias(g, k)
                    if not last and k < K4 - 1:
                        take_x(g + 1, k + 1)
                    norm.gpsimd(nc, pool, g * K4 + k, passed_pool)

            groups(pool, body)


def ffn_binary(nc, shared, name, a):
    x, ident = shared["x"], shared["ident"]
    HALF = FC // 2
    with ExitStack() as ctx:
        buf = Buffers(nc, ctx, name, shared["semaphores"])
        w1, w2 = buf.sb("w1", [P, EC, HID]), buf.sb("w2", [P, FC, E])
        w1_rows, w2_rows = buf.sb("w1_rows", [P, FC, E]), buf.sb("w2_rows", [P, EC, HID])
        negative = buf.sb("negative", [P, EC * HID])
        alpha1, alpha2 = buf.sb("alpha1", [P, FC]), buf.sb("alpha2", [P, EC])
        alpha2_diag, alpha2_row = buf.sb("alpha2_diag", [P, E]), buf.sb("alpha2_row", [S, E])
        bias1, bias2 = buf.sb("bias1", [P, FC]), buf.sb("bias2", [S, E])
        ones = buf.sb("ones", [P, P])
        xs, xT = buf.sb("xs", [S, E]), buf.sb("xT", [P, EC, S])
        hidden = buf.sb("hidden", [P, FC, S])
        x_bias, z_raw = buf.sb("x_bias", [S, E]), buf.sb("z_raw", [S, E])
        norm = Norm(buf, shared)
        ps_x, ps_y, ps_w = buf.psum("ps_x"), buf.psum("ps_y"), buf.psum("ps_w")
        ps_h = [buf.psum(f"ps_h{i}") for i in range(2)]

        loaded, passed, passed_pool, ones_ready = (buf.sem(n) for n in ("loaded", "passed", "passed_pool", "ones_ready"))
        prep, signs_ready, diag_ready, row_raw, row_ready = (buf.sem(n) for n in (
            "prep", "signs_ready", "diag_ready", "row_raw", "row_ready"))
        xs_ready, xT_raw, xT_ready, h_raw, gelu_done = (buf.sem(n) for n in (
            "xs_ready", "xT_raw", "xT_ready", "h_raw", "gelu_done"))
        y_raw, scaled, x_bias_ready, z_ready = (buf.sem(n) for n in ("y_raw", "scaled", "x_bias_ready", "z_ready"))

        loads = [(w1[:], a["L1_ffn_w1T"].rearrange("(c p) n -> p c n", p=P)),
                 (w2[:], a["L1_ffn_w2T"].rearrange("(c p) n -> p c n", p=P)),
                 (w1_rows[:], a["L1_ffn_w1"].rearrange("(c p) n -> p c n", p=P)),
                 (w2_rows[:], a["L1_ffn_w2"].rearrange("(c p) n -> p c n", p=P)),
                 (bias1[:], a["L1_ffn_b1"]),
                 (bias2[:], a["L1_ffn_b2"].rearrange("(a n) -> a n", a=1).partition_broadcast(S))]
        all_loaded = 16 * len(loads)
        block = ctx.enter_context(nc.Block())

        @block.sync
        def _(sp):
            for to, w in loads:
                sp.dma_start(to, w).then_inc(loaded, 16)

        @block.tensor
        def _(pe):
            def turn_x(b):
                pe.wait_ge(xs_ready, b + 1)
                wait(pe, xT_ready, b)
                for c in range(EC):
                    last = nc.tensor.transpose(ps_x[:, c * S:(c + 1) * S], xs[:, c * P:(c + 1) * P], ident[:S, :S])
                last.then_inc(xT_raw, 1)

            def up(b):
                pe.wait_ge(xT_ready, b + 1)
                for m in range(FC):
                    if m % HALF == 0:
                        wait(pe, gelu_done, 2 * (b - 1) + m // HALF + 1)
                    for c in range(EC):
                        last = nc.tensor.matmul(ps_h[m // HALF][:, m % HALF * S:(m % HALF + 1) * S],
                                                w1[:, c, m * P:(m + 1) * P], xT[:, c, :],
                                                start=(c == 0), stop=(c == EC - 1))
                    if m % HALF == HALF - 1:
                        last.then_inc(h_raw, 1)

            def down(b):
                wait(pe, scaled, b)
                for m in range(FC):
                    if m % HALF == 0:
                        pe.wait_ge(gelu_done, 2 * b + m // HALF + 1)
                    last = nc.tensor.matmul(ps_y[:S, 0:E], hidden[:, m, :], w2[:, m, :], start=(m == 0), stop=(m == FC - 1))
                last.then_inc(y_raw, 1)

            pe.wait_ge(diag_ready, 1)
            pe.wait_ge(ones_ready, 1)
            nc.tensor.matmul(ps_w[:S, 0:E], ones[:, 0:S], alpha2_diag[:], start=True, stop=True).then_inc(row_raw, 1)
            pe.wait_ge(signs_ready, 2)
            turn_x(0)
            up(0)

            def body(b, first, last):
                if not last:
                    turn_x(b + 1)
                down(b)
                if not last:
                    up(b + 1)

            sequences(pe, body)

        @block.scalar
        def _(act):
            def take_xT(b):
                act.wait_ge(xT_raw, b + 1)
                wait(act, h_raw, 2 * b)
                nc.scalar.copy(xT[:], ps_x[:, 0:EC * S].rearrange("p (c s) -> p c s", c=EC)).then_inc(xT_ready, 1)

            def gelu(b):
                wait(act, y_raw, b)
                for m in range(FC):
                    if m % HALF == 0:
                        act.wait_ge(h_raw, 2 * b + m // HALF + 1)
                    last = nc.scalar.activation(hidden[:, m, :], ps_h[m // HALF][:, m % HALF * S:(m % HALF + 1) * S],
                                                ACT.Gelu, bias=bias1[:, m:m + 1], scale=alpha1[:, m:m + 1])
                    if m % HALF == HALF - 1:
                        last.then_inc(gelu_done, 1)

            act.wait_ge(row_raw, 1)
            nc.scalar.copy(alpha2_row[:], ps_w[:S, 0:E]).then_inc(row_ready, 1)
            act.wait_ge(prep, 2)
            take_xT(0)
            gelu(0)

            def body(b, first, last):
                if not last:
                    take_xT(b + 1)
                    gelu(b + 1)

            sequences(act, body)

        @block.vector
        def _(dve):
            dve.wait_ge(loaded, all_loaded)
            nc.vector.tensor_reduce(alpha2[:], w2_rows[:], AX_X, ALU.add, apply_absolute_value=True)
            nc.vector.tensor_reduce(alpha1[:], w1_rows[:], AX_X, ALU.add, apply_absolute_value=True).then_inc(prep, 1)
            dve.wait_ge(prep, 1)
            nc.vector.tensor_scalar(alpha1[:], alpha1[:], 1.0 / E, None, ALU.mult)
            nc.vector.tensor_scalar(alpha2[:], alpha2[:], 1.0 / HID, None, ALU.mult).then_inc(prep, 1)
            dve.wait_ge(prep, 2)
            for c in range(EC):
                last = nc.vector.tensor_scalar(alpha2_diag[:, c * P:(c + 1) * P], ident[:], alpha2[:, c:c + 1], None,
                                               ALU.mult)
            last.then_inc(diag_ready, 1)
            for i, w in enumerate((w1, w2)):
                flat = w[:].rearrange("p c n -> p (c n)")
                wait(dve, signs_ready, i)
                nc.vector.tensor_scalar(negative[:], flat, 0.0, None, ALU.is_lt).then_inc(prep, 1)
                dve.wait_ge(prep, 3 + i)
                nc.vector.scalar_tensor_tensor(flat, flat, 0.0, negative[:], ALU.is_gt, ALU.subtract).then_inc(
                    signs_ready, 1)
            dve.wait_ge(row_ready, 1)

            def body(b, first, last):
                dve.wait_ge(y_raw, b + 1)
                nc.vector.tensor_tensor(z_raw[:], ps_y[:S, 0:E], alpha2_row[:], ALU.mult).then_inc(scaled, 1)
                dve.wait_ge(scaled, b + 1)
                dve.wait_ge(x_bias_ready, b + 1)
                nc.vector.tensor_tensor(norm.z[:], z_raw[:], x_bias[:], ALU.add).then_inc(z_ready, 1)
                norm.vector(nc, dve, b, z_ready, b + 1, passed)

            sequences(dve, body)

        @block.gpsimd
        def _(pool):
            def take_x(b):
                wait(pool, xT_raw, b)
                nc.gpsimd.tensor_copy(xs[:], row_of(x, b)).then_inc(xs_ready, 1)

            def add_bias(b):
                wait(pool, z_ready, b)
                nc.gpsimd.tensor_tensor(x_bias[:], row_of(x, b), bias2[:], ALU.add).then_inc(x_bias_ready, 1)

            nc.gpsimd.memset(ones[:], 1.0).then_inc(ones_ready, 1)
            pool.wait_ge(loaded, all_loaded)
            take_x(0)

            def body(b, first, last):
                if not last:
                    take_x(b + 1)
                add_bias(b)
                norm.gpsimd(nc, pool, b, passed_pool)

            sequences(pool, body)


def build(nc, a, out):
    with ExitStack() as ctx:
        semaphores = []
        buf = Buffers(nc, ctx, "all", semaphores)
        shared = {
            "semaphores": semaphores,
            "x": buf.sb("x", [S, B, E]),
            "ident": buf.sb("ident", [P, P]),
            "minus_half": buf.sb("minus_half", [S, 1]),
            "mask16": a["c_mask16"],
            "mask16_fine": a["c_mask16_fine"],
        }
        with ExitStack() as inner:
            start = Buffers(nc, inner, "start", semaphores)
            x_loaded, zeroed, ident_ready = start.sem("x_loaded"), start.sem("zeroed"), start.sem("ident_ready")
            block = inner.enter_context(nc.Block())

            @block.sync
            def _(sp):
                sp.dma_start(shared["x"][:], a["x"].rearrange("b s e -> s b e")).then_inc(x_loaded, 16)
                sp.wait_ge(x_loaded, 16)

            @block.gpsimd
            def _(pool):
                nc.gpsimd.memset(shared["ident"][:], 0.0).then_inc(zeroed, 1)
                nc.gpsimd.memset(shared["minus_half"][:], -0.5)
                pool.wait_ge(zeroed, 1)
                nc.gpsimd.affine_select(out=shared["ident"][:], in_=shared["ident"][:], compare_op=ALU.not_equal,
                                        fill=1.0, base=0, pattern=[[-1, P]], channel_multiplier=1).then_inc(
                    ident_ready, 1)
                pool.wait_ge(ident_ready, 1)

        start_anew(nc, semaphores)
        for n in range(LAYERS):
            if n == 0:
                self_attention(nc, shared, "l0sa", a["L0_attn_Wq"], a["L0_attn_Wk"], a["L0_attn_Wv"], a["L0_attn_Wo"],
                               biases=[a["L0_attn_bq"], a["L0_attn_bk"], a["L0_attn_bv"], a["L0_attn_bo"]])
            if n == 1:
                cross_attention_rope(nc, shared, "l0xa", a["ctxT"], a["L0_xattn_W_q"], a["L0_xattn_W_q_swap"],
                                     a["L0_xattn_W_k"], a["L0_xattn_W_k_swap"], a["L0_xattn_W_v"], a["L0_xattn_W_o"],
                                     a["c_rope"])
            if n == 2:
                ffn_quantised(nc, shared, "l0ff", a["L0_ffn_w1"], a["L0_ffn_conv_w"], a["L0_ffn_conv_b"], a["L0_ffn_w2"])
            if n == 3:
                self_attention(nc, shared, "l1sa", a["L1_attn_Wq"], a["L1_attn_Wk"], a["L1_attn_Wv"], a["L1_attn_Wo"],
                               pos=[a["c_posT"], a["c_causal"]])
            if n == 4:
                cross_attention_relative(nc, shared, "l1xa", a)
            if n == 5:
                ffn_binary(nc, shared, "l1ff", a)
            start_anew(nc, semaphores)

        with ExitStack() as inner:
            stored = Buffers(nc, inner, "end", semaphores).sem("stored")
            block = inner.enter_context(nc.Block())

            @block.sync
            def _(sp):
                sp.dma_start(out.rearrange("b s e -> s b e"), shared["x"][:]).then_inc(stored, 16)
                sp.wait_ge(stored, 16)


LAYERS = 6


def kernel(**inputs):
    import numpy as np
    import concourse.bacc as bacc
    from concourse.bass_utils import run_bass_kernel_spmd

    arrays = {n: np.ascontiguousarray(v) for n, v in inputs.items()}
    turned = ["L0_attn_Wq", "L0_attn_Wk", "L0_attn_Wv", "L0_attn_Wo", "L0_xattn_W_q", "L0_xattn_W_k", "L0_xattn_W_v",
              "L0_xattn_W_o", "L0_ffn_w1", "L0_ffn_w2"]
    for n in turned:
        arrays[n] = np.ascontiguousarray(arrays[n].T)
    for n in ("L0_attn_bq", "L0_attn_bk"):
        arrays[n] = np.ascontiguousarray(arrays[n].reshape(EC, P).T)
    swap = np.arange(E) ^ 1
    for n in ("L0_xattn_W_q", "L0_xattn_W_k"):
        arrays[n + "_swap"] = np.ascontiguousarray(arrays[n][:, swap])
    arrays["ctxT"] = np.ascontiguousarray(arrays.pop("ctx_1024").transpose(2, 0, 1))
    arrays["L0_ffn_conv_w"] = np.ascontiguousarray(arrays["L0_ffn_conv_w"].reshape(HID, 3))
    for n in ("L0_ffn_conv_b", "L1_ffn_b1"):
        arrays[n] = np.ascontiguousarray(arrays[n].reshape(FC, P).T)
    arrays["L1_ffn_w1T"] = np.ascontiguousarray(arrays["L1_ffn_w1"].T)
    arrays["L1_ffn_w2T"] = np.ascontiguousarray(arrays["L1_ffn_w2"].T)
    for n in ("L1_xattn_alpha", "L1_xattn_beta"):
        arrays[n] = arrays[n].reshape(1, 1)
    rel_v = arrays["L1_xattn_rel_v"]
    arrays["L1_xattn_rel_k"] = np.ascontiguousarray(arrays["L1_xattn_rel_k"].T)
    arrays["rel_v_wide"] = np.ascontiguousarray(
        np.concatenate([np.repeat(rel_v[:1], S - 1 - 16, 0), rel_v, np.repeat(rel_v[-1:], TEXT - 1 - 16, 0)]))

    own = (np.arange(P)[:, None] // D == np.arange(HC)[None, :])
    arrays["c_mask16"] = (own * 0.25).astype(np.float32)
    arrays["c_mask16_fine"] = (own * 0.0625).astype(np.float32)
    f = np.float32
    inv_freq = (f(1.0) / f(10000.0) ** (np.arange(0, D, 2, dtype=f) / f(D))).astype(f)
    ang = np.outer(np.arange(CTX, dtype=f), inv_freq).astype(f)
    cos, sin = np.cos(ang).T, np.sin(ang).T
    pair, odd = (np.arange(P) % D) // 2, np.arange(P) % 2
    arrays["c_rope"] = np.stack([cos[pair], sin[pair] * np.where(odd, 1.0, -1.0)[:, None]], 1).astype(f)
    idx = np.arange(S, dtype=f)
    scale = (f(1.0) / (f(10000.0) ** (np.arange(0, D, 2, dtype=f) / f(D)) + np.finfo(f).eps)).astype(f)
    ang = (idx[:, None] * scale[None, :]).astype(f)
    pos = np.stack([np.sin(ang), np.cos(ang)], -1).reshape(S, D)
    arrays["c_posT"] = np.ascontiguousarray(pos.T[np.arange(P) % D]).astype(f)
    arrays["c_causal"] = np.where(np.triu(np.ones((S, S), bool), 1), f(-1e37), f(0.0)).astype(f)

    nc = bacc.Bacc("TRN2", target_bir_lowering=False, num_devices=1)
    args = {n: nc.dram_tensor(f"in_{n}", v.shape, mybir.dt.from_np(v.dtype), kind="ExternalInput").ap()
            for n, v in arrays.items()}
    out = nc.dram_tensor("out_x", (B, S, E), F32, kind="ExternalOutput").ap()
    build(nc, args, out)
    result = run_bass_kernel_spmd(nc, [{f"in_{n}": v for n, v in arrays.items()}], core_ids=[0])
    return result.results[0]["out_x"]
```

```python
from contextlib import ExitStack

import concourse.bass as bass
from concourse import mybir

F32 = mybir.dt.float32
BF16 = mybir.dt.bfloat16
ALU = mybir.AluOpType
ACT = mybir.ActivationFunctionType
AX_X = mybir.AxisListType.X

P = 128
B, S, E = 16, 112, 256
H, D = 16, 16
EC = E // P
HC = P // D
CTX = 375
TEXT, IMG = 77, 16
AUD = CTX - TEXT - IMG
HID = 1024
FC = HID // P
LN_EPS = 1e-5
ROUND = 12582912.0
TAKEN = -3.0e38
TOP_K = 32


def wait(engine, semaphore, value):
    if isinstance(value, int) and value <= 0:
        return
    engine.wait_ge(semaphore, value)


def wait_apart(engine, semaphore, value, passed):
    if isinstance(value, int) and value <= 0:
        return
    engine.wait_ge(semaphore, value)
    engine.sem_inc(passed, 1)


def sequences(engine, body):
    body(0, True, False)
    with engine.Fori(1, B - 1) as b:
        body(b, False, False)
    body(B - 1, False, True)


def staggered(engine, body):
    body(0, 1, 2)
    with engine.Fori(1, B - 2) as b:
        body(b, b + 1, b + 2)
    body(B - 2, B - 1, None)
    body(B - 1, None, None)


class Buffers:

    def __init__(self, nc, ctx, name, semaphores):
        self.nc, self.ctx, self.name, self.semaphores = nc, ctx, name, semaphores

    def sb(self, name, shape, dtype=F32):
        return self.ctx.enter_context(self.nc.sbuf_tensor(f"{self.name}_{name}", shape, dtype))

    def psum(self, name, dtype=F32):
        return self.ctx.enter_context(self.nc.psum_tensor(f"{self.name}_{name}", [P, 2048 // (4 if dtype == F32 else 2)], dtype))

    def sem(self, name):
        handle = self.nc.alloc_semaphore(name=f"{self.name}_{name}")
        self.semaphores.append(handle)
        return handle


def start_anew(nc, semaphores):
    nc.clear_and_free_semaphores(semaphores)
    semaphores.clear()
    nc.all_engine_barrier()


def row_of(x, b):
    return x[:, bass.ds(b, 1), :].rearrange("p a n -> p (a n)")


class Norm:

    def __init__(self, buf, shared):
        self.z = buf.sb("z", [S, E])
        self.stats = buf.sb("stats", [S, 6])
        self.mean_var = buf.sb("mean_var", [S, 2])
        self.rstd = buf.sb("rstd", [S, 1])
        self.shared = shared
        self.var_ready = buf.sem("var_ready")
        self.rstd_ready = buf.sem("rstd_ready")
        self.eps_added = buf.sem("eps_added")
        self.stats_ready = buf.sem("stats_ready")
        self.mean_ready = buf.sem("mean_ready")
        self.x_ready = buf.sem("x_ready")

    def vector(self, nc, dve, b, z_ready, count, passed):
        self.take_stats(nc, dve, b, z_ready, count, passed)
        self.apply(nc, dve, b)

    def take_stats(self, nc, dve, b, z_ready, count, passed):
        dve.wait_ge(z_ready, count)
        nc.vector.bn_stats(self.stats[:], self.z[:]).then_inc(self.stats_ready, 1)
        wait_apart(dve, self.stats_ready, b + 1, passed)
        nc.vector.bn_aggr(self.mean_var[:], self.stats[:]).then_inc(self.mean_ready, 1)

    def apply(self, nc, dve, b):
        dve.wait_ge(self.rstd_ready, b + 1)
        nc.vector.tensor_scalar(row_of(self.shared["x"], b), self.z[:], self.mean_var[:, 0:1], self.rstd[:, 0:1],
                                ALU.subtract, ALU.mult).then_inc(self.x_ready, 1)

    def gpsimd(self, nc, pool, b, passed):
        wait_apart(pool, self.mean_ready, b + 1, passed)
        nc.gpsimd.tensor_scalar(self.rstd[:], self.mean_var[:, 1:2], LN_EPS, None, ALU.add).then_inc(self.eps_added, 1)
        pool.wait_ge(self.eps_added, b + 1)
        nc.gpsimd.tensor_tensor(self.rstd[:], self.rstd[:], self.shared["minus_half"][:], ALU.pow).then_inc(
            self.rstd_ready, 1)


def self_attention_weights(buf, wq, wk, wv, wo, head_mask, biases=None, pos=None):
    w = {n: buf.sb(n, [P, EC, E]) for n in ("w_q", "w_k", "w_v", "w_o")}
    loads = [(w[n][:], a.rearrange("(c p) n -> p c n", p=P)) for n, a in zip(w, (wq, wk, wv, wo))]
    w["head_mask"] = buf.sb("head_mask", [P, HC])
    loads.append((w["head_mask"][:], head_mask))
    if biases is not None:
        for n, a in zip(("b_q", "b_k"), biases):
            w[n] = buf.sb(n, [P, EC])
            loads.append((w[n][:], a))
        for n, a in zip(("b_v", "b_o"), biases[2:]):
            w[n] = buf.sb(n, [S, E])
            loads.append((w[n][:], a.rearrange("(a n) -> a n", a=1).partition_broadcast(S)))
    else:
        w.update(posT=buf.sb("posT", [P, S]), causal=buf.sb("causal", [S, S]))
        loads += [(w["posT"][:], pos[0]), (w["causal"][:], pos[1])]
    return w, loads


def self_attention(nc, shared, name, weights, top_k, prefetch=()):
    G, HG = 4, 4
    PAIR = 2
    CHAIN = 2 * (TOP_K // 8) * (HG // PAIR)
    FOUND_MAX = HG // PAIR
    DV = D + 1
    x, ident = shared["x"], shared["ident"]
    with ExitStack() as ctx:
        buf = Buffers(nc, ctx, name, shared["semaphores"])
        w_q, w_k, w_v, w_o, head_mask = (weights[n] for n in ("w_q", "w_k", "w_v", "w_o", "head_mask"))
        xs = buf.sb("xs", [S, E])
        xT = buf.sb("xT", [P, EC, S])
        qT = buf.sb("qT", [P, EC, S])
        kT = buf.sb("kT", [P, EC, S])
        q_head = buf.sb("q_head", [P, EC, HC, S])
        v_one = buf.sb("v_one", [S, H, DV])
        s_sb = buf.sb("s_sb", [S, 2, HG, S])
        neg_max = buf.sb("neg_max", [S, 2, HG])
        probs = buf.sb("probs", [S, 2, HG, S])
        probsT = buf.sb("probsT", [S, 2, HG, S])
        rden = buf.sb("rden", [S, H])
        o_sb = buf.sb("o_sb", [S, E])
        oT = buf.sb("oT", [P, EC, S])
        norm = Norm(buf, shared)
        if top_k:
            b_q, b_k, b_v, b_o = (weights[n] for n in ("b_q", "b_k", "b_v", "b_o"))
            top8 = buf.sb("top8", [S, 2, HG, TOP_K // 8, 8])
            left = buf.sb("left", [S, 2, HG, S])
            exps = buf.sb("exps", [S, 2, HG, S])
            taken = buf.sb("taken", [S, HG, S])
            x_bias = buf.sb("x_bias", [S, E])
        else:
            posT, causal = weights["posT"], weights["causal"]
        ps_s = [buf.psum(f"ps_s{i}") for i in range(2)]
        ps_t = [buf.psum(f"ps_t{i}") for i in range(2)]
        ps_o = buf.psum("ps_o")
        ps_a, ps_b, ps_c = buf.psum("ps_a"), buf.psum("ps_b"), buf.psum("ps_c")

        prefetched, passed = buf.sem("prefetched"), buf.sem("passed")
        ones_ready = buf.sem("ones_ready")
        xs_ready, xT_raw, xT_ready = buf.sem("xs_ready"), buf.sem("xT_raw"), buf.sem("xT_ready")
        q_raw, q_ready, k_raw, k_ready = (buf.sem(n) for n in ("q_raw", "q_ready", "k_raw", "k_ready"))
        v_raw, v_ready, q_head_ready = buf.sem("v_raw"), buf.sem("v_ready"), buf.sem("q_head_ready")
        scores_raw, scores_ready = buf.sem("scores_raw"), buf.sem("scores_ready")
        searched = buf.sem("searched")
        neg_ready, exps_done = buf.sem("neg_ready"), buf.sem("exps_done")
        taken_ready, probs_ready = buf.sem("taken_ready"), buf.sem("probs_ready")
        probsT_raw, probsT_ready = buf.sem("probsT_raw"), buf.sem("probsT_ready")
        av_done, rden_ready, o_ready = buf.sem("av_done"), buf.sem("rden_ready"), buf.sem("o_ready")
        oT_raw, oT_ready, y_raw = buf.sem("oT_raw"), buf.sem("oT_ready"), buf.sem("y_raw")
        z_ready, x_bias_ready = buf.sem("z_ready"), buf.sem("x_bias_ready")

        block = ctx.enter_context(nc.Block())

        @block.sync
        def _(sp):
            for to, a in prefetch:
                sp.dma_start(to, a).then_inc(prefetched, 16)
            if prefetch:
                sp.wait_ge(prefetched, 16 * len(prefetch))

        @block.tensor
        def _(pe):
            def project_xT(b):
                pe.wait_ge(xs_ready, b + 1)
                wait(pe, q_ready, b)
                for c in range(EC):
                    last = nc.tensor.transpose(ps_b[:, c * S:(c + 1) * S], xs[:, c * P:(c + 1) * P], ident[:S, :S])
                last.then_inc(xT_raw, 1)

            def project_qk(b):
                pe.wait_ge(xT_ready, b + 1)
                for w, out, raw in ((w_q, ps_b, q_raw), (w_k, ps_c, k_raw)):
                    for m in range(EC):
                        for c in range(EC):
                            last = nc.tensor.matmul(out[:, m * S:(m + 1) * S], w[:, c, m * P:(m + 1) * P], xT[:, c, :],
                                                    start=(c == 0), stop=(c == EC - 1))
                    last.then_inc(raw, 1)

            def project_v(b):
                wait(pe, z_ready, b)
                for c in range(EC):
                    last = nc.tensor.matmul(ps_a[:S, 0:E], xT[:, c, :], w_v[:, c, :], start=(c == 0), stop=(c == EC - 1))
                last.then_inc(v_raw, 1)

            def scores(b, g):
                if g == 0:
                    pe.wait_ge(k_ready, b + 1)
                if g % (G // EC) == 0:
                    pe.wait_ge(q_head_ready, b * EC + g // (G // EC) + 1)
                wait(pe, scores_ready, b * G + g - 1)
                for i in range(HG):
                    h = g * HG + i
                    last = nc.tensor.matmul(ps_s[g % 2][:S, i * S:(i + 1) * S], q_head[:, h // HC, h % HC, :],
                                            kT[:, h // HC, :], start=True, stop=True)
                last.then_inc(scores_raw, 1)

            def turn_probs(b, g):
                pe.wait_ge(probs_ready, b * G + g + 1)
                wait(pe, probsT_ready, b * G + g - 1)
                for i in range(HG):
                    last = nc.tensor.transpose(ps_t[g % 2][:S, i * S:(i + 1) * S], probs[:, g % 2, i, :], ident[:S, :S])
                last.then_inc(probsT_raw, 1)

            def weigh_values(b, g):
                pe.wait_ge(probsT_ready, b * G + g + 1)
                if g == 0:
                    pe.wait_ge(v_ready, b + 1)
                    wait(pe, o_ready, b)
                for i in range(HG):
                    h = g * HG + i
                    last = nc.tensor.matmul(ps_o[:S, h * DV:(h + 1) * DV], probsT[:, g % 2, i, :], v_one[:, h, :],
                                            start=True, stop=True)
                last.then_inc(av_done, 1)

            def turn_output(b, last_b=False):
                pe.wait_ge(o_ready, b + 1)
                if not last_b:
                    pe.wait_ge(k_ready, b + 3)
                for c in range(EC):
                    last = nc.tensor.transpose(ps_c[:, c * S:(c + 1) * S], o_sb[:, c * P:(c + 1) * P], ident[:S, :S])
                last.then_inc(oT_raw, 1)

            def project_out(b, last_b=False):
                pe.wait_ge(oT_ready, b + 1)
                if not last_b:
                    pe.wait_ge(v_ready, b + 2)
                for c in range(EC):
                    last = nc.tensor.matmul(ps_a[:S, 0:E], oT[:, c, :], w_o[:, c, :], start=(c == 0), stop=(c == EC - 1))
                last.then_inc(y_raw, 1)

            project_xT(0)
            project_qk(0)

            def body(b, first, last):
                scores(b, 0)
                if not first:
                    turn_probs(b - 1, 2)
                    weigh_values(b - 1, 1)
                project_v(b)
                scores(b, 1)
                if not first:
                    turn_probs(b - 1, 3)
                if not last:
                    project_xT(b + 1)
                if not first:
                    weigh_values(b - 1, 2)
                scores(b, 2)
                if not last:
                    project_qk(b + 1)
                if not first:
                    weigh_values(b - 1, 3)
                turn_probs(b, 0)
                scores(b, 3)
                weigh_values(b, 0)
                if not first:
                    turn_output(b - 1, last)
                turn_probs(b, 1)
                if not first:
                    project_out(b - 1)

            sequences(pe, body)
            turn_probs(B - 1, 2)
            weigh_values(B - 1, 1)
            turn_probs(B - 1, 3)
            weigh_values(B - 1, 2)
            weigh_values(B - 1, 3)
            turn_output(B - 1, True)
            project_out(B - 1, True)

        @block.scalar
        def _(act):
            def take_xT(b):
                act.wait_ge(xT_raw, b + 1)
                wait(act, v_raw, b)
                nc.scalar.copy(xT[:], ps_b[:, 0:EC * S].rearrange("p (c s) -> p c s", c=EC)).then_inc(xT_ready, 1)

            def take_q(b):
                act.wait_ge(q_raw, b + 1)
                wait(act, q_head_ready, b * EC)
                for m in range(EC):
                    last = nc.scalar.activation(qT[:, m, :], ps_b[:, m * S:(m + 1) * S], ACT.Identity,
                                                bias=b_q[:, m:m + 1])
                last.then_inc(q_ready, 1)

            def take_k(b):
                act.wait_ge(k_raw, b + 1)
                wait(act, scores_raw, b * G)
                for m in range(EC):
                    last = nc.scalar.activation(kT[:, m, :], ps_c[:, m * S:(m + 1) * S], ACT.Identity,
                                                bias=b_k[:, m:m + 1])
                last.then_inc(k_ready, 1)

            def take_scores(b, g):
                act.wait_ge(scores_raw, b * G + g + 1)
                wait(act, searched, (b * G + g - 1) * CHAIN)
                nc.scalar.copy(s_sb[:, g % 2], ps_s[g % 2][:S, 0:HG * S].rearrange("p (h s) -> p h s", h=HG)).then_inc(
                    scores_ready, 1)

            def exponentials(b, g):
                out, out_free = (exps, taken_ready) if top_k else (probs, probsT_raw)
                if top_k:
                    act.wait_ge(searched, (b * G + g) * CHAIN + FOUND_MAX)
                    nc.scalar.mul(neg_max[:, g % 2, :], top8[:, g % 2, :, 0, 0], -1.0).then_inc(neg_ready, 1)
                    wait(act, probs_ready, b * G + g - 1)
                else:
                    wait(act, probsT_raw, b * G + g - 1)
                act.wait_ge(neg_ready, b * G + g + 1)
                for i in range(HG):
                    last = nc.scalar.activation(out[:, g % 2, i, :], s_sb[:, g % 2, i, :], ACT.Exp,
                                                bias=neg_max[:, g % 2, i:i + 1])
                last.then_inc(exps_done if top_k else probs_ready, 1)

            def take_probsT(b, g):
                act.wait_ge(probsT_raw, b * G + g + 1)
                wait(act, av_done, b * G + g - 1)
                nc.scalar.copy(probsT[:, g % 2], ps_t[g % 2][:S, 0:HG * S].rearrange("p (h s) -> p h s", h=HG)).then_inc(
                    probsT_ready, 1)

            def take_oT(b):
                act.wait_ge(oT_raw, b + 1)
                nc.scalar.copy(oT[:], ps_c[:, 0:EC * S].rearrange("p (c s) -> p c s", c=EC)).then_inc(oT_ready, 1)

            take_xT(0)
            if top_k:
                take_q(0)
                take_k(0)

            def body(b, first, last):
                for g in range(G):
                    if top_k:
                        take_scores(b, g)
                    if top_k and g == 2 and not last:
                        take_q(b + 1)
                    if not top_k and g == 3 and not first:
                        take_oT(b - 1)
                    if g >= 2:
                        take_probsT(b, g - 2)
                    elif not first:
                        take_probsT(b - 1, g + 2)
                    if g == 1 and not last:
                        take_xT(b + 1)
                    if top_k and g == 2:
                        if not last:
                            take_k(b + 1)
                        if not first:
                            take_oT(b - 1)
                    exponentials(b, g)

            sequences(act, body)
            take_probsT(B - 1, 2)
            take_probsT(B - 1, 3)
            take_oT(B - 1)

        @block.vector
        def _(dve):
            def search(b, g):
                wait_apart(dve, scores_ready, b * G + g + 1, passed)
                wait(dve, exps_done, b * G + g - 1)
                wait_apart(dve, taken_ready, b * G + g - 1, passed)
                for step in range(2 * (TOP_K // 8)):
                    r = step // 2
                    source = s_sb if r == 0 else left
                    for pair in range(HG // PAIR):
                        if step:
                            wait_apart(dve, searched, (b * G + g) * CHAIN + (step - 1) * (HG // PAIR) + pair + 1, passed)
                        for i in range(pair * PAIR, (pair + 1) * PAIR):
                            if step % 2 == 0:
                                ins = nc.vector.max(top8[:, g % 2, i, r, :], source[:, g % 2, i, :])
                            else:
                                ins = nc.vector.match_replace(left[:, g % 2, i, :], top8[:, g % 2, i, r, :],
                                                              source[:, g % 2, i, :], TAKEN)
                        ins.then_inc(searched, 1)

            def mask_scores(b, g):
                dve.wait_ge(scores_raw, b * G + g + 1)
                wait(dve, probs_ready, b * G + g - 1)
                nc.vector.tensor_tensor(s_sb[:, g % 2], ps_s[g % 2][:S, 0:HG * S].rearrange("p (h s) -> p h s", h=HG),
                                        causal[:].unsqueeze(1).broadcast_to([S, HG, S]), ALU.add).then_inc(
                    scores_ready, 1)
                dve.wait_ge(scores_ready, b * G + g + 1)
                nc.vector.tensor_reduce(neg_max[:, g % 2, :], s_sb[:, g % 2], AX_X, ALU.max, negate=True).then_inc(
                    neg_ready, 1)

            def take_q(b):
                dve.wait_ge(q_raw, b + 1)
                wait(dve, q_head_ready, b * EC)
                nc.vector.tensor_tensor(qT[:], ps_b[:, 0:EC * S].rearrange("p (c s) -> p c s", c=EC),
                                        posT[:].unsqueeze(1).broadcast_to([P, EC, S]), ALU.add).then_inc(q_ready, 1)

            def take_k(b):
                dve.wait_ge(k_raw, b + 1)
                wait(dve, scores_raw, b * G)
                nc.vector.tensor_tensor(kT[:], ps_c[:, 0:EC * S].rearrange("p (c s) -> p c s", c=EC),
                                        posT[:].unsqueeze(1).broadcast_to([P, EC, S]), ALU.add).then_inc(k_ready, 1)

            def take_v(b):
                dve.wait_ge(v_raw, b + 1)
                wait(dve, av_done, b * G)
                v_ps = ps_a[:S, 0:E].rearrange("p (h d) -> p h d", h=H)
                if top_k:
                    nc.vector.tensor_tensor(v_one[:, :, 0:D], v_ps, b_v[:].rearrange("p (h d) -> p h d", h=H),
                                            ALU.add).then_inc(v_ready, 1)
                else:
                    nc.vector.tensor_copy(v_one[:, :, 0:D], v_ps).then_inc(v_ready, 1)

            def normalise(b):
                o_ps = ps_o[:S, 0:H * DV].rearrange("p (h d) -> p h d", h=H)
                dve.wait_ge(av_done, (b + 1) * G)
                nc.vector.reciprocal(rden[:], o_ps[:, :, D]).then_inc(rden_ready, 1)
                dve.wait_ge(rden_ready, b + 1)
                wait(dve, oT_raw, b)
                nc.vector.tensor_tensor(o_sb[:].rearrange("p (h d) -> p h d", h=H), o_ps[:, :, 0:D],
                                        rden[:].unsqueeze(2).broadcast_to([S, H, D]), ALU.mult).then_inc(o_ready, 1)

            def add_residual(b):
                dve.wait_ge(y_raw, b + 1)
                wait(dve, norm.x_ready, b)
                if top_k:
                    dve.wait_ge(x_bias_ready, b + 1)
                nc.vector.tensor_tensor(norm.z[:], ps_a[:S, 0:E], x_bias[:] if top_k else row_of(x, b), ALU.add).then_inc(
                    z_ready, 1)
                norm.take_stats(nc, dve, b, z_ready, b + 2, passed)

            dve.wait_ge(ones_ready, 1)
            dve.sem_inc(z_ready, 1)
            if top_k:
                def body(b, first, last):
                    search(b, 0)
                    search(b, 1)
                    if not first:
                        normalise(b - 1)
                    take_v(b)
                    search(b, 2)
                    if not first:
                        add_residual(b - 1)
                    search(b, 3)
                    if not first:
                        norm.apply(nc, dve, b - 1)
            else:
                def body(b, first, last):
                    mask_scores(b, 1)
                    mask_scores(b, 2)
                    if not last:
                        take_q(b + 1)
                    if not first:
                        normalise(b - 1)
                    take_v(b)
                    if not last:
                        take_k(b + 1)
                    mask_scores(b, 3)
                    if not first:
                        add_residual(b - 1)
                    if not last:
                        mask_scores(b + 1, 0)
                    if not first:
                        norm.apply(nc, dve, b - 1)

                take_q(0)
                take_k(0)
                mask_scores(0, 0)

            sequences(dve, body)
            normalise(B - 1)
            add_residual(B - 1)
            norm.apply(nc, dve, B - 1)

        @block.gpsimd
        def _(pool):
            def take_x(b):
                wait(pool, xT_raw, b)
                nc.gpsimd.tensor_copy(xs[:], row_of(x, b)).then_inc(xs_ready, 1)

            def spread_q(b):
                pool.wait_ge(q_ready, b + 1)
                for c in range(EC):
                    wait(pool, scores_raw, (b - 1) * G + (c + 1) * (G // EC))
                    nc.gpsimd.tensor_tensor(q_head[:, c], qT[:, c, :].unsqueeze(1).broadcast_to([P, HC, S]),
                                            head_mask[:].unsqueeze(2).broadcast_to([P, HC, S]), ALU.mult).then_inc(
                        q_head_ready, 1)

            def keep_taken(b, g):
                wait(pool, probs_ready, b * G + g)
                wait_apart(pool, searched, (b * G + g + 1) * CHAIN, passed)
                nc.gpsimd.tensor_scalar(taken[:], left[:, g % 2], TAKEN * 0.9, None, ALU.is_le).then_inc(taken_ready, 1)
                pool.wait_ge(taken_ready, b * G + g + 1)
                pool.wait_ge(exps_done, b * G + g + 1)
                wait(pool, probsT_raw, b * G + g - 1)
                nc.gpsimd.tensor_tensor(probs[:, g % 2], taken[:], exps[:, g % 2], ALU.mult).then_inc(probs_ready, 1)

            def add_bias(b):
                wait(pool, z_ready, b + 1)
                nc.gpsimd.tensor_tensor(x_bias[:], row_of(x, b), b_o[:], ALU.add).then_inc(x_bias_ready, 1)

            nc.gpsimd.memset(v_one[:], 1.0).then_inc(ones_ready, 1)
            take_x(0)
            spread_q(0)

            def body(b, first, last):
                if not last:
                    take_x(b + 1)
                if top_k:
                    if not first:
                        add_bias(b - 1)
                    keep_taken(b, 0)
                if not last:
                    spread_q(b + 1)
                if top_k:
                    keep_taken(b, 1)
                    keep_taken(b, 2)
                if not first:
                    norm.gpsimd(nc, pool, b - 1, passed)
                if top_k:
                    keep_taken(b, 3)

            sequences(pool, body)
            if top_k:
                add_bias(B - 1)
            norm.gpsimd(nc, pool, B - 1, passed)


def cross_attention_rope_weights(buf, wq, wk, wv, wo, rope, head_mask):
    w = {n: buf.sb(n, [P, EC, E]) for n in ("w_q", "w_k", "w_v", "w_o")}
    loads = [(w[n][:], a.rearrange("(c p) n -> p c n", p=P)) for n, a in zip(w, (wq, wk, wv, wo))]
    w.update(cos_sin=buf.sb("cos_sin", [P, 2, CTX]), head_mask=buf.sb("head_mask", [P, HC]))
    loads += [(w["cos_sin"][:], rope), (w["head_mask"][:], head_mask)]
    return w, loads


def cross_attention_rope(nc, shared, name, ctxT, weights):
    KC = CTX // 3
    NC = CTX // KC
    T_LAG, AV_LAG = 2, 3
    DV = D + 1
    x, ident = shared["x"], shared["ident"]
    with ExitStack() as ctx:
        buf = Buffers(nc, ctx, name, shared["semaphores"])
        w_q, w_k, w_v, w_o = (weights[n] for n in ("w_q", "w_k", "w_v", "w_o"))
        cos_sin, head_mask = weights["cos_sin"], weights["head_mask"]
        context = buf.sb("context", [P, EC, CTX])
        xs = buf.sb("xs", [S, E])
        xT = buf.sb("xT", [P, EC, S])
        q_plain, q_swap, q_cos, q_sin, qT = (buf.sb(n, [P, EC, S]) for n in ("q_plain", "q_swap", "q_cos", "q_sin", "qT"))
        k_plain, k_swap, k_cos, k_sin, kT = (
            buf.sb(n, [P, EC, CTX]) for n in ("k_plain", "k_swap", "k_cos", "k_sin", "kT"))
        q_head = buf.sb("q_head", [P, EC, HC, S])
        v_one = buf.sb("v_one", [KC, NC, H, DV])
        neg_max = buf.sb("neg_max", [S, 2])
        probs = buf.sb("probs", [S, 2, CTX])
        probsT = buf.sb("probsT", [KC, 2, NC, S])
        rden = buf.sb("rden", [S, H])
        o_sb = buf.sb("o_sb", [S, E])
        oT = buf.sb("oT", [P, EC, S])
        norm = Norm(buf, shared)
        ps_s = [buf.psum(f"ps_s{i}") for i in range(2)]
        ps_t = [buf.psum(f"ps_t{i}") for i in range(2)]
        ps_o = buf.psum("ps_o")
        ps_a, ps_b, ps_c = buf.psum("ps_a"), buf.psum("ps_b"), buf.psum("ps_c")

        ones_ready, passed, passed_sp = buf.sem("ones_ready"), buf.sem("passed"), buf.sem("passed_sp")
        context_loaded = buf.sem("context_loaded")
        xs_ready, xT_raw, xT_ready = buf.sem("xs_ready"), buf.sem("xT_raw"), buf.sem("xT_ready")
        q_raw, q_turned, q_ready, q_head_ready = (buf.sem(n) for n in ("q_raw", "q_turned", "q_ready", "q_head_ready"))
        q_taken, q_swapped = buf.sem("q_taken"), buf.sem("q_swapped")
        k_raw = [buf.sem(f"k_raw{m}") for m in range(EC)]
        k_taken = [buf.sem(f"k_taken{m}") for m in range(EC)]
        k_swapped = [buf.sem(f"k_swapped{m}") for m in range(EC)]
        k_turned = [buf.sem(f"k_turned{m}") for m in range(EC)]
        k_ready = [buf.sem(f"k_ready{m}") for m in range(EC)]
        v_raw, v_ready = buf.sem("v_raw"), buf.sem("v_ready")
        scores_raw, max_ready, probs_ready = buf.sem("scores_raw"), buf.sem("max_ready"), buf.sem("probs_ready")
        probsT_raw, probsT_ready, av_done = buf.sem("probsT_raw"), buf.sem("probsT_ready"), buf.sem("av_done")
        rden_ready, o_ready = buf.sem("rden_ready"), buf.sem("o_ready")
        oT_raw, oT_ready, y_raw, z_ready = (buf.sem(n) for n in ("oT_raw", "oT_ready", "y_raw", "z_ready"))

        context_of = ctxT.rearrange("(c p) b t -> p c b t", p=P)

        def back(b, h, lag):
            return (b, h - lag) if h >= lag else (b - 1, h - lag + H)

        block = ctx.enter_context(nc.Block())

        @block.sync
        def _(sp):
            def swap(source, to, ready, count, swapped):
                wait_apart(sp, ready, count, passed_sp)
                for odd in range(2):
                    sp.dma_start(to[odd:P:2], source[1 - odd:P:2]).then_inc(swapped, 16)

            def swap_all(b):
                swap(q_plain, q_swap, q_taken, b + 1, q_swapped)
                for m in range(EC):
                    swap(k_plain[:, m], k_swap[:, m], k_taken[m], b + 1, k_swapped[m])

            swap_all(0)

            def body(b, first, last):
                if not last:
                    swap_all(b + 1)

            sequences(sp, body)

        @block.tensor
        def _(pe):
            def project_xT(b):
                pe.wait_ge(xs_ready, b + 1)
                for c in range(EC):
                    last = nc.tensor.transpose(ps_c[:, c * S:(c + 1) * S], xs[:, c * P:(c + 1) * P], ident[:S, :S])
                last.then_inc(xT_raw, 1)

            def project_q(b):
                pe.wait_ge(xT_ready, b + 1)
                for m in range(EC):
                    for c in range(EC):
                        last = nc.tensor.matmul(ps_a[:, m * S:(m + 1) * S], w_q[:, c, m * P:(m + 1) * P], xT[:, c, :],
                                                start=(c == 0), stop=(c == EC - 1))
                last.then_inc(q_raw, 1)

            def project_k(b, m, out):
                pe.wait_ge(context_loaded, 16 * (b + 1))
                for c in range(EC):
                    last = nc.tensor.matmul(out[:, 0:CTX], w_k[:, c, m * P:(m + 1) * P], context[:, c, :],
                                            start=(c == 0), stop=(c == EC - 1))
                last.then_inc(k_raw[m], 1)

            def project_v(b):
                for t in range(NC):
                    out = (ps_a[:KC, 0:E], ps_a[:KC, E:2 * E], ps_b[:KC, 0:E])[t]
                    for c in range(EC):
                        last = nc.tensor.matmul(out, context[:, c, t * KC:(t + 1) * KC], w_v[:, c, :],
                                                start=(c == 0), stop=(c == EC - 1))
                last.then_inc(v_raw, 1)

            def scores(b, h):
                if h == 0:
                    pe.wait_ge(q_head_ready, EC * b + 1)
                    pe.wait_ge(k_ready[0], b + 1)
                if h == HC:
                    pe.wait_ge(q_head_ready, EC * b + 2)
                    pe.wait_ge(k_ready[1], b + 1)
                wait(pe, probs_ready, b * H + h - 1)
                nc.tensor.matmul(ps_s[h % 2][:S, 0:CTX], q_head[:, h // HC, h % HC, :], kT[:, h // HC, :],
                                 start=True, stop=True).then_inc(scores_raw, 1)

            def turn_probs(b, h):
                pe.wait_ge(probs_ready, b * H + h + 1)
                wait(pe, probsT_ready, b * H + h - 1)
                for t in range(NC):
                    last = nc.tensor.transpose(ps_t[h % 2][:KC, t * S:(t + 1) * S],
                                               probs[:, h % 2, t * KC:(t + 1) * KC], ident[:S, :S])
                last.then_inc(probsT_raw, 1)

            def weigh_values(b, h):
                pe.wait_ge(probsT_ready, b * H + h + 1)
                if h == 0:
                    pe.wait_ge(v_ready, b + 1)
                    wait(pe, o_ready, b)
                for t in range(NC):
                    last = nc.tensor.matmul(ps_o[:S, h * DV:(h + 1) * DV], probsT[:, h % 2, t, :], v_one[:, t, h, :],
                                            start=(t == 0), stop=(t == NC - 1))
                last.then_inc(av_done, 1)

            def turn_output(b):
                pe.wait_ge(o_ready, b + 1)
                for c in range(EC):
                    last = nc.tensor.transpose(ps_b[:, c * S:(c + 1) * S], o_sb[:, c * P:(c + 1) * P], ident[:S, :S])
                last.then_inc(oT_raw, 1)

            def project_out(b):
                pe.wait_ge(oT_ready, b + 1)
                for c in range(EC):
                    last = nc.tensor.matmul(ps_c[:S, 0:E], oT[:, c, :], w_o[:, c, :], start=(c == 0), stop=(c == EC - 1))
                last.then_inc(y_raw, 1)

            project_xT(0)
            project_q(0)
            pe.wait_ge(q_taken, 1)
            project_k(0, 0, ps_a)
            project_k(0, 1, ps_b)

            def body(b, first, last):
                for h in range(H):
                    scores(b, h)
                    if h >= T_LAG or not first:
                        turn_probs(*back(b, h, T_LAG))
                    if h >= AV_LAG or not first:
                        weigh_values(*back(b, h, AV_LAG))
                    if h == AV_LAG - 1:
                        for m in range(EC):
                            pe.wait_ge(k_taken[m], b + 1)
                        project_v(b)
                    if h == 3 and not last:
                        project_xT(b + 1)
                    if h == 4 and not last:
                        pe.wait_ge(v_ready, b + 1)
                        project_q(b + 1)
                    if h == 5 and not first:
                        pe.wait_ge(v_ready, b + 1)
                        turn_output(b - 1)
                    if h == 6 and not first:
                        if not last:
                            pe.wait_ge(xT_ready, b + 2)
                        project_out(b - 1)
                    if h == 8 and not last:
                        pe.wait_ge(q_taken, b + 2)
                        project_k(b + 1, 0, ps_a)
                    if h == 9 and not last:
                        wait(pe, oT_ready, b)
                        project_k(b + 1, 1, ps_b)

            sequences(pe, body)
            turn_probs(B - 1, H - 2)
            weigh_values(B - 1, H - 3)
            turn_probs(B - 1, H - 1)
            weigh_values(B - 1, H - 2)
            weigh_values(B - 1, H - 1)
            turn_output(B - 1)
            project_out(B - 1)

        @block.scalar
        def _(act):
            def take_xT(b):
                act.wait_ge(xT_raw, b + 1)
                nc.scalar.copy(xT[:], ps_c[:, 0:EC * S].rearrange("p (c s) -> p c s", c=EC)).then_inc(xT_ready, 1)

            def take_q(b):
                act.wait_ge(q_raw, b + 1)
                wait(act, q_turned, b)
                nc.scalar.copy(q_plain[:], ps_a[:, 0:EC * S].rearrange("p (c s) -> p c s", c=EC)).then_inc(q_taken, 1)

            def take_k(b, m):
                act.wait_ge(k_raw[m], b + 1)
                wait(act, k_turned[m], b)
                nc.scalar.copy(k_plain[:, m], (ps_a, ps_b)[m][:, 0:CTX]).then_inc(k_taken[m], 1)

            def take_v(b):
                act.wait_ge(v_raw, b + 1)
                nc.scalar.copy(v_one[:, 0:2, :, 0:D], ps_a[:KC, :].rearrange("p (t h d) -> p t h d", t=2, h=H))
                nc.scalar.copy(v_one[:, 2, :, 0:D], ps_b[:KC, 0:E].rearrange("p (h d) -> p h d", h=H)).then_inc(v_ready, 1)

            def exponentials(b, h):
                act.wait_ge(max_ready, b * H + h + 1)
                wait(act, probsT_raw, b * H + h - 1)
                nc.scalar.activation(probs[:, h % 2, :], ps_s[h % 2][:S, 0:CTX], ACT.Exp,
                                     bias=neg_max[:, h % 2:h % 2 + 1]).then_inc(probs_ready, 1)

            def take_oT(b):
                act.wait_ge(oT_raw, b + 1)
                nc.scalar.copy(oT[:], ps_b[:, 0:EC * S].rearrange("p (c s) -> p c s", c=EC)).then_inc(oT_ready, 1)

            act.wait_ge(ones_ready, 1)

            def load_context(b):
                act.dma_start(context[:], context_of[:, :, bass.ds(b, 1), :].rearrange("p c b t -> p c (b t)")).then_inc(
                    context_loaded, 16)

            load_context(0)
            take_xT(0)
            take_q(0)
            for m in range(EC):
                take_k(0, m)

            def body(b, first, last):
                for h in range(H):
                    exponentials(b, h)
                    if h == AV_LAG - 1:
                        take_v(b)
                        if not last:
                            load_context(b + 1)
                    if h == 3 and not last:
                        take_xT(b + 1)
                    if h == 4 and not last:
                        take_q(b + 1)
                    if h == 5 and not first:
                        take_oT(b - 1)
                    if h in (8, 9) and not last:
                        take_k(b + 1, h - 8)

            sequences(act, body)
            take_oT(B - 1)

        @block.vector
        def _(dve):
            def row_max(b, h):
                dve.wait_ge(scores_raw, b * H + h + 1)
                wait(dve, probs_ready, b * H + h - 1)
                nc.vector.tensor_reduce(neg_max[:, h % 2:h % 2 + 1], ps_s[h % 2][:S, 0:CTX], AX_X, ALU.max,
                                        negate=True).then_inc(max_ready, 1)

            def take_probsT(b, h):
                dve.wait_ge(probsT_raw, b * H + h + 1)
                wait(dve, av_done, b * H + h - 1)
                nc.vector.tensor_copy(probsT[:, h % 2], ps_t[h % 2][:KC, 0:NC * S].rearrange(
                    "p (t s) -> p t s", t=NC)).then_inc(probsT_ready, 1)

            def turn_q(b):
                dve.wait_ge(q_swapped, 32 * (b + 1))
                wait(dve, q_ready, b)
                for which, source, out in ((0, q_plain, q_cos), (1, q_swap, q_sin)):
                    last = nc.vector.tensor_tensor(out[:], source[:],
                                                   cos_sin[:, which, 0:S].unsqueeze(1).broadcast_to([P, EC, S]), ALU.mult)
                last.then_inc(q_turned, 1)

            def turn_k(b, m):
                dve.wait_ge(k_swapped[m], 32 * (b + 1))
                wait(dve, k_ready[m], b)
                nc.vector.tensor_tensor(k_cos[:, m], k_plain[:, m], cos_sin[:, 0, :], ALU.mult)
                nc.vector.tensor_tensor(k_sin[:, m], k_swap[:, m], cos_sin[:, 1, :], ALU.mult).then_inc(k_turned[m], 1)

            def normalise(b):
                o_ps = ps_o[:S, 0:H * DV].rearrange("p (h d) -> p h d", h=H)
                dve.wait_ge(av_done, (b + 1) * H)
                nc.vector.reciprocal(rden[:], o_ps[:, :, D]).then_inc(rden_ready, 1)
                dve.wait_ge(rden_ready, b + 1)
                wait(dve, oT_raw, b)
                nc.vector.tensor_tensor(o_sb[:].rearrange("p (h d) -> p h d", h=H), o_ps[:, :, 0:D],
                                        rden[:].unsqueeze(2).broadcast_to([S, H, D]), ALU.mult).then_inc(o_ready, 1)

            def add_residual(b):
                dve.wait_ge(y_raw, b + 1)
                wait(dve, norm.x_ready, b)
                nc.vector.tensor_tensor(norm.z[:], ps_c[:S, 0:E], row_of(x, b), ALU.add).then_inc(z_ready, 1)

            turn_q(0)
            for m in range(EC):
                turn_k(0, m)

            def body(b, first, last):
                for h in range(H):
                    row_max(b, h)
                    if h >= T_LAG or not first:
                        take_probsT(*back(b, h, T_LAG))
                    if h == AV_LAG - 1:
                        if not first:
                            normalise(b - 1)
                    if h == 7 and not first:
                        add_residual(b - 1)
                        norm.take_stats(nc, dve, b - 1, z_ready, b, passed)
                    if h == 10 and not first:
                        norm.apply(nc, dve, b - 1)
                    if h == 8 and not last:
                        turn_q(b + 1)
                    if h in (12, 13) and not last:
                        turn_k(b + 1, h - 12)

            sequences(dve, body)
            take_probsT(B - 1, H - 2)
            take_probsT(B - 1, H - 1)
            normalise(B - 1)
            add_residual(B - 1)
            norm.vector(nc, dve, B - 1, z_ready, B, passed)

        @block.gpsimd
        def _(pool):
            def take_x(b):
                wait(pool, xT_raw, b)
                nc.gpsimd.tensor_copy(xs[:], row_of(x, b)).then_inc(xs_ready, 1)

            def add_q(b):
                pool.wait_ge(q_turned, b + 1)
                wait(pool, q_head_ready, EC * b)
                nc.gpsimd.tensor_tensor(qT[:], q_cos[:], q_sin[:], ALU.add).then_inc(q_ready, 1)

            def spread_q(b, c):
                pool.wait_ge(q_ready, b + 1)
                wait(pool, scores_raw, (b - 1) * H + (c + 1) * HC)
                nc.gpsimd.tensor_tensor(q_head[:, c], qT[:, c, :].unsqueeze(1).broadcast_to([P, HC, S]),
                                        head_mask[:].unsqueeze(2).broadcast_to([P, HC, S]), ALU.mult).then_inc(
                    q_head_ready, 1)

            def add_k(b, m):
                pool.wait_ge(k_turned[m], b + 1)
                wait(pool, scores_raw, (b - 1) * H + (m + 1) * HC)
                nc.gpsimd.tensor_tensor(kT[:, m], k_cos[:, m], k_sin[:, m], ALU.add).then_inc(k_ready[m], 1)

            nc.gpsimd.memset(v_one[:], 1.0).then_inc(ones_ready, 1)
            take_x(0)
            add_q(0)
            spread_q(0, 0)
            add_k(0, 0)

            def body(b, first, last):
                if not last:
                    take_x(b + 1)
                spread_q(b, 1)
                add_k(b, 1)
                if not first:
                    norm.gpsimd(nc, pool, b - 1, passed)
                if not last:
                    add_q(b + 1)
                    spread_q(b + 1, 0)
                    add_k(b + 1, 0)

            sequences(pool, body)
            norm.gpsimd(nc, pool, B - 1, passed)


def ffn_quantised_weights(buf, w1T, conv_w, conv_b, w2T):
    w = {f"raw{i}": buf.sb(f"raw{i}", [P, EC * HID]) for i in range(2)}
    w.update(taps=buf.sb("taps", [P, FC, 3]), conv_bias=buf.sb("conv_bias", [P, FC]))
    loads = [(w["raw0"][:].rearrange("p (c n) -> p c n", c=EC), w1T.rearrange("(c p) n -> p c n", p=P)),
             (w["raw1"][:].rearrange("p (c n) -> p c n", c=FC), w2T.rearrange("(c p) n -> p c n", p=P)),
             (w["taps"][:], conv_w.rearrange("(c p) k -> p c k", p=P)), (w["conv_bias"][:], conv_b)]
    return w, loads


def ffn_quantised(nc, shared, name, weights):
    x, ident = shared["x"], shared["ident"]
    HALF = FC // 2
    with ExitStack() as ctx:
        buf = Buffers(nc, ctx, name, shared["semaphores"])
        raw = [weights[f"raw{i}"] for i in range(2)]
        w1 = buf.sb("w1", [P, EC, HID], BF16)
        w2 = buf.sb("w2", [P, FC, E], BF16)
        w_abs = buf.sb("w_abs", [P, EC * HID])
        taps, conv_bias = weights["taps"], weights["conv_bias"]
        ones, ident_bf = buf.sb("ones", [P, P]), buf.sb("ident_bf", [P, P], BF16)
        abs_sum, mean_abs, w_scale = (buf.sb(n, [P, 2]) for n in ("abs_sum", "mean_abs", "w_scale"))
        peak, peak_clip, inverse, scale, unscale = (buf.sb(n, [S, 2]) for n in (
            "peak", "peak_clip", "inverse", "scale", "unscale"))
        x_round, xq = buf.sb("x_round", [S, E]), buf.sb("xq", [S, E], BF16)
        xqT = buf.sb("xqT", [P, EC, S], BF16)
        unscale_diag, unscale_row = buf.sb("unscale_diag", [S, S]), buf.sb("unscale_row", [P, S])
        h = buf.sb("h", [P, FC, S + 2])
        tap_diag = buf.sb("tap_diag", [P, FC, 3, P])
        act_out = buf.sb("act_out", [P, FC, S])
        h_round, hq = buf.sb("h_round", [S, HID]), buf.sb("hq", [S, HID], BF16)
        hqT = buf.sb("hqT", [P, FC, S], BF16)
        norm = Norm(buf, shared)
        ps_xT, ps_row = buf.psum("ps_xT", BF16), buf.psum("ps_row")
        ps_h = [buf.psum(f"ps_h{i}") for i in range(2)]
        ps_u = ctx.enter_context(nc.psum_tensor(f"{name}_ps_u", [P, HID], F32))
        ps_hT, ps_y = buf.psum("ps_hT", BF16), buf.psum("ps_y")

        passed, passed_pool, zeroed = (buf.sem(n) for n in ("passed", "passed_pool", "zeroed"))
        scale_ready = [buf.sem(f"scale_ready{i}") for i in range(2)]
        abs_done, w_sum_done, w_prep = buf.sem("abs_done"), buf.sem("w_sum_done"), buf.sem("w_prep")
        prep_chain, peak_chain = buf.sem("prep_chain"), [buf.sem(f"peak_chain{i}") for i in range(2)]
        unscale_ready, diag_ready = buf.sem("unscale_ready"), buf.sem("diag_ready")
        x_rounded, xq_ready, xqT_raw, xqT_ready = (buf.sem(n) for n in ("x_rounded", "xq_ready", "xqT_raw", "xqT_ready"))
        row_raw, row_ready, h_raw, h_ready = (buf.sem(n) for n in ("row_raw", "row_ready", "h_raw", "h_ready"))
        tap_diag_ready, conv_raw, silu_done = (buf.sem(n) for n in ("tap_diag_ready", "conv_raw", "silu_done"))
        turned, h_rounded, hq_ready, hqT_raw, hqT_ready = (buf.sem(n) for n in (
            "turned", "h_rounded", "hq_ready", "hqT_raw", "hqT_ready"))
        y_raw, z_ready = buf.sem("y_raw"), buf.sem("z_ready")

        block = ctx.enter_context(nc.Block())

        @block.tensor
        def _(pe):
            def turn_x(b):
                pe.wait_ge(xq_ready, b + 1)
                wait(pe, xqT_ready, b)
                for c in range(EC):
                    last = nc.tensor.transpose(ps_xT[:, c * S:(c + 1) * S], xq[:, c * P:(c + 1) * P], ident_bf[:S, :S])
                last.then_inc(xqT_raw, 1)
                pe.wait_ge(diag_ready, b + 1)
                wait(pe, row_ready, b)
                nc.tensor.matmul(ps_row[:, 0:S], ones[:S, :], unscale_diag[:], start=True, stop=True).then_inc(row_raw, 1)

            def up(b):
                pe.wait_ge(xqT_ready, b + 1)
                wait(pe, silu_done, 2 * b)
                for m in range(FC):
                    for c in range(EC):
                        last = nc.tensor.matmul(ps_h[m // HALF][:, m % HALF * S:(m % HALF + 1) * S],
                                                w1[:, c, m * P:(m + 1) * P], xqT[:, c, :],
                                                start=(c == 0), stop=(c == EC - 1))
                    if m % HALF == HALF - 1:
                        last.then_inc(h_raw, 1)

            def convolve(b):
                for m in range(FC):
                    if m % HALF == 0:
                        pe.wait_ge(h_ready, 2 * b + m // HALF + 1)
                    for k in range(3):
                        last = nc.tensor.matmul(ps_h[m // HALF][:, m % HALF * S:(m % HALF + 1) * S], tap_diag[:, m, k, :],
                                                h[:, m, k:k + S], start=(k == 0), stop=(k == 2))
                    if m % HALF == HALF - 1:
                        last.then_inc(conv_raw, 1)

            def turn_hidden(b):
                wait(pe, h_rounded, b)
                for m in range(FC):
                    if m % HALF == 0:
                        pe.wait_ge(silu_done, 2 * b + m // HALF + 1)
                    last = nc.tensor.transpose(ps_u[:S, m * P:(m + 1) * P], act_out[:, m, :], ident[:])
                last.then_inc(turned, 1)

            def turn_quantised(b):
                pe.wait_ge(hq_ready, b + 1)
                wait(pe, hqT_ready, b)
                for m in range(FC):
                    last = nc.tensor.transpose(ps_hT[:, m * S:(m + 1) * S], hq[:, m * P:(m + 1) * P], ident_bf[:S, :S])
                last.then_inc(hqT_raw, 1)

            def down(b):
                pe.wait_ge(hqT_ready, b + 1)
                wait(pe, z_ready, b)
                for m in range(FC):
                    last = nc.tensor.matmul(ps_y[:S, 0:E], hqT[:, m, :], w2[:, m, :], start=(m == 0), stop=(m == FC - 1))
                last.then_inc(y_raw, 1)

            pe.wait_ge(zeroed, 4)
            pe.wait_ge(abs_done, 2)
            nc.tensor.matmul(ps_row[:, 0:2], ones[:], abs_sum[:], start=True, stop=True).then_inc(w_sum_done, 1)
            pe.wait_ge(w_prep, 2)
            turn_x(0)
            up(0)
            pe.wait_ge(tap_diag_ready, 1)
            convolve(0)
            turn_x(1)
            up(1)
            turn_hidden(0)

            def body(b, next, after):
                if next is not None:
                    convolve(next)
                if after is not None:
                    turn_x(after)
                turn_quantised(b)
                if after is not None:
                    up(after)
                down(b)
                if next is not None:
                    turn_hidden(next)

            staggered(pe, body)

        @block.scalar
        def _(act):
            def take_xT(b):
                act.wait_ge(xqT_raw, b + 1)
                wait(act, h_raw, 2 * b)
                nc.scalar.copy(xqT[:], ps_xT[:, 0:EC * S].rearrange("p (c s) -> p c s", c=EC)).then_inc(xqT_ready, 1)
                act.wait_ge(row_raw, b + 1)
                wait(act, h_ready, 2 * b)
                nc.scalar.copy(unscale_row[:], ps_row[:, 0:S]).then_inc(row_ready, 1)

            def silu(b):
                wait(act, turned, b)
                for m in range(FC):
                    if m % HALF == 0:
                        act.wait_ge(conv_raw, 2 * b + m // HALF + 1)
                    last = nc.scalar.activation(act_out[:, m, :], ps_h[m // HALF][:, m % HALF * S:(m % HALF + 1) * S],
                                                ACT.Silu, bias=conv_bias[:, m:m + 1])
                    if m % HALF == HALF - 1:
                        last.then_inc(silu_done, 1)

            def take_hqT(b):
                act.wait_ge(hqT_raw, b + 1)
                wait(act, y_raw, b)
                nc.scalar.copy(hqT[:], ps_hT[:, 0:FC * S].rearrange("p (c s) -> p c s", c=FC)).then_inc(hqT_ready, 1)

            for i in range(2):
                wait(act, abs_done, i)
                nc.scalar.activation(w_abs[:], raw[i][:], ACT.Abs, accum_out=abs_sum[:, i:i + 1]).then_inc(abs_done, 1)
            for m in range(FC):
                for k in range(3):
                    last = nc.scalar.activation(tap_diag[:, m, k, :], ident[:], ACT.Identity, scale=taps[:, m, k:k + 1])
            last.then_inc(tap_diag_ready, 1)
            take_xT(0)
            silu(0)
            take_xT(1)

            def body(b, next, after):
                if next is not None:
                    silu(next)
                if after is not None:
                    take_xT(after)
                take_hqT(b)

            staggered(act, body)

        @block.vector
        def _(dve):
            def scales(b, i):
                n = (2, 3)[i] * b
                wait_apart(dve, peak_chain[i], n + 1, passed)
                nc.vector.tensor_scalar(peak_clip[:, i:i + 1], peak[:, i:i + 1], 1e-5, None, ALU.max).then_inc(
                    peak_chain[i], 1)
                wait_apart(dve, peak_chain[i], n + 2, passed)
                nc.vector.reciprocal(inverse[:, i:i + 1], peak_clip[:, i:i + 1])
                nc.vector.tensor_scalar(unscale[:, i:i + 1], peak_clip[:, i:i + 1], 1.0 / 127.0, mean_abs[:S, i:i + 1],
                                        ALU.mult, ALU.mult).then_inc(unscale_ready if i == 0 else peak_chain[i], 1)
                if i == 0:
                    wait_apart(dve, unscale_ready, b + 1, passed)
                else:
                    wait_apart(dve, peak_chain[i], n + 3, passed)
                nc.vector.tensor_scalar(scale[:, i:i + 1], inverse[:, i:i + 1], 127.0, None, ALU.mult).then_inc(
                    scale_ready[i], 1)
                dve.wait_ge(scale_ready[i], b + 1)

            def quantise_x(b):
                wait(dve, diag_ready, b)
                nc.vector.tensor_reduce(peak[:, 0:1], row_of(x, b), AX_X, ALU.max, apply_absolute_value=True).then_inc(
                    peak_chain[0], 1)
                scales(b, 0)
                nc.vector.tensor_scalar(x_round[:], row_of(x, b), scale[:, 0:1], ROUND, ALU.mult, ALU.add).then_inc(
                    x_rounded, 1)
                dve.wait_ge(x_rounded, b + 1)
                wait(dve, xqT_raw, b)
                nc.vector.tensor_scalar(xq[:], x_round[:], ROUND, 127.0, ALU.subtract, ALU.min).then_inc(xq_ready, 1)

            def scale_hidden(b):
                wait(dve, conv_raw, 2 * b)
                dve.wait_ge(row_ready, b + 1)
                for i in range(2):
                    dve.wait_ge(h_raw, 2 * b + i + 1)
                    nc.vector.tensor_tensor(h[:, i * HALF:(i + 1) * HALF, 1:S + 1],
                                            ps_h[i][:, 0:HALF * S].rearrange("p (c s) -> p c s", c=HALF),
                                            unscale_row[:].unsqueeze(1).broadcast_to([P, HALF, S]), ALU.mult).then_inc(
                        h_ready, 1)

            def quantise_hidden(b):
                dve.wait_ge(turned, b + 1)
                nc.vector.tensor_reduce(peak[:, 1:2], ps_u[:S, :], AX_X, ALU.max, apply_absolute_value=True).then_inc(
                    peak_chain[1], 1)
                scales(b, 1)
                nc.vector.tensor_scalar(h_round[:], ps_u[:S, :], scale[:, 1:2], ROUND, ALU.mult, ALU.add).then_inc(
                    h_rounded, 1)
                dve.wait_ge(h_rounded, b + 1)
                wait(dve, hqT_raw, b)
                nc.vector.tensor_scalar(hq[:], h_round[:], ROUND, 127.0, ALU.subtract, ALU.min).then_inc(hq_ready, 1)

            def add_residual(b):
                dve.wait_ge(y_raw, b + 1)
                dve.wait_ge(norm.x_ready, b + 1)
                nc.vector.scalar_tensor_tensor(norm.z[:], ps_y[:S, 0:E], unscale[:, 1:2], row_of(x, b), ALU.mult,
                                               ALU.add).then_inc(z_ready, 1)
                norm.take_stats(nc, dve, b, z_ready, b + 1, passed)

            dve.wait_ge(w_sum_done, 1)
            dve.wait_ge(zeroed, 4)
            nc.vector.tensor_scalar(mean_abs[:], ps_row[:, 0:2], 1.0 / (E * HID), 1e-5, ALU.mult, ALU.max).then_inc(
                prep_chain, 1)
            dve.wait_ge(prep_chain, 1)
            nc.vector.reciprocal(w_scale[:], mean_abs[:]).then_inc(prep_chain, 1)
            dve.wait_ge(prep_chain, 2)
            for i, w in enumerate((w1, w2)):
                nc.vector.tensor_scalar(raw[i][:], raw[i][:], w_scale[:, i:i + 1], ROUND, ALU.mult, ALU.add).then_inc(
                    prep_chain, 1)
                dve.wait_ge(prep_chain, 3 + 2 * i)
                nc.vector.tensor_scalar(raw[i][:], raw[i][:], ROUND, 1.0, ALU.subtract, ALU.min).then_inc(prep_chain, 1)
                dve.wait_ge(prep_chain, 4 + 2 * i)
                nc.vector.tensor_scalar(w[:].rearrange("p c n -> p (c n)"), raw[i][:], -1.0, None, ALU.max).then_inc(
                    w_prep, 1)
            quantise_x(0)
            scale_hidden(0)
            quantise_x(1)
            dve.sem_inc(norm.x_ready, 1)

            def body(b, next, after):
                started = not (isinstance(b, int) and b == 0)
                if next is not None:
                    scale_hidden(next)
                if started:
                    add_residual(b - 1)
                if after is not None:
                    quantise_x(after)
                quantise_hidden(b)
                if started:
                    norm.apply(nc, dve, b - 1)

            staggered(dve, body)
            add_residual(B - 1)
            norm.apply(nc, dve, B - 1)

        @block.gpsimd
        def _(pool):
            def scale_diagonal(b):
                wait(pool, row_raw, b)
                wait_apart(pool, unscale_ready, b + 1, passed_pool)
                nc.gpsimd.tensor_scalar(unscale_diag[:], ident[:S, :S], unscale[:, 0:1], None, ALU.mult).then_inc(
                    diag_ready, 1)

            nc.gpsimd.memset(ones[:], 1.0).then_inc(zeroed, 1)
            nc.gpsimd.tensor_copy(ident_bf[:], ident[:]).then_inc(zeroed, 1)
            for at in (0, S + 1):
                nc.gpsimd.memset(h[:, :, at:at + 1], 0.0).then_inc(zeroed, 1)
            scale_diagonal(0)
            scale_diagonal(1)

            def body(b, next, after):
                if not (isinstance(b, int) and b == 0):
                    norm.gpsimd(nc, pool, b - 1, passed_pool)
                if after is not None:
                    scale_diagonal(after)

            staggered(pool, body)
            norm.gpsimd(nc, pool, B - 1, passed_pool)


def cross_attention_relative_weights(buf, a):
    DH, W = 64, "L1_xattn_"
    w, loads = {}, []
    names = {"w_q": "Wq", "w_k": "Wk", "w_k_image": "Wk_ip", "w_k_audio": "Wk_ap", "w_v": "Wv", "w_v_image": "Wv_ip",
             "w_v_audio": "Wv_ap"}
    for n, source in names.items():
        w[n] = buf.sb(n, [P, EC, H * DH])
        loads.append((w[n][:], a[W + source].rearrange("(c p) n -> p c n", p=P)))
    w.update(w_o=buf.sb("w_o", [P, H // 2, E]), b_o=buf.sb("b_o", [S, E]),
             gain=buf.sb("gain", [S, 3]),
             rel_k=buf.sb("rel_k", [P, S - 1 + TEXT]))
    loads += [(w["w_o"][:], a[W + "Wo"].rearrange("(c p) n -> p c n", p=P)),
              (w["b_o"][:], a[W + "bo"].rearrange("(a n) -> a n", a=1).partition_broadcast(S)),
              (w["gain"][:, 1:2], a[W + "beta"].partition_broadcast(S)),
              (w["gain"][:, 2:3], a[W + "alpha"].partition_broadcast(S)),
              (w["rel_k"][0:DH, S - 17:S + 16], a[W + "rel_k"]), (w["rel_k"][DH:P, S - 17:S + 16], a[W + "rel_k"])]
    return w, loads


def cross_attention_relative(nc, shared, name, a, weights):
    K4 = 4
    NG = B // K4
    DH = 64
    NP = H // 2
    HH = H // 2
    REST = AUD - 2 * P
    IMG_ROW = P // 2
    IMG_AT = TEXT + 2 * P + IMG_ROW
    PW = TEXT + 3 * P
    WIDE = S - 1 + TEXT
    T_LAG, AV_LAG = 3, 4
    RING = 4
    QI = 512 // (K4 * H)
    VI = 8
    NV = S // VI
    VSLOTS = 8
    x, ident = shared["x"], shared["ident"]
    with ExitStack() as ctx:
        buf = Buffers(nc, ctx, name, shared["semaphores"])
        w_q, w_o, b_o, gain, rel_k = (weights[n] for n in ("w_q", "w_o", "b_o", "gain", "rel_k"))
        w_k = [weights[n] for n in ("w_k", "w_k_image", "w_k_audio")]
        w_v = [weights[n] for n in ("w_v", "w_v_image", "w_v_audio")]
        context_image = buf.sb("context_image", [P, EC, K4, IMG])
        k_image = buf.sb("k_image", [P, NP, K4 * IMG])
        rel_v = buf.sb("rel_v", [TEXT, 2, VI, DH])
        context = buf.sb("context", [P, 2, EC, CTX])
        xs = buf.sb("xs", [S, E])
        xT = buf.sb("xT", [P, EC, S])
        q_head = buf.sb("q_head", [P, K4, H, S])
        turned = buf.sb("turned", [TEXT, K4, H, S])
        outT = buf.sb("outT", [P, K4, NP, S])
        kT = buf.sb("kT", [P, NP, CTX])
        v = buf.sb("v", [P, 4, H * DH])
        neg_max, total, inverse = (buf.sb(n, [S, RING, 3]) for n in ("neg_max", "total", "inverse"))
        probs = buf.sb("probs", [S, RING, PW])
        audT = buf.sb("audT", [P, 2, 3, S])
        norm = Norm(buf, shared)
        x_bias = buf.sb("x_bias", [S, E])
        ps_s = [buf.psum(f"ps_s{i}") for i in range(2)]
        ps_t = [buf.psum(f"ps_t{i}") for i in range(2)]
        ps_o = [buf.psum(f"ps_o{i}") for i in range(2)]
        ps_p = [buf.psum(f"ps_p{i}") for i in range(2)]

        passed, passed_pool, passed_sp = (buf.sem(n) for n in ("passed", "passed_pool", "passed_sp"))
        zeroed, gain_ready, rel_k_ready, tanh_done = (buf.sem(n) for n in ("zeroed", "gain_ready", "rel_k_ready", "tanh_done"))
        image_loaded, k_image_placed = buf.sem("image_loaded"), buf.sem("k_image_placed")
        context_loaded = [buf.sem(f"context_loaded{i}") for i in range(2)]
        rel_v_loaded = [buf.sem(f"rel_v_loaded{i}") for i in range(VSLOTS)]
        raw = [buf.sem(f"raw{i}") for i in range(2)]
        taken = [buf.sem(f"taken{i}") for i in range(2)]
        xs_ready = buf.sem("xs_ready")
        rel_raw, rel_taken = [buf.sem(f"rel_raw{i}") for i in range(2)], [buf.sem(f"rel_taken{i}") for i in range(2)]
        scores_raw, max_ready, exps_done, inverse_ready = (buf.sem(n) for n in (
            "scores_raw", "max_ready", "exps_done", "inverse_ready"))
        probs_ready, probsT_raw, probsT_ready, av_done = (buf.sem(n) for n in (
            "probs_ready", "probsT_raw", "probsT_ready", "av_done"))
        out_taken = [buf.sem(f"out_taken{i}") for i in range(2)]
        rel_v_raw, rel_v_added = buf.sem("rel_v_raw"), buf.sem("rel_v_added")
        y_raw, z_ready, x_bias_ready = buf.sem("y_raw"), buf.sem("z_ready"), buf.sem("x_bias_ready")

        def use_x(k):
            return 3 * k

        def use_q(k, j):
            return 3 * k + 1 + j

        def use_image(j):
            return 3 * K4 + j

        def use_k(k, m):
            return 3 * K4 + 4 + 16 * k + m

        def use_v(k, j):
            return use_k(k, 8 + j)

        USES = use_k(K4, 0) // 2

        def bank_count(g, u):
            return u % 2, USES * g + u // 2

        def head_count(g, k, h):
            return (g * K4 + k) * H + h + 1

        columns = ((0, TEXT), (TEXT, TEXT + AUD), (TEXT + AUD, CTX))

        def places(k):
            return (columns[0], columns[1], (IMG_AT + k * IMG, IMG_AT + (k + 1) * IMG))

        def value_rows(t):
            return ((0, TEXT), (TEXT + IMG, P), (TEXT + IMG + P, P), (TEXT + IMG + 2 * P, REST))[t]

        context_of = a["ctxT"].rearrange("(c p) b t -> p c b t", p=P)
        wide = a["rel_v_wide"]

        def rel_v_piece(n):
            slot = n % VSLOTS
            if slot < 2:
                return rel_v[:, slot].rearrange("p i d -> p (i d)")
            return v[:TEXT, slot // 2 - 1, slot % 2 * VI * DH:(slot % 2 + 1) * VI * DH]

        def groups(engine, body):
            body(0, False)
            with engine.Fori(1, NG - 1) as g:
                body(g, False)
            body(NG - 1, True)

        block = ctx.enter_context(nc.Block())

        @block.sync
        def _(sp):
            def load_image(g):
                if not isinstance(g, int) or g > 0:
                    i, n = bank_count(g - 1, use_image(3))
                    wait_apart(sp, raw[i], n + 1, passed_sp)
                for c in range(EC):
                    sp.dma_start(context_image[:, c], context_of[:, c, bass.ds(g * K4, K4), TEXT:TEXT + IMG]).then_inc(
                        image_loaded, 16)

            def load_context(g, k):
                if k >= 2 or not isinstance(g, int):
                    i, n = bank_count(g, use_v(k - 2, 7)) if k >= 2 else bank_count(g - 1, use_v(k + 2, 7))
                    wait_apart(sp, raw[i], n + 1, passed_sp)
                sp.dma_start(context[:, k % 2], context_of[:, :, bass.ds(g * K4 + k, 1), :].rearrange(
                    "p c b t -> p c (b t)")).then_inc(context_loaded[k % 2], 16)

            def load_rel_v(g, n):
                slot = n % VSLOTS
                if n >= VSLOTS:
                    wait_apart(sp, rel_v_raw, g * NV + n - VSLOTS + 1, passed_sp)
                elif slot >= 2:
                    wait_apart(sp, av_done, head_count(g, K4 - 1, H - 1), passed_sp)
                elif not isinstance(g, int) or g > 0:
                    wait_apart(sp, rel_v_raw, g * NV, passed_sp)
                source = bass.AP(tensor=wide.tensor, offset=n * VI * DH, ap=[[DH, TEXT], [1, VI * DH]])
                sp.dma_start(rel_v_piece(n), source).then_inc(rel_v_loaded[slot], 16)

            def body(g, last):
                load_image(g)
                for k in range(K4):
                    load_context(g, k)
                for n in range(NV):
                    load_rel_v(g, n)

            groups(sp, body)

        @block.tensor
        def _(pe):
            def free_bank(g, u):
                i, n = bank_count(g, u)
                wait(pe, taken[i], n)
                return i

            def project_x(g, k):
                pe.wait_ge(xs_ready, g * K4 + k + 1)
                i = free_bank(g, use_x(k))
                for c in range(EC):
                    last = nc.tensor.transpose(ps_p[i][:, c * S:(c + 1) * S], xs[:, c * P:(c + 1) * P], ident[:S, :S])
                last.then_inc(raw[i], 1)

            def project_q(g, k, j):
                if j == 0:
                    xi, xn = bank_count(g, use_x(k))
                    pe.wait_ge(taken[xi], xn + 1)
                i = free_bank(g, use_q(k, j))
                for m in range(4):
                    for c in range(EC):
                        at = (4 * j + m) * P
                        last = nc.tensor.matmul(ps_p[i][:, m * S:(m + 1) * S], w_q[:, c, at:at + P], xT[:, c, :],
                                                start=(c == 0), stop=(c == EC - 1))
                last.then_inc(raw[i], 1)

            def relative_keys(g):
                for n in range(S // QI):
                    if n == 0:
                        pe.wait_ge(rel_k_ready, 1)
                        pe.wait_ge(zeroed, 4)
                        for i in range(2):
                            u = use_image(0) - 2 + i
                            pe.wait_ge(taken[u % 2], bank_count(g, u)[1] + 1)
                        wait(pe, exps_done, head_count(g, 0, -1))
                    wait(pe, rel_taken[n % 2], g * (S // QI // 2) + n // 2)
                    for j in range(QI):
                        i = n * QI + j
                        last = nc.tensor.matmul(ps_s[n % 2][:TEXT, j * K4 * H:(j + 1) * K4 * H],
                                                rel_k[:, S - 1 - i:S - 1 - i + TEXT],
                                                q_head[:, :, :, i].rearrange("p k h -> p (k h)"), start=True, stop=True)
                    last.then_inc(rel_raw[n % 2], 1)

            def project_image(g, j):
                i = free_bank(g, use_image(j))
                pe.wait_ge(image_loaded, 16 * EC * (g + 1))
                image = [context_image[:, c].rearrange("p k t -> p (k t)") for c in range(EC)]
                if j < 2:
                    for m in range(4):
                        at = (4 * j + m) * P
                        for c in range(EC):
                            last = nc.tensor.matmul(ps_p[i][:, m * K4 * IMG:(m + 1) * K4 * IMG], w_k[1][:, c, at:at + P],
                                                    image[c], start=(c == 0), stop=(c == EC - 1))
                else:
                    half = slice((j - 2) * 512, (j - 1) * 512)
                    for c in range(EC):
                        last = nc.tensor.matmul(ps_p[i][IMG_ROW:P, :], image[c], w_v[1][:, c, half], start=(c == 0),
                                                stop=(c == EC - 1), tile_position=(0, IMG_ROW))
                last.then_inc(raw[i], 1)

            def project_k(g, k, m):
                i = free_bank(g, use_k(k, m))
                if m == 0:
                    pe.wait_ge(context_loaded[k % 2], 16 * (g * (K4 // 2) + k // 2 + 1))
                for w, (lo, hi), token in ((w_k[0], columns[0], 0), (w_k[2], columns[1], TEXT + IMG)):
                    for c in range(EC):
                        last = nc.tensor.matmul(ps_p[i][:, lo:hi], w[:, c, m * P:(m + 1) * P],
                                                context[:, k % 2, c, token:token + hi - lo], start=(c == 0),
                                                stop=(c == EC - 1))
                last.then_inc(raw[i], 1)

            def project_v(g, k, j):
                t, half = j // 2, slice(j % 2 * 512, j % 2 * 512 + 512)
                i = free_bank(g, use_v(k, j))
                token, rows = value_rows(t)
                w = w_v[0] if t == 0 else w_v[2]
                for c in range(EC):
                    last = nc.tensor.matmul(ps_p[i][:rows, :], context[:, k % 2, c, token:token + rows], w[:, c, half],
                                            start=(c == 0), stop=(c == EC - 1))
                last.then_inc(raw[i], 1)

            def scores(g, k, h):
                n = head_count(g, k, h)
                if h == 0:
                    u = use_v(k, 0) - 2
                    for i in range(2):
                        pe.wait_ge(taken[(u + i) % 2], bank_count(g, u + i)[1] + 1)
                    pe.wait_ge(k_image_placed, g * K4 + k + 1)
                    if k == 0:
                        for i in range(2):
                            pe.wait_ge(rel_taken[i], (g + 1) * (S // QI // 2))
                wait(pe, exps_done, n - 2)
                out = ps_s[h % 2]
                nc.tensor.matmul(out[:S, 0:CTX], q_head[:, k, h, :], kT[:, h // 2, :], start=True, stop=False)
                nc.tensor.matmul(out[:S, 0:TEXT], turned[:TEXT, k, h, :], ident[:TEXT, :TEXT], start=False,
                                 stop=True).then_inc(scores_raw, 1)

            def turn_probs(g, k, h):
                n = head_count(g, k, h)
                pe.wait_ge(probs_ready, n)
                wait(pe, probsT_ready, n - 2)
                if k == 0 and h < 2:
                    wait(pe, rel_v_added, g * NV)
                out, slot = ps_t[h % 2], h % RING
                nc.tensor.transpose(out[:TEXT, 0:S], probs[:, slot, 0:TEXT], ident[:S, :S])
                for t in range(3):
                    at = TEXT + t * P
                    last = nc.tensor.transpose(out[:, (t + 1) * S:(t + 2) * S], probs[:, slot, at:at + P], ident[:S, :S])
                last.then_inc(probsT_raw, 1)

            def weigh_values(g, k, h):
                pe.wait_ge(probsT_ready, head_count(g, k, h))
                if h % HH == 0:
                    wait(pe, out_taken[h // HH], g * K4 + k)
                    if k == 0:
                        wait(pe, z_ready, g * K4)
                if h == 0:
                    for i in range(2):
                        u = use_v(k, 6 + i)
                        pe.wait_ge(taken[u % 2], bank_count(g, u)[1] + 1)
                row, at = h % 2 * DH, h % HH // 2 * S
                out = ps_o[h // HH][row:row + DH, at:at + S]
                feat = slice(h * DH, (h + 1) * DH)
                nc.tensor.matmul(out, v[:TEXT, 0, feat], turned[:TEXT, k, h, :], start=True, stop=False,
                                 tile_position=(0, row), skip_group_check=True)
                for t in range(3):
                    last = nc.tensor.matmul(out, v[:, t + 1, feat], audT[:, h % 2, t, :], start=False, stop=(t == 2),
                                            tile_position=(0, row), skip_group_check=True)
                last.then_inc(av_done, 1)

            def relative_values(g):
                for n in range(NV):
                    slot, used = n % VSLOTS, n // VSLOTS
                    a_group = (NV - 1 - slot) // VSLOTS + 1
                    pe.wait_ge(rel_v_loaded[slot], 16 * (g * a_group + used + 1))
                    wait(pe, rel_v_added, g * NV + n - 1)
                    for j in range(VI):
                        i, at = S - 1 - (n * VI + j), (VI - 1 - j) * K4 * H
                        last = nc.tensor.matmul(ps_t[n % 2][:DH, at:at + K4 * H], rel_v_piece(n)[:, j * DH:(j + 1) * DH],
                                                turned[:TEXT, :, :, i].rearrange("p k h -> p (k h)"),
                                                start=True, stop=True)
                    last.then_inc(rel_v_raw, 1)

            def project_out(g, k):
                if k == 0:
                    pe.wait_ge(rel_v_added, (g + 1) * NV)
                if k >= 2:
                    pe.wait_ge(z_ready, g * K4 + k - 1)
                for m in range(NP):
                    last = nc.tensor.matmul(ps_o[k % 2][:S, 0:E], outT[:, k, m, :], w_o[:, m, :], start=(m == 0),
                                            stop=(m == NP - 1))
                last.then_inc(y_raw, 1)


            for k in range(K4):
                project_x(0, k)
                project_q(0, k, 0)
                project_q(0, k, 1)

            def body(g, last):
                relative_keys(g)
                for j in range(4):
                    project_image(g, j)
                for m in range(NP):
                    project_k(g, 0, m)
                for k in range(K4):
                    for j in range(8):
                        project_v(g, k, j)
                    for h in range(H + AV_LAG):
                        if h < H:
                            scores(g, k, h)
                        if T_LAG <= h < H + T_LAG:
                            turn_probs(g, k, h - T_LAG)
                        if AV_LAG <= h:
                            weigh_values(g, k, h - AV_LAG)
                        if h >= H and k < K4 - 1:
                            project_k(g, k + 1, 2 * (h - H))
                            project_k(g, k + 1, 2 * (h - H) + 1)
                if not last:
                    project_x(g + 1, 0)
                relative_values(g)
                for k in range(K4):
                    if not last:
                        project_q(g + 1, k, 0)
                        project_q(g + 1, k, 1)
                        if k < K4 - 1:
                            project_x(g + 1, k + 1)
                    project_out(g, k)

            groups(pe, body)

        @block.scalar
        def _(act):
            def arrived(g, u):
                act.wait_ge(raw[0], bank_count(g, u)[1] + 1)

            def take_x(g, k):
                arrived(g, use_x(k))
                nc.scalar.copy(xT[:], ps_p[0][:, 0:EC * S].rearrange("p (c s) -> p c s", c=EC)).then_inc(taken[0], 1)

            def take_q(g, k, j):
                arrived(g, use_q(k, j))
                if k == 0:
                    wait(act, scores_raw, head_count(g, 0, -1))
                for odd in range(2):
                    rows = slice(odd * DH, odd * DH + DH)
                    last = nc.scalar.mul(q_head[rows, k, 8 * j + odd:8 * j + 8:2, :],
                                         ps_p[0][rows, 0:4 * S].rearrange("p (m s) -> p m s", m=4), DH ** -0.5)
                last.then_inc(taken[0], 1)

            def take_rel(g, n):
                act.wait_ge(rel_raw[0], g * (S // QI // 2) + n // 2 + 1)
                wait(act, rel_v_raw, g * NV)
                nc.scalar.copy(turned[:TEXT, :, :, n * QI:(n + 1) * QI].rearrange("p k h i -> p (k h) i"),
                               ps_s[0][:TEXT, :].rearrange("p (i n) -> p n i", i=QI)).then_inc(rel_taken[0], 1)

            def take_k(g, k, m):
                arrived(g, use_k(k, m))
                wait(act, scores_raw, head_count(g, k, -1))
                nc.scalar.copy(kT[:, m, 0:TEXT + AUD], ps_p[0][:, 0:TEXT + AUD]).then_inc(taken[0], 1)

            def take_image(g, j):
                arrived(g, use_image(j))
                if j < 2:
                    nc.scalar.copy(k_image[:, 4 * j:4 * j + 4].rearrange("p m t -> p (m t)"), ps_p[0][:, 0:4 * K4 * IMG]).then_inc(
                        taken[0], 1)
                else:
                    half = slice((j - 2) * 512, (j - 1) * 512)
                    wait(act, av_done, head_count(g, 0, -1))
                    nc.scalar.copy(v[IMG_ROW:P, 3, half], ps_p[0][IMG_ROW:P, :]).then_inc(taken[0], 1)

            def take_v(g, k, j):
                t, half = j // 2, slice(j % 2 * 512, j % 2 * 512 + 512)
                arrived(g, use_v(k, j))
                wait(act, av_done, head_count(g, k, -1))
                rows = value_rows(t)[1]
                nc.scalar.copy(v[:rows, t, half], ps_p[0][:rows, :]).then_inc(taken[0], 1)

            def exponentials(g, k, h):
                n = head_count(g, k, h)
                act.wait_ge(max_ready, n)
                wait(act, probsT_raw, n - RING)
                wait(act, inverse_ready, n - RING)
                slot = h % RING
                for j in range(3):
                    lo, hi = columns[j]
                    to, end = places(k)[j]
                    last = nc.scalar.activation(probs[:, slot, to:end], ps_s[h % 2][:S, lo:hi], ACT.Exp,
                                                bias=neg_max[:, slot, j:j + 1], accum_out=total[:, slot, j:j + 1])
                last.then_inc(exps_done, 1)

            def place_image(g, k):
                if k == 0:
                    for j in range(2):
                        i, n = bank_count(g, use_image(j))
                        act.wait_ge(taken[i], n + 1)
                wait(act, scores_raw, head_count(g, k, -1))
                nc.scalar.copy(kT[:, :, TEXT + AUD:CTX], k_image[:, :, k * IMG:(k + 1) * IMG]).then_inc(k_image_placed, 1)

            def take_out(g, k, half):
                act.wait_ge(av_done, head_count(g, k, (half + 1) * HH - 1))
                if k == 0:
                    wait(act, y_raw, g * K4)
                nc.scalar.copy(outT[:, k, half * 4:half * 4 + 4, :],
                               ps_o[half][:, 0:4 * S].rearrange("p (m s) -> p m s", m=4)).then_inc(out_taken[half], 1)

            nc.scalar.activation(gain[:, 1:3], gain[:, 1:3], ACT.Tanh).then_inc(tanh_done, 1)
            act.wait_ge(zeroed, 4)

            def mine(u):
                return u % 2 == 0

            def take_xq(g, k):
                if mine(use_x(k)):
                    take_x(g, k)
                for j in range(2):
                    if mine(use_q(k, j)):
                        take_q(g, k, j)

            for k in range(K4):
                take_xq(0, k)

            def body(g, last):
                for n in range(0, S // QI, 2):
                    take_rel(g, n)
                for j in range(0, 4, 2):
                    take_image(g, j)
                place_image(g, 0)
                for m in range(0, NP, 2):
                    take_k(g, 0, m)
                for k in range(K4):
                    for j in range(0, 8, 2):
                        take_v(g, k, j)
                    for h in range(H + AV_LAG):
                        if h < H:
                            exponentials(g, k, h)
                        if h == HH + AV_LAG:
                            take_out(g, k, 0)
                        if h == H and k < K4 - 1:
                            place_image(g, k + 1)
                        if h >= H and k < K4 - 1:
                            take_k(g, k + 1, 2 * (h - H))
                    take_out(g, k, 1)
                if not last:
                    for k in range(K4):
                        take_xq(g + 1, k)

            groups(act, body)

        @block.vector
        def _(dve):
            def arrived(g, u):
                dve.wait_ge(raw[1], bank_count(g, u)[1] + 1)

            def take_x(g, k):
                arrived(g, use_x(k))
                nc.vector.tensor_copy(xT[:], ps_p[1][:, 0:EC * S].rearrange("p (c s) -> p c s", c=EC)).then_inc(taken[1], 1)

            def take_q(g, k, j):
                arrived(g, use_q(k, j))
                if k == 0:
                    wait(dve, scores_raw, head_count(g, 0, -1))
                for odd in range(2):
                    rows = slice(odd * DH, odd * DH + DH)
                    last = nc.vector.tensor_scalar(q_head[rows, k, 8 * j + odd:8 * j + 8:2, :],
                                                   ps_p[1][rows, 0:4 * S].rearrange("p (m s) -> p m s", m=4),
                                                   DH ** -0.5, None, ALU.mult)
                last.then_inc(taken[1], 1)

            def take_rel(g, n):
                dve.wait_ge(rel_raw[1], g * (S // QI // 2) + n // 2 + 1)
                wait(dve, rel_v_raw, g * NV)
                nc.vector.tensor_copy(turned[:TEXT, :, :, n * QI:(n + 1) * QI].rearrange("p k h i -> p (k h) i"),
                                      ps_s[1][:TEXT, :].rearrange("p (i n) -> p n i", i=QI)).then_inc(rel_taken[1], 1)

            def take_k(g, k, m):
                arrived(g, use_k(k, m))
                wait(dve, scores_raw, head_count(g, k, -1))
                nc.vector.tensor_copy(kT[:, m, 0:TEXT + AUD], ps_p[1][:, 0:TEXT + AUD]).then_inc(taken[1], 1)

            def take_image(g, j):
                arrived(g, use_image(j))
                if j < 2:
                    nc.vector.tensor_copy(k_image[:, 4 * j:4 * j + 4].rearrange("p m t -> p (m t)"), ps_p[1][:, 0:4 * K4 * IMG]).then_inc(
                        taken[1], 1)
                else:
                    half = slice((j - 2) * 512, (j - 1) * 512)
                    wait(dve, av_done, head_count(g, 0, -1))
                    nc.vector.tensor_copy(v[IMG_ROW:P, 3, half], ps_p[1][IMG_ROW:P, :]).then_inc(taken[1], 1)

            def take_v(g, k, j):
                t, half = j // 2, slice(j % 2 * 512, j % 2 * 512 + 512)
                arrived(g, use_v(k, j))
                wait(dve, av_done, head_count(g, k, -1))
                rows = value_rows(t)[1]
                nc.vector.tensor_copy(v[:rows, t, half], ps_p[1][:rows, :]).then_inc(taken[1], 1)

            def row_max(g, k, h):
                n = head_count(g, k, h)
                dve.wait_ge(scores_raw, n)
                wait(dve, exps_done, n - RING)
                for j, (lo, hi) in enumerate(columns):
                    last = nc.vector.tensor_reduce(neg_max[:, h % RING, j:j + 1], ps_s[h % 2][:S, lo:hi], AX_X, ALU.max,
                                                   negate=True)
                last.then_inc(max_ready, 1)

            def invert(g, k, h):
                n = head_count(g, k, h)
                dve.wait_ge(exps_done, n)
                wait(dve, probs_ready, n - RING)
                nc.vector.reciprocal(inverse[:, h % RING, :], total[:, h % RING, :]).then_inc(inverse_ready, 1)

            def take_probsT(g, k, h):
                n = head_count(g, k, h)
                dve.wait_ge(probsT_raw, n)
                wait(dve, av_done, n - 2)
                nc.vector.tensor_copy(turned[:, k, h, :], ps_t[h % 2][:TEXT, 0:S])
                nc.vector.tensor_copy(audT[:, h % 2], ps_t[h % 2][:, S:4 * S].rearrange("p (t s) -> p t s", t=3)).then_inc(
                    probsT_ready, 1)

            def add_rel_v(g, n):
                dve.wait_ge(rel_v_raw, g * NV + n + 1)
                if n == 0:
                    for i in range(2):
                        dve.wait_ge(out_taken[i], (g + 1) * K4)
                lo = S - (n + 1) * VI
                for odd in range(2):
                    to = outT[odd * DH:(odd + 1) * DH, :, :, lo:lo + VI].rearrange("p k m i -> p (k m) i")
                    product = ps_t[n % 2][:DH, 0:VI * K4 * H].rearrange("p (i n two) -> p two n i", i=VI, two=2)
                    last = nc.vector.tensor_tensor(to, product[:, odd], to, ALU.add)
                last.then_inc(rel_v_added, 1)

            def add_residual(g, k):
                b = g * K4 + k
                dve.wait_ge(y_raw, b + 1)
                dve.wait_ge(x_bias_ready, b + 1)
                wait(dve, norm.x_ready, b)
                nc.vector.tensor_tensor(norm.z[:], ps_o[k % 2][:S, 0:E], x_bias[:], ALU.add).then_inc(z_ready, 1)
                norm.take_stats(nc, dve, b, z_ready, b + 1, passed)

            nc.vector.memset(q_head[:, 0:K4 // 2], 0.0).then_inc(zeroed, 1)
            nc.vector.tensor_copy(rel_k[:, 0:S - 17], rel_k[:, S - 17:S - 16].broadcast_to([P, S - 17]))
            nc.vector.tensor_copy(rel_k[:, S + 16:WIDE], rel_k[:, S + 15:S + 16].broadcast_to([P, WIDE - S - 16])).then_inc(
                rel_k_ready, 1)
            dve.wait_ge(tanh_done, 1)
            nc.vector.tensor_scalar(gain[:, 1:3], gain[:, 1:3], 1.0, None, ALU.add).then_inc(gain_ready, 1)
            dve.wait_ge(zeroed, 4)

            def mine(u):
                return u % 2 == 1

            for k in range(K4):
                if mine(use_x(k)):
                    take_x(0, k)
                for j in range(2):
                    if mine(use_q(k, j)):
                        take_q(0, k, j)

            def body(g, last):
                for n in range(1, S // QI, 2):
                    take_rel(g, n)
                for j in range(1, 4, 2):
                    take_image(g, j)
                for m in range(1, NP, 2):
                    take_k(g, 0, m)
                for k in range(K4):
                    for j in range(1, 8, 2):
                        take_v(g, k, j)
                    for h in range(H + AV_LAG):
                        if h < H:
                            row_max(g, k, h)
                        if 1 <= h <= H:
                            invert(g, k, h - 1)
                        if T_LAG <= h < H + T_LAG:
                            take_probsT(g, k, h - T_LAG)
                        if h >= H and k < K4 - 1:
                            take_k(g, k + 1, 2 * (h - H) + 1)
                for n in range(NV):
                    add_rel_v(g, n)
                for k in range(K4):
                    for j in range(2):
                        if not last and mine(use_q(k, j)):
                            take_q(g + 1, k, j)
                    if not last and k < K4 - 1 and mine(use_x(k + 1)):
                        take_x(g + 1, k + 1)
                    add_residual(g, k)
                    norm.apply(nc, dve, g * K4 + k)

            groups(dve, body)

        @block.gpsimd
        def _(pool):
            def take_x(g, k):
                b = g * K4 + k
                if k > 0:
                    i, n = bank_count(g, use_x(k - 1))
                    wait(pool, raw[i], n + 1)
                nc.gpsimd.tensor_copy(xs[:], row_of(x, b)).then_inc(xs_ready, 1)

            def normalise(g, k, h):
                n = head_count(g, k, h)
                wait_apart(pool, inverse_ready, n, passed_pool)
                if h < RING and not (isinstance(g, int) and g == 0 and k == 0):
                    lo, hi = places((k - 1) % K4)[2]
                    nc.gpsimd.memset(probs[:, h % RING, lo:hi], 0.0)
                for j, (lo, hi) in enumerate(places(k)):
                    at = probs[:, h % RING, lo:hi]
                    last = nc.gpsimd.tensor_scalar(at, at, inverse[:, h % RING, j:j + 1], gain[:, j:j + 1], ALU.mult,
                                                   ALU.mult)
                last.then_inc(probs_ready, 1)

            def add_bias(g, k):
                b = g * K4 + k
                wait(pool, z_ready, b)
                nc.gpsimd.tensor_tensor(x_bias[:], row_of(x, b), b_o[:], ALU.add).then_inc(x_bias_ready, 1)

            take_x(0, 0)
            nc.gpsimd.memset(q_head[:, K4 // 2:], 0.0).then_inc(zeroed, 1)
            nc.gpsimd.memset(v[:, 3], 0.0).then_inc(zeroed, 1)
            nc.gpsimd.memset(probs[:], 0.0).then_inc(zeroed, 1)
            nc.gpsimd.memset(gain[:, 0:1], 1.0)
            pool.wait_ge(gain_ready, 1)

            for k in range(1, K4):
                take_x(0, k)

            def body(g, last):
                for k in range(K4):
                    for h in range(H):
                        normalise(g, k, h)
                if not last:
                    take_x(g + 1, 0)
                for k in range(K4):
                    add_bias(g, k)
                    if not last and k < K4 - 1:
                        take_x(g + 1, k + 1)
                    norm.gpsimd(nc, pool, g * K4 + k, passed_pool)

            groups(pool, body)


def ffn_binary(nc, shared, name, a, out):
    x, ident = shared["x"], shared["ident"]
    HALF = FC // 2
    with ExitStack() as ctx:
        buf = Buffers(nc, ctx, name, shared["semaphores"])
        w1, w2 = buf.sb("w1", [P, EC, HID]), buf.sb("w2", [P, FC, E])
        w1_rows, w2_rows = buf.sb("w1_rows", [P, FC, E]), buf.sb("w2_rows", [P, EC, HID])
        negative = buf.sb("negative", [P, EC * HID])
        alpha1, alpha2 = buf.sb("alpha1", [P, FC]), buf.sb("alpha2", [P, EC])
        alpha2_diag, alpha2_row = buf.sb("alpha2_diag", [P, E]), buf.sb("alpha2_row", [S, E])
        bias1, bias2 = buf.sb("bias1", [P, FC]), buf.sb("bias2", [S, E])
        ones = buf.sb("ones", [P, P])
        xs, xT = buf.sb("xs", [S, E]), buf.sb("xT", [P, EC, S])
        hidden = buf.sb("hidden", [P, FC, S])
        x_bias, z_raw = buf.sb("x_bias", [S, E]), buf.sb("z_raw", [S, E])
        norm = Norm(buf, shared)
        ps_x, ps_y, ps_w = buf.psum("ps_x"), buf.psum("ps_y"), buf.psum("ps_w")
        ps_h = [buf.psum(f"ps_h{i}") for i in range(2)]

        w1_loaded, bias1_loaded, w1_rows_loaded, w2_loaded, w2_rows_loaded, bias2_loaded = (buf.sem(n) for n in (
            "w1_loaded", "bias1_loaded", "w1_rows_loaded", "w2_loaded", "w2_rows_loaded", "bias2_loaded"))
        passed, passed_pool, passed_sp, ones_ready, stored = (buf.sem(n) for n in (
            "passed", "passed_pool", "passed_sp", "ones_ready", "stored"))
        alpha1_sum, alpha2_sum, alpha1_ready, alpha2_ready = (buf.sem(n) for n in (
            "alpha1_sum", "alpha2_sum", "alpha1_ready", "alpha2_ready"))
        prep, signs_ready, diag_ready, row_raw, row_ready = (buf.sem(n) for n in (
            "prep", "signs_ready", "diag_ready", "row_raw", "row_ready"))
        xs_ready, xT_raw, xT_ready, h_raw, gelu_done = (buf.sem(n) for n in (
            "xs_ready", "xT_raw", "xT_ready", "h_raw", "gelu_done"))
        y_raw, scaled, x_bias_ready, z_ready = (buf.sem(n) for n in ("y_raw", "scaled", "x_bias_ready", "z_ready"))

        loads = [(w1[:], a["L1_ffn_w1T"].rearrange("(c p) n -> p c n", p=P)),
                 (bias1[:], a["L1_ffn_b1"]),
                 (w1_rows[:], a["L1_ffn_w1"].rearrange("(c p) n -> p c n", p=P)),
                 (w2[:], a["L1_ffn_w2T"].rearrange("(c p) n -> p c n", p=P)),
                 (w2_rows[:], a["L1_ffn_w2"].rearrange("(c p) n -> p c n", p=P)),
                 (bias2[:], a["L1_ffn_b2"].rearrange("(a n) -> a n", a=1).partition_broadcast(S))]
        all_loaded = (w1_loaded, bias1_loaded, w1_rows_loaded, w2_loaded, w2_rows_loaded, bias2_loaded)
        block = ctx.enter_context(nc.Block())

        @block.sync
        def _(sp):
            for (to, w), loaded in zip(loads, all_loaded):
                sp.dma_start(to, w).then_inc(loaded, 16)

            def store(b, first, last):
                wait_apart(sp, norm.x_ready, b + 1, passed_sp)
                sp.dma_start(out[bass.ds(b, 1)].rearrange("b s e -> s (b e)"), row_of(x, b)).then_inc(stored, 16)

            sequences(sp, store)
            sp.wait_ge(stored, 16 * B)

        @block.tensor
        def _(pe):
            def turn_x(b):
                pe.wait_ge(xs_ready, b + 1)
                wait(pe, xT_ready, b)
                for c in range(EC):
                    last = nc.tensor.transpose(ps_x[:, c * S:(c + 1) * S], xs[:, c * P:(c + 1) * P], ident[:S, :S])
                last.then_inc(xT_raw, 1)

            def up(b):
                pe.wait_ge(xT_ready, b + 1)
                for m in range(FC):
                    if m % HALF == 0:
                        wait(pe, gelu_done, 2 * (b - 1) + m // HALF + 1)
                    for c in range(EC):
                        last = nc.tensor.matmul(ps_h[m // HALF][:, m % HALF * S:(m % HALF + 1) * S],
                                                w1[:, c, m * P:(m + 1) * P], xT[:, c, :],
                                                start=(c == 0), stop=(c == EC - 1))
                    if m % HALF == HALF - 1:
                        last.then_inc(h_raw, 1)

            def down(b):
                wait(pe, scaled, b)
                for m in range(FC):
                    if m % HALF == 0:
                        pe.wait_ge(gelu_done, 2 * b + m // HALF + 1)
                    last = nc.tensor.matmul(ps_y[:S, 0:E], hidden[:, m, :], w2[:, m, :], start=(m == 0), stop=(m == FC - 1))
                    if m % HALF == HALF - 1:
                        last.then_inc(y_raw, 1)

            turn_x(0)
            pe.wait_ge(signs_ready, 1)
            up(0)
            turn_x(1)
            pe.wait_ge(signs_ready, 2)
            pe.wait_ge(diag_ready, 1)
            pe.wait_ge(ones_ready, 1)
            nc.tensor.matmul(ps_w[:S, 0:E], ones[:, 0:S], alpha2_diag[:], start=True, stop=True).then_inc(row_raw, 1)

            def body(b, next, after):
                if next is not None:
                    up(next)
                if after is not None:
                    turn_x(after)
                down(b)

            staggered(pe, body)

        @block.scalar
        def _(act):
            def take_xT(b):
                act.wait_ge(xT_raw, b + 1)
                wait(act, h_raw, 2 * b)
                nc.scalar.copy(xT[:], ps_x[:, 0:EC * S].rearrange("p (c s) -> p c s", c=EC)).then_inc(xT_ready, 1)

            def gelu(b):
                for m in range(FC):
                    if m % HALF == 0:
                        act.wait_ge(h_raw, 2 * b + m // HALF + 1)
                        wait(act, y_raw, 2 * b + m // HALF - 1)
                    last = nc.scalar.activation(hidden[:, m, :], ps_h[m // HALF][:, m % HALF * S:(m % HALF + 1) * S],
                                                ACT.Gelu, bias=bias1[:, m:m + 1], scale=alpha1[:, m:m + 1])
                    if m % HALF == HALF - 1:
                        last.then_inc(gelu_done, 1)

            take_xT(0)
            act.wait_ge(alpha1_ready, 1)
            act.wait_ge(bias1_loaded, 16)
            gelu(0)
            take_xT(1)
            act.wait_ge(row_raw, 1)
            nc.scalar.copy(alpha2_row[:], ps_w[:S, 0:E]).then_inc(row_ready, 1)

            def body(b, next, after):
                if after is not None:
                    take_xT(after)
                if next is not None:
                    gelu(next)

            staggered(act, body)

        @block.vector
        def _(dve):
            def take_signs(i, w):
                flat = w[:].rearrange("p c n -> p (c n)")
                wait(dve, signs_ready, i)
                nc.vector.tensor_scalar(negative[:], flat, 0.0, None, ALU.is_lt).then_inc(prep, 1)
                dve.wait_ge(prep, i + 1)
                nc.vector.scalar_tensor_tensor(flat, flat, 0.0, negative[:], ALU.is_gt, ALU.subtract).then_inc(
                    signs_ready, 1)

            def take_means(alpha, rows, size, summed, ready):
                nc.vector.tensor_reduce(alpha[:], rows[:], AX_X, ALU.add, apply_absolute_value=True).then_inc(summed, 1)
                dve.wait_ge(summed, 1)
                nc.vector.tensor_scalar(alpha[:], alpha[:], 1.0 / size, None, ALU.mult).then_inc(ready, 1)

            dve.wait_ge(w1_loaded, 16)
            take_signs(0, w1)
            dve.wait_ge(w1_rows_loaded, 16)
            take_means(alpha1, w1_rows, E, alpha1_sum, alpha1_ready)
            dve.wait_ge(w2_loaded, 16)
            take_signs(1, w2)
            dve.wait_ge(w2_rows_loaded, 16)
            take_means(alpha2, w2_rows, HID, alpha2_sum, alpha2_ready)
            dve.wait_ge(alpha2_ready, 1)
            for c in range(EC):
                last = nc.vector.tensor_scalar(alpha2_diag[:, c * P:(c + 1) * P], ident[:], alpha2[:, c:c + 1], None,
                                               ALU.mult)
            last.then_inc(diag_ready, 1)
            dve.wait_ge(row_ready, 1)

            def body(b, first, last):
                dve.wait_ge(y_raw, 2 * (b + 1))
                nc.vector.tensor_tensor(z_raw[:], ps_y[:S, 0:E], alpha2_row[:], ALU.mult).then_inc(scaled, 1)
                dve.wait_ge(scaled, b + 1)
                dve.wait_ge(x_bias_ready, b + 1)
                nc.vector.tensor_tensor(norm.z[:], z_raw[:], x_bias[:], ALU.add).then_inc(z_ready, 1)
                norm.vector(nc, dve, b, z_ready, b + 1, passed)

            sequences(dve, body)

        @block.gpsimd
        def _(pool):
            def take_x(b):
                wait(pool, xT_raw, b)
                nc.gpsimd.tensor_copy(xs[:], row_of(x, b)).then_inc(xs_ready, 1)

            def add_bias(b):
                wait(pool, z_ready, b)
                nc.gpsimd.tensor_tensor(x_bias[:], row_of(x, b), bias2[:], ALU.add).then_inc(x_bias_ready, 1)

            nc.gpsimd.memset(ones[:], 1.0).then_inc(ones_ready, 1)
            take_x(0)
            take_x(1)
            pool.wait_ge(bias2_loaded, 16)

            def body(b, next, after):
                if after is not None:
                    take_x(after)
                add_bias(b)
                norm.gpsimd(nc, pool, b, passed_pool)

            staggered(pool, body)


def start(nc, shared, x, loads):
    with ExitStack() as ctx:
        buf = Buffers(nc, ctx, "start", shared["semaphores"])
        loaded, zeroed, ident_ready = buf.sem("loaded"), buf.sem("zeroed"), buf.sem("ident_ready")
        block = ctx.enter_context(nc.Block())

        @block.sync
        def _(sp):
            for to, a in loads + [(shared["x"][:], x.rearrange("b s e -> s b e"))]:
                sp.dma_start(to, a).then_inc(loaded, 16)
            sp.wait_ge(loaded, 16 * (len(loads) + 1))

        @block.gpsimd
        def _(pool):
            nc.gpsimd.memset(shared["ident"][:], 0.0).then_inc(zeroed, 1)
            nc.gpsimd.memset(shared["minus_half"][:], -0.5)
            pool.wait_ge(zeroed, 1)
            nc.gpsimd.affine_select(out=shared["ident"][:], in_=shared["ident"][:], compare_op=ALU.not_equal,
                                    fill=1.0, base=0, pattern=[[-1, P]], channel_multiplier=1).then_inc(
                ident_ready, 1)
            pool.wait_ge(ident_ready, 1)


def build(nc, a, out):
    with ExitStack() as ctx:
        semaphores = []
        buf = Buffers(nc, ctx, "all", semaphores)
        shared = {
            "semaphores": semaphores,
            "x": buf.sb("x", [S, B, E]),
            "ident": buf.sb("ident", [P, P]),
            "minus_half": buf.sb("minus_half", [S, 1]),
        }
        with ExitStack() as five:
            relative, relative_loads = cross_attention_relative_weights(Buffers(nc, five, "l1xa", semaphores), a)
            with ExitStack() as four:
                first, first_loads = self_attention_weights(
                    Buffers(nc, four, "l0sa", semaphores), *(a[f"L0_attn_{n}"] for n in ("Wq", "Wk", "Wv", "Wo")),
                    a["c_mask16"], biases=[a[f"L0_attn_{n}"] for n in ("bq", "bk", "bv", "bo")])
                rope, rope_loads = cross_attention_rope_weights(
                    Buffers(nc, four, "l0xa", semaphores),
                    *(a[f"L0_xattn_{n}"] for n in ("W_q", "W_k", "W_v", "W_o")), a["c_rope"],
                    a["c_mask16"])
                quantised, quantised_loads = ffn_quantised_weights(
                    Buffers(nc, four, "l0ff", semaphores), *(a[f"L0_ffn_{n}"] for n in ("w1", "conv_w", "conv_b", "w2")))
                causal, causal_loads = self_attention_weights(
                    Buffers(nc, four, "l1sa", semaphores), *(a[f"L1_attn_{n}"] for n in ("Wq", "Wk", "Wv", "Wo")),
                    a["c_mask16_fine"], pos=[a["c_posT"], a["c_causal"]])
                start(nc, shared, a["x"], first_loads)
                start_anew(nc, semaphores)
                self_attention(nc, shared, "l0sa", first, True, rope_loads + quantised_loads + causal_loads + relative_loads)
                start_anew(nc, semaphores)
                cross_attention_rope(nc, shared, "l0xa", a["ctxT"], rope)
                start_anew(nc, semaphores)
                ffn_quantised(nc, shared, "l0ff", quantised)
                start_anew(nc, semaphores)
                self_attention(nc, shared, "l1sa", causal, False)
                start_anew(nc, semaphores)
            cross_attention_relative(nc, shared, "l1xa", a, relative)
            start_anew(nc, semaphores)
        ffn_binary(nc, shared, "l1ff", a, out)


def kernel(**inputs):
    import numpy as np
    import concourse.bacc as bacc
    from concourse.bass_utils import run_bass_kernel_spmd

    arrays = {n: np.ascontiguousarray(v) for n, v in inputs.items()}
    turned = ["L0_attn_Wq", "L0_attn_Wk", "L0_attn_Wv", "L0_attn_Wo", "L0_xattn_W_q", "L0_xattn_W_k", "L0_xattn_W_v",
              "L0_xattn_W_o", "L0_ffn_w1", "L0_ffn_w2"]
    for n in turned:
        arrays[n] = np.ascontiguousarray(arrays[n].T)
    for n in ("L0_attn_bq", "L0_attn_bk"):
        arrays[n] = np.ascontiguousarray(arrays[n].reshape(EC, P).T)
    arrays["ctxT"] = np.ascontiguousarray(arrays.pop("ctx_1024").transpose(2, 0, 1))
    arrays["L0_ffn_conv_w"] = np.ascontiguousarray(arrays["L0_ffn_conv_w"].reshape(HID, 3))
    for n in ("L0_ffn_conv_b", "L1_ffn_b1"):
        arrays[n] = np.ascontiguousarray(arrays[n].reshape(FC, P).T)
    arrays["L1_ffn_w1T"] = np.ascontiguousarray(arrays["L1_ffn_w1"].T)
    arrays["L1_ffn_w2T"] = np.ascontiguousarray(arrays["L1_ffn_w2"].T)
    for n in ("L1_xattn_alpha", "L1_xattn_beta"):
        arrays[n] = arrays[n].reshape(1, 1)
    rel_v = arrays["L1_xattn_rel_v"]
    arrays["L1_xattn_rel_k"] = np.ascontiguousarray(arrays["L1_xattn_rel_k"].T)
    arrays["rel_v_wide"] = np.ascontiguousarray(
        np.concatenate([np.repeat(rel_v[:1], S - 1 - 16, 0), rel_v, np.repeat(rel_v[-1:], TEXT - 1 - 16, 0)]))

    own = (np.arange(P)[:, None] // D == np.arange(HC)[None, :])
    arrays["c_mask16"] = (own * 0.25).astype(np.float32)
    arrays["c_mask16_fine"] = (own * 0.0625).astype(np.float32)
    f = np.float32
    inv_freq = (f(1.0) / f(10000.0) ** (np.arange(0, D, 2, dtype=f) / f(D))).astype(f)
    ang = np.outer(np.arange(CTX, dtype=f), inv_freq).astype(f)
    cos, sin = np.cos(ang).T, np.sin(ang).T
    pair, odd = (np.arange(P) % D) // 2, np.arange(P) % 2
    arrays["c_rope"] = np.stack([cos[pair], sin[pair] * np.where(odd, 1.0, -1.0)[:, None]], 1).astype(f)
    idx = np.arange(S, dtype=f)
    scale = (f(1.0) / (f(10000.0) ** (np.arange(0, D, 2, dtype=f) / f(D)) + np.finfo(f).eps)).astype(f)
    ang = (idx[:, None] * scale[None, :]).astype(f)
    pos = np.stack([np.sin(ang), np.cos(ang)], -1).reshape(S, D)
    arrays["c_posT"] = np.ascontiguousarray(pos.T[np.arange(P) % D]).astype(f)
    arrays["c_causal"] = np.where(np.triu(np.ones((S, S), bool), 1), f(-1e37), f(0.0)).astype(f)

    nc = bacc.Bacc("TRN2", target_bir_lowering=False, num_devices=1)
    args = {n: nc.dram_tensor(f"in_{n}", v.shape, mybir.dt.from_np(v.dtype), kind="ExternalInput").ap()
            for n, v in arrays.items()}
    out = nc.dram_tensor("out_x", (B, S, E), F32, kind="ExternalOutput").ap()
    build(nc, args, out)
    result = run_bass_kernel_spmd(nc, [{f"in_{n}": v for n, v in arrays.items()}], core_ids=[0])
    return result.results[0]["out_x"]
```
